# Optimizing a Trainium2 kernel written in Bass

```python
import numpy as np
import jax
import jax.numpy as jnp

def _softmax(x, axis=-1):
    return jax.nn.softmax(x, axis=axis)

def _gelu(x):
    return jax.nn.gelu(x, approximate=True)

def _silu(x):
    return jax.nn.silu(x)

def _sigmoid(x):
    return jax.nn.sigmoid(x)

def _layernorm(x, axis=-1, eps=1e-05):
    m = jnp.mean(x, axis=axis, keepdims=True)
    v = jnp.var(x, axis=axis, keepdims=True)
    return (x - m) / jnp.sqrt(v + eps)

def _scatter_add(tgt, idx, src, axis=0):
    return tgt.at[idx].add(src)

def _segment_sum(src, seg, n):
    return jax.ops.segment_sum(src, seg, n)
kernel_name = 'mk_prb_d2_jaxref_r8_5f08c1'

def setup_inputs(seed: int=0):
    np.random.seed(seed)
    _w = jnp.asarray

    def _L0_attn_setup():
        import jax, jax.numpy as jnp
        import numpy as np
        B, N, E = (4, 512, 256)
        H_DIM = 256
        HEADS = 16
        DH = H_DIM // HEADS
        LN_EPS = 1e-05

        def _heads(t):
            b, n, _ = t.shape
            return t.reshape(b, n, HEADS, DH).transpose(0, 2, 1, 3)

        def _layernorm(x, g, b):
            mu = jnp.mean(x, axis=-1, keepdims=True)
            var = jnp.mean(jnp.square(x - mu), axis=-1, keepdims=True)
            return (x - mu) * jax.lax.rsqrt(var + LN_EPS) * g + b
        key = jax.random.key(seed)
        ks = jax.random.split(key, 10)
        s = 1.0 / np.sqrt(E)
        so = 1.0 / np.sqrt(H_DIM)
        return {'x': jax.random.normal(ks[0], (B, N, E), jnp.float32), 'Wqk': jax.random.normal(ks[1], (E, H_DIM), jnp.float32) * s, 'bqk': jnp.zeros((H_DIM,), jnp.float32), 'Wv': jax.random.normal(ks[2], (E, H_DIM), jnp.float32) * s, 'bv': jnp.zeros((H_DIM,), jnp.float32), 'Wu': jax.random.normal(ks[3], (E, H_DIM), jnp.float32) * s, 'bu': jnp.zeros((H_DIM,), jnp.float32), 'Wo': jax.random.normal(ks[4], (H_DIM, E), jnp.float32) * so, 'bo': jnp.zeros((E,), jnp.float32), 'ln_g': jnp.ones((H_DIM,), jnp.float32), 'ln_b': jnp.zeros((H_DIM,), jnp.float32)}
    _L0_attn_in = _L0_attn_setup()

    def _L0_ffn_setup():
        import jax, jax.numpy as jnp
        import numpy as np
        HIDDEN = 256
        INTER = 1024
        MOE_INTER = 128
        N_ROUTED = 8
        NUM_LOCAL = 8
        TOP_K = 2
        B, S = (4, 256)

        def _mlp(x, gw, uw, dw):
            g = x @ gw.T
            u = x @ uw.T
            return g * jax.nn.sigmoid(g) * u @ dw.T
        key = jax.random.key(seed)
        ks = jax.random.split(key, 8)
        std = 0.02
        return {'hidden_states': jax.random.normal(ks[0], (B, S, HIDDEN), jnp.float32), 'router_weight': jax.random.normal(ks[1], (N_ROUTED, HIDDEN), jnp.float32) * std, 'sh_gate': jax.random.normal(ks[2], (INTER, HIDDEN), jnp.float32) * std, 'sh_up': jax.random.normal(ks[3], (INTER, HIDDEN), jnp.float32) * std, 'sh_down': jax.random.normal(ks[4], (HIDDEN, INTER), jnp.float32) * std, 'r_gate': jax.random.normal(ks[5], (MOE_INTER, HIDDEN), jnp.float32) * std, 'r_up': jax.random.normal(ks[6], (MOE_INTER, HIDDEN), jnp.float32) * std, 'r_down': jax.random.normal(ks[7], (HIDDEN, MOE_INTER), jnp.float32) * std}
    _L0_ffn_in = _L0_ffn_setup()

    def _L1_attn_setup():
        import jax, jax.numpy as jnp
        import numpy as np
        D_MODEL = 256
        N_HEADS = 16
        HEAD_DIM = D_MODEL // N_HEADS
        D_LATENT = 64
        B = 2
        S = 256
        key = jax.random.key(seed)
        ks = jax.random.split(key, 7)
        sc = 0.02
        return {'x': jax.random.normal(ks[0], (B, S, D_MODEL), dtype=jnp.float32), 'W_q': jax.random.normal(ks[1], (D_MODEL, D_MODEL), dtype=jnp.float32) * sc, 'W_dkv': jax.random.normal(ks[2], (D_LATENT, D_MODEL), dtype=jnp.float32) * sc, 'W_uk': jax.random.normal(ks[3], (D_MODEL, D_LATENT), dtype=jnp.float32) * sc, 'W_uv': jax.random.normal(ks[4], (D_MODEL, D_LATENT), dtype=jnp.float32) * sc, 'W_o_w': jax.random.normal(ks[5], (D_MODEL, D_MODEL), dtype=jnp.float32) * sc, 'W_o_b': jax.random.normal(ks[6], (D_MODEL,), dtype=jnp.float32) * sc}
    _L1_attn_in = _L1_attn_setup()

    def _L1_ffn_setup():
        import jax, jax.numpy as jnp
        import numpy as np
        HIDDEN = 256
        INTER = 704
        B, S = (2, 256)

        def _ternary(key, shape):
            return jax.random.randint(key, shape, -1, 2).astype(jnp.float32)
        key = jax.random.key(seed)
        ks = jax.random.split(key, 7)
        x = jax.random.normal(ks[0], (B, S, HIDDEN), dtype=jnp.float32)
        gate_w = _ternary(ks[1], (INTER, HIDDEN))
        up_w = _ternary(ks[2], (INTER, HIDDEN))
        down_w = _ternary(ks[3], (HIDDEN, INTER))
        gate_s = jax.random.uniform(ks[4], (INTER,), minval=0.01, maxval=0.1, dtype=jnp.float32)
        up_s = jax.random.uniform(ks[5], (INTER,), minval=0.01, maxval=0.1, dtype=jnp.float32)
        down_s = jax.random.uniform(ks[6], (HIDDEN,), minval=0.01, maxval=0.1, dtype=jnp.float32)
        return {'x': x, 'gate_w': gate_w, 'up_w': up_w, 'down_w': down_w, 'gate_s': gate_s, 'up_s': up_s, 'down_s': down_s}
    _L1_ffn_in = _L1_ffn_setup()
    _d = {'L0_attn_x': _L0_attn_in['x'], 'L0_attn_Wqk': _L0_attn_in['Wqk'], 'L0_attn_bqk': _L0_attn_in['bqk'], 'L0_attn_Wv': _L0_attn_in['Wv'], 'L0_attn_bv': _L0_attn_in['bv'], 'L0_attn_Wu': _L0_attn_in['Wu'], 'L0_attn_bu': _L0_attn_in['bu'], 'L0_attn_Wo': _L0_attn_in['Wo'], 'L0_attn_bo': _L0_attn_in['bo'], 'L0_attn_ln_g': _L0_attn_in['ln_g'], 'L0_attn_ln_b': _L0_attn_in['ln_b'], 'L0_ffn_router_weight': _L0_ffn_in['router_weight'], 'L0_ffn_sh_gate': _L0_ffn_in['sh_gate'], 'L0_ffn_sh_up': _L0_ffn_in['sh_up'], 'L0_ffn_sh_down': _L0_ffn_in['sh_down'], 'L0_ffn_r_gate': _L0_ffn_in['r_gate'], 'L0_ffn_r_up': _L0_ffn_in['r_up'], 'L0_ffn_r_down': _L0_ffn_in['r_down'], 'L1_attn_W_q': _L1_attn_in['W_q'], 'L1_attn_W_dkv': _L1_attn_in['W_dkv'], 'L1_attn_W_uk': _L1_attn_in['W_uk'], 'L1_attn_W_uv': _L1_attn_in['W_uv'], 'L1_attn_W_o_w': _L1_attn_in['W_o_w'], 'L1_attn_W_o_b': _L1_attn_in['W_o_b'], 'L1_ffn_gate_w': _L1_ffn_in['gate_w'], 'L1_ffn_up_w': _L1_ffn_in['up_w'], 'L1_ffn_down_w': _L1_ffn_in['down_w'], 'L1_ffn_gate_s': _L1_ffn_in['gate_s'], 'L1_ffn_up_s': _L1_ffn_in['up_s'], 'L1_ffn_down_s': _L1_ffn_in['down_s']}
    _x0 = _d['L0_attn_x']
    _d['L0_attn_x'] = jax.random.normal(jax.random.fold_in(jax.random.key(seed), 1), (1, 2048, 256), dtype=_x0.dtype)
    del _x0
    return _d

def reference(L0_attn_x, L0_attn_Wqk, L0_attn_bqk, L0_attn_Wv, L0_attn_bv, L0_attn_Wu, L0_attn_bu, L0_attn_Wo, L0_attn_bo, L0_attn_ln_g, L0_attn_ln_b, L0_ffn_router_weight, L0_ffn_sh_gate, L0_ffn_sh_up, L0_ffn_sh_down, L0_ffn_r_gate, L0_ffn_r_up, L0_ffn_r_down, L1_attn_W_q, L1_attn_W_dkv, L1_attn_W_uk, L1_attn_W_uv, L1_attn_W_o_w, L1_attn_W_o_b, L1_ffn_gate_w, L1_ffn_up_w, L1_ffn_down_w, L1_ffn_gate_s, L1_ffn_up_s, L1_ffn_down_s):

    def _L0_attn_ref(x, Wqk, bqk, Wv, bv, Wu, bu, Wo, bo, ln_g, ln_b):
        import jax, jax.numpy as jnp
        import numpy as np
        B, N, E = (4, 512, 256)
        H_DIM = 256
        HEADS = 16
        DH = H_DIM // HEADS
        LN_EPS = 1e-05

        def _heads(t):
            b, n, _ = t.shape
            return t.reshape(b, n, HEADS, DH).transpose(0, 2, 1, 3)

        def _layernorm(x, g, b):
            mu = jnp.mean(x, axis=-1, keepdims=True)
            var = jnp.mean(jnp.square(x - mu), axis=-1, keepdims=True)
            return (x - mu) * jax.lax.rsqrt(var + LN_EPS) * g + b
        q = x @ Wqk + bqk
        k = x @ Wqk + bqk
        v = jax.nn.silu(x @ Wv + bv)
        u = jax.nn.silu(x @ Wu + bu)
        q = jax.nn.elu(_heads(q))
        kh = jax.nn.elu(_heads(k))
        vh = _heads(v)
        kv = jnp.einsum('bhnd,bhne->bhde', kh, vh)
        out = jnp.einsum('bhnd,bhde->bhne', q, kv)
        out = out.transpose(0, 2, 1, 3).reshape(x.shape[0], x.shape[1], H_DIM)
        out = _layernorm(out, ln_g, ln_b)
        out = u * out
        return out @ Wo + bo

    def _L0_ffn_ref(hidden_states, router_weight, sh_gate, sh_up, sh_down, r_gate, r_up, r_down):
        import jax, jax.numpy as jnp
        import numpy as np
        HIDDEN = 256
        INTER = 1024
        MOE_INTER = 128
        N_ROUTED = 8
        NUM_LOCAL = 8
        TOP_K = 2
        B, S = (4, 256)

        def _mlp(x, gw, uw, dw):
            g = x @ gw.T
            u = x @ uw.T
            return g * jax.nn.sigmoid(g) * u @ dw.T
        Bsz, Seq, H = hidden_states.shape
        x = hidden_states.reshape(-1, H)
        logits = x.astype(jnp.float32) @ router_weight.astype(jnp.float32).T
        topk_vals, topk_idx = jax.lax.top_k(logits, TOP_K)
        topk_w = jax.nn.softmax(topk_vals, axis=-1)
        slot_mask = (topk_idx < NUM_LOCAL).astype(topk_w.dtype)
        comb_w = jnp.sum(topk_w * slot_mask, axis=-1).astype(x.dtype)
        shared = _mlp(x, sh_gate, sh_up, sh_down)
        routed = _mlp(x, r_gate, r_up, r_down) * comb_w[:, None]
        return (shared + routed).reshape(Bsz, Seq, H)

    def _L1_attn_ref(x, W_q, W_dkv, W_uk, W_uv, W_o_w, W_o_b):
        import jax, jax.numpy as jnp
        import numpy as np
        D_MODEL = 256
        N_HEADS = 16
        HEAD_DIM = D_MODEL // N_HEADS
        D_LATENT = 64
        B = 2
        S = 256
        b, s, d = x.shape
        q = (x @ W_q.T).reshape(b, s, N_HEADS, HEAD_DIM).transpose(0, 2, 1, 3)
        c_kv = x @ W_dkv.T
        k = (c_kv @ W_uk.T).reshape(b, s, N_HEADS, HEAD_DIM).transpose(0, 2, 1, 3)
        v = (c_kv @ W_uv.T).reshape(b, s, N_HEADS, HEAD_DIM).transpose(0, 2, 1, 3)
        scores = jnp.einsum('bhqd,bhkd->bhqk', q, k)
        causal = jnp.arange(s)[:, None] < jnp.arange(s)[None, :]
        scores = jnp.where(causal, -jnp.inf, scores)
        attn = jax.nn.softmax(scores / np.sqrt(HEAD_DIM).astype(np.float32), axis=-1)
        ctx = jnp.einsum('bhqk,bhkd->bhqd', attn, v).transpose(0, 2, 1, 3).reshape(b, s, d)
        return ctx @ W_o_w.T + W_o_b

    def _L1_ffn_ref(x, gate_w, up_w, down_w, gate_s, up_s, down_s):
        import jax, jax.numpy as jnp
        import numpy as np
        HIDDEN = 256
        INTER = 704
        B, S = (2, 256)

        def _ternary(key, shape):
            return jax.random.randint(key, shape, -1, 2).astype(jnp.float32)
        b, s, h = x.shape
        xf = x.reshape(b * s, h)
        g = jnp.einsum('th,ih->ti', xf, gate_w) * gate_s
        u = jnp.einsum('th,ih->ti', xf, up_w) * up_s
        hdn = jax.nn.silu(g) * u
        out = jnp.einsum('ti,hi->th', hdn, down_w) * down_s
        return out.reshape(b, s, -1)
    x = L0_attn_x
    xn = _layernorm(x, axis=-1)
    x = x + _L0_attn_ref(xn, L0_attn_Wqk, L0_attn_bqk, L0_attn_Wv, L0_attn_bv, L0_attn_Wu, L0_attn_bu, L0_attn_Wo, L0_attn_bo, L0_attn_ln_g, L0_attn_ln_b) + _L0_ffn_ref(xn, L0_ffn_router_weight, L0_ffn_sh_gate, L0_ffn_sh_up, L0_ffn_sh_down, L0_ffn_r_gate, L0_ffn_r_up, L0_ffn_r_down)
    xn = _layernorm(x, axis=-1)
    x = x + _L1_attn_ref(xn, L1_attn_W_q, L1_attn_W_dkv, L1_attn_W_uk, L1_attn_W_uv, L1_attn_W_o_w, L1_attn_W_o_b) + _L1_ffn_ref(xn, L1_ffn_gate_w, L1_ffn_up_w, L1_ffn_down_w, L1_ffn_gate_s, L1_ffn_up_s, L1_ffn_down_s)
    return x

_drawn_inputs = setup_inputs


def setup_inputs(seed=0):
    import zlib

    import numpy as np

    out = dict(_drawn_inputs(seed))
    spreads = {'L0_attn_bqk': (0.0, 0.1),
     'L0_attn_bv': (0.0, 0.1),
     'L0_attn_bu': (0.0, 0.1),
     'L0_attn_bo': (0.0, 0.1),
     'L0_attn_ln_g': (1.0, 0.2),
     'L0_attn_ln_b': (0.0, 0.1)}
    factors = {'L0_ffn_router_weight': 64.0,
     'L0_ffn_r_gate': 5.288,
     'L0_ffn_r_up': 5.195,
     'L0_ffn_r_down': 5.177,
     'L1_attn_W_q': 8.0,
     'L1_attn_W_dkv': 8.0,
     'L1_attn_W_uk': 8.0,
     'L1_attn_W_uv': 8.0,
     'L1_attn_W_o_w': 8.0,
     'L1_attn_W_o_b': 21.012}
    for name, (base, spread) in spreads.items():
        noise = np.random.default_rng([zlib.crc32(name.encode()), seed]).standard_normal(out[name].shape)
        drawn = base * np.exp(spread * noise) if base else spread * noise
        out[name] = jnp.asarray(drawn.astype(out[name].dtype))
    for name, factor in factors.items():
        out[name] = (out[name] * factor).astype(out[name].dtype)
    return out
```

```python
from contextlib import ExitStack

import concourse.bass as bass
from concourse import mybir

F32 = mybir.dt.float32
F32R = mybir.dt.float32r
BF16 = mybir.dt.bfloat16
ALU = mybir.AluOpType
ACT = mybir.ActivationFunctionType
AX_X = mybir.AxisListType.X

P = 128
T = 2048
D = 256
HEADS = 16
DH = D // HEADS
BLK = 512
NB = T // BLK
TPB = BLK // P
KD = D // P
INTER = 1024
MS = INTER // P
M0 = MS + 1
NR = 8
LAT = 64
M1 = 6
EPS = 1e-5
PAIRS = HEADS // 2
STACK = 3 * DH
QK_SCALE = 1.0 / DH ** 0.5
HI, LO = 0, 1
PASSES = ((HI, HI), (HI, LO), (LO, HI))
NEG = -1e30
LEAD, LAG = 12, 2
NSTK = 3
RAW1 = KD * 512 + KD * 264 + KD * D + 2 * KD * M0 * P + M0 * D
RAW2 = KD * D + KD * 2 * LAT + 2 * D + 2 * KD * M1 * P + M1 * D + KD * D


def tally(plan, signals):
    count, table = {}, {}
    for step in plan:
        for name, n in signals[step[0]]:
            count[name] = count.get(name, 0) + n
            table[name, step] = count[name]
    return table


def stage1_plan():
    plan = [("ln", 0), ("w", 0), ("w", 1), ("T", 0, 0), ("T", 0, 1), ("wp", 2), ("proj", 0), ("w", 3), ("proj", 1),
            ("proj", 2), ("w", 4), ("proj", 3), ("w", 5), ("xb", 0)]
    for b in range(NB):
        for i in range(TPB):
            if b:
                plan.append(("proj", TPB * b + i))
            plan += [("ffn", b, 2 * i), ("ffn", b, 2 * i + 1)]
            if i == 1 and b + 1 < NB:
                plan += [("ln", b + 1), ("xb", b + 1)]
        if b + 1 < NB:
            plan.append(("T", b + 1, 0))
        plan += [("ffn", b, MS), ("comb", b), ("kv", b)]
        if b + 1 < NB:
            plan.append(("T", b + 1, 1))
        plan += [("down", TPB * b + i) for i in range(TPB)]
    return plan


SIGNALS1 = {
    "w": [("w_hi", 1), ("w_lo", 1)],
    "wp": [("w_hi", 1), ("wp_lo", 1)],
    "ln": [("stats", TPB), ("aggr", TPB), ("vareps", 1), ("rstd", 1), ("ln_done", TPB)],
    "xb": [("xb_done", 1)],
    "T": [("T_done", 1), ("T_hi", 1), ("T_lo", 1)],
    "proj": [("proj_done", 1), ("z_done", 2), ("top_done", 1), ("zrelu", 1), ("act_z", 2), ("q_done", 1), ("zt", 1), ("quv", 2)],
    "ffn": [("gu_done", 1), ("tanh_done", 1), ("w_done", 1), ("h_raw", 1), ("h_hi", 1), ("h_lo", 1)],
    "kv": [("kv_done", 1)],
    "comb": [("gap", 1), ("egap", 1), ("comb_step", 3)],
    "down": [("down_done", 1), ("routed", 1), ("res_done", 1)],
}


def stage2_plan():
    def chain(b):
        return {"qT": [("qT", b, 0)], "qT'": [("qT", b, 1)], "out": [("out", b, 0)], "out'": [("out", b, 1)],
                "oT": [("oT", b, 0)], "oT'": [("oT", b, 1)], "wo": [("wo", b, 0)],
                "wo'": [("wo", b, 1), ("ln2", b), ("xb2", b)], "xT": [("xT", b, 0)], "xT'": [("xT", b, 1)]}

    first = chain(0)
    plan = [("kvx",)] + first["qT"] + [("w2", 0)] + first["qT'"] + first["out"] + first["out'"]
    plan += [("w2", 1), ("w2", 2), ("w2", 3)] + first["oT"] + first["oT'"] + first["wo"] + first["wo'"]
    plan += [("w2s",), ("w2p", 5), ("w2", 4)] + first["xT"] + first["xT'"]
    for b in range(NB):
        nxt = chain(b + 1) if b + 1 < NB else dict.fromkeys(first, [])
        plan += [("q", b, 0)] + nxt["qT"] + [("q", b, 1), ("st", b, 0), ("c", b)] + nxt["qT'"]
        if b == 0:
            plan += [("w2d",), ("w2", 6), ("w2p", 7)]
        plan += [("f1", b, 0)] + nxt["out"] + [("k", b, 0)]
        plan += nxt["out'"] + [("k", b, 1), ("st", b, 1), ("f1", b, 1), ("v", b, 0)]
        plan += [("v", b, 1), ("f1", b, 2)] + nxt["oT"] + [("f1", b, 3)] + nxt["oT'"] + nxt["wo"] + nxt["wo'"]
        plan += [("f1", b, 4), ("f1", b, 5), ("d1", b, 0)] + nxt["xT"] + [("d1", b, 1)] + nxt["xT'"]
    return plan


SIGNALS2 = {
    "w2": [("w2_hi", 1), ("w2_lo", 1)],
    "w2p": [("w2_hi", 1), ("w2p_lo", 1)],
    "w2s": [("scaled", 2)],
    "w2d": [("down_scaled", 1)],
    "kvx": [("kv_raw", 1), ("kv_hi", 1), ("kv_lo", 1), ("ln_halved", 2)],
    "qT": [("T2_done", 1), ("T2_hi", 1), ("T2_lo", 1)],
    "oT": [("T2_done", 1), ("T2_hi", 1), ("T2_lo", 1)],
    "xT": [("T2_done", 1), ("T2_hi", 1), ("T2_lo", 1)],
    "out": [("nat_done", 1), ("o_stats", 2), ("o_aggr", 2), ("o_eps", 1), ("o_rstd", 1), ("o_centred", 1),
            ("o_norm", 2), ("o_gate", 1), ("nat_free", 1)],
    "wo": [("nat_done", 1), ("nat_free", 1)],
    "ln2": [("stats2", TPB), ("aggr2", TPB), ("vareps2", 1), ("rstd2", 1), ("ln2_done", TPB)],
    "xb2": [("xb2_done", 1)],
    "q": [("col_done", 1), ("col_hi", 1), ("col_lo", 1)],
    "k": [("col_done", 1), ("col_hi", 1), ("col_lo", 1)],
    "c": [("col_done", 1), ("col_hi", 1), ("col_lo", 1)],
    "v": [("nat_done", 1), ("nat_free", 1)],
    "f1": [("gu2_done", 1), ("tanh2_done", 1), ("w2_done", 1), ("h2_raw", 1), ("h2_hi", 1), ("h2_lo", 1)],
    "st": [("staged", 16 * 6)],
    "d1": [("nat_done", 1), ("nat_free", 1)],
}


def stage3_plan():
    steps = [(j, p) for j in range(NB) for p in range(PAIRS)]
    maxima, ends, begins, turn = [], [], [], []
    for s in steps:
        begins.append(len(maxima) + 1)
        maxima.append(("ld", *s))
        for n, unit in enumerate((i, c, e) for i in range(TPB) for c in range(s[0] + 1) for e in range(2)):
            maxima.append(("mx", *s, *unit))
            if n == 3:
                maxima += turn
        turn = [("mt", *s)]
        maxima.append(("mr", *s))
        ends.append(len(maxima) + 6)
    maxima += turn
    plan, done, products, extras = [], 0, [], []
    for n, s in enumerate(steps):
        count = TPB * (s[0] + 1)
        for kt in range(count):
            after = ends[n + 1] - ends[n] if n + 1 < len(steps) else 0
            goal = min(len(maxima), ends[n] + LEAD + kt * after // count)
            if n + NSTK < len(steps):
                goal = min(goal, begins[n + NSTK])
            goal = max(done, goal)
            half = max((done + goal) // 2, min(goal, ends[n]))
            plan += maxima[done:half]
            plan.append(("sxd" if kt >= TPB * s[0] else "sx", *s, kt))
            plan += maxima[half:goal]
            done = goal
            products.append(("pv", *s, kt))
            if len(products) > LAG:
                step = products.pop(0)
                plan.append(step)
                if step[3] == TPB * (step[1] + 1) - 1:
                    plan.append(("cx", *step[1:3]))
                    extras.append(("ct", *step[1:3]))
                    if step[2] == PAIRS - 1:
                        extras += [(kind, step[1], i) for i in range(TPB) for kind in ("fa", "fb")]
                elif extras:
                    plan.append(extras.pop(0))
    plan += products + extras
    plan += [("cx", *steps[-1]), ("ct", *steps[-1])] + [(k, NB - 1, i) for i in range(TPB) for k in ("fa", "fb")]
    return plan


SIGNALS3 = {
    "ld": [],
    "mx": [("mx_done", 1), ("mx_red", 1)],
    "mr": [("m_all", 1)],
    "mt": [("m_turned", 1), ("m_neg", 1)],
    "sx": [("s_done", 1), ("p_exp", 1)],
    "sxd": [("s_done", 1), ("p_exp", 1), ("p_masked", 1)],
    "pv": [("pv_done", 1)],
    "cx": [("cx_out", 1)],
    "ct": [("cx_turned", 1), ("cx_rden", 1), ("cx_norm", 2)],
    "fa": [("fin_turned", 1), ("fin_hi", 1), ("fin_lo", 1)],
    "fb": [("fin_done", 1), ("fin_sum", 1)],
}


def build(nc, A, out):
    plan1, plan2, plan3 = stage1_plan(), stage2_plan(), stage3_plan()
    at1, at2, at3 = tally(plan1, SIGNALS1), tally(plan2, SIGNALS2), tally(plan3, SIGNALS3)

    def before(plan, step, kinds, n=1):
        where = plan.index(step)
        for s in reversed(plan[:where]):
            if s[0] in kinds:
                n -= 1
                if n == 0:
                    return s
        return None

    ctx = ExitStack()
    with ctx:
        def sb(name, shape, dt=F32, scope=ctx):
            return scope.enter_context(nc.sbuf_tensor(name, shape, dt))

        x = sb("x_res", [P, T // P, D])
        ident = sb("ident", [P, P])
        mvar = sb("mvar", [P, 3, TPB, 2])
        stat = sb("stat", [P, 3, TPB, 6])
        rstd = sb("rstd_c", [P, 3, TPB])
        veps = sb("veps_c", [P, 3, TPB])
        mhalf = sb("mhalf", [P, TPB])
        s12 = ExitStack()
        qn = sb("qn", [P, T // P, D], F32, s12)
        un = sb("un", [P, T // P, D], F32, s12)
        wo0 = sb("wo0", [P, 2, KD, D], F32R, s12)
        lng = sb("lng", [P, D], F32, s12)
        lnb = sb("lnb", [P, D], F32, s12)
        kvr = sb("kvr", [P, 2, P], F32, s12)
        kvb = sb("kvb", [P, 2, 2, P], F32R, s12)
        bdmask = sb("bdmask", [P, P], F32, s12)
        s1, raw_scope = ExitStack(), ExitStack()
        wqv = sb("wqv", [P, 2, KD, 512], F32R, s1)
        wur = sb("wur", [P, 2, KD, 264], F32R, s1)
        wg = sb("wg", [P, 2, KD, M0 * P], F32R, s1)
        wup = sb("wup", [P, 2, KD, M0 * P], F32R, s1)
        wdn = sb("wdn", [P, 2, M0, D], F32R, s1)
        bias_z = sb("bias_z", [P, 776], F32, s1)
        bo0 = sb("bo0", [P, D], F32, s1)
        xT1 = sb("xT1", [P, 2, KD, BLK], F32R, s1)
        xn1 = sb("xn1", [P, TPB, D], F32, s1)
        z = sb("z", [P, 2, 776], F32, s1)
        zr = sb("zr", [P, 2, D], F32, s1)
        ez = sb("ez", [P, 2, D], F32, s1)
        tz = sb("tz", [P, 2, 2 * D], F32, s1)
        vn = sb("vn", [P, 2, TPB, D], F32, s1)
        tg1 = sb("tg1", [P, 2, BLK], F32, s1)
        hr1 = sb("hr1", [P, 2, BLK], F32, s1)
        raw1 = sb("raw1", [P, RAW1], F32, raw_scope)
        raw_scope.close()
        hT1 = sb("hT1", [P, 2, M0, BLK], F32R, s1)
        top = sb("top", [P, T // P, 8], F32, s1)
        gate = sb("gate", [P, 4, T // P], F32, s1)
        s1.close()
        s23 = ExitStack()
        vv = sb("vv", [P, T // P, HEADS, 32], F32, s23)
        wo1 = sb("wo1", [P, 2, KD, D], F32R, s23)
        s2, raw2_scope = ExitStack(), ExitStack()
        wq1 = sb("wq1", [P, 2, KD, D], F32R, s2)
        wc1 = sb("wc1", [P, 2, KD, 2 * LAT], F32R, s2)
        wk1 = sb("wk1", [LAT, 2, D], F32R, s2)
        wv1 = sb("wv1", [LAT, 2, D], F32R, s2)
        wg1 = sb("wg1", [P, 2, KD, M1 * P], F32R, s2)
        wu1 = sb("wu1", [P, 2, KD, M1 * P], F32R, s2)
        wd1 = sb("wd1", [P, 2, M1, D], F32R, s2)
        ones_row = sb("ones_row", [HEADS, 2, P], F32, s2)
        gs1 = sb("gs1", [P, M1], F32, s2)
        us1 = sb("us1", [P, M1], F32, s2)
        gus1 = sb("gus1", [P, M1], F32, s2)
        ds1 = sb("ds1", [P, D], F32, s2)
        bo1 = sb("bo1", [P, D], F32, s2)
        qT2 = sb("qT2", [P, 2, KD, BLK], F32R, s2)
        xT2 = sb("xT2", [P, 2, KD, BLK], F32R, s2)
        on = sb("on", [P, TPB, D], F32, s2)
        cT = sb("cT", [P, 2, BLK], F32R, s2)
        tg2 = sb("tg2", [P, 2, BLK], F32, s2)
        hr2 = sb("hr2", [P, 2, BLK], F32, s2)
        raw2 = sb("raw2", [P, RAW2], F32, raw2_scope)
        raw2_scope.close()
        qks = sb("qks", [P, 2, 2, BLK], F32R, s2)
        hT2 = sb("hT2", [P, 2, M1, BLK], F32R, s2)
        s2.close()
        ks = sb("ks", [P, NSTK, T], F32R, s23)
        qs = sb("qs", [P, NSTK, 2, BLK], F32R, s23)
        pr = sb("pr", [P, 4, 2, BLK], F32, s23)
        cmask = sb("cmask", [P, BLK], F32, s23)
        junk = sb("junk", [P, 2, BLK], BF16, s23)
        mxp = sb("mxp", [P, 2, 2 * TPB, NB], F32, s23)
        mall = sb("mall", [P, 2, 2 * TPB], F32, s23)
        mT = sb("mT", [2 * TPB, 2, P], F32R, s23)
        cxT = sb("cxT", [P, 2, 2 * P], F32, s23)
        rden = sb("rden", [P, 2, 2, 4], F32, s23)
        cx = sb("cx", [P, 2, TPB, D], F32, s23)
        fT = sb("fT", [P, 2, KD, P], F32R, s23)
        yo = sb("yo", [P, 2, D], F32, s23)
        s23.close()
        s12.close()

        bank = [ctx.enter_context(nc.psum_tensor(f"bank{i}", [P, 512], F32)) for i in range(4)]
        pairA = ctx.enter_context(nc.psum_tensor("pairA", [P, 2, 512], F32))
        pairB = ctx.enter_context(nc.psum_tensor("pairB", [P, 2, 512], F32))
        gu = [pairA, pairB]

        scr_q = nc.dram_tensor("scr_q", [HEADS, STACK + 1, T], F32, kind="Internal").ap()
        scr_k = nc.dram_tensor("scr_k", [HEADS, STACK + 1, T], F32, kind="Internal").ap()

        names = {n for sig in (SIGNALS1, SIGNALS2, SIGNALS3) for v in sig.values() for n, _ in v}
        names |= {"x_first", "x_rest", "z_bias_in", "qv_in", "gate_up_in", "down_in", "const_in", "mhalf_set",
                  "raw2_in", "vec2_in", "ones_set", "ones_stored", "vv_set", "cmask_in", "ident_in", "slot_zero"}
        names |= {f"stack_in{i}" for i in range(NSTK)} | {f"{n}{i}" for n in ("m_row", "fin_stored") for i in range(2)}
        S = {n: ctx.enter_context(nc.semaphore(n)) for n in sorted(names)}

        def wait1(eng, name, step):
            eng.wait_ge(S[name], at1[name, step])

        def wait2(eng, name, step):
            eng.wait_ge(S[name], at2[name, step])

        def wait3(eng, name, step):
            eng.wait_ge(S[name], at3[name, step])

        def wait_stacks(eng, j, p):
            s = j * PAIRS + p
            eng.wait_ge(S[f"stack_in{s % NSTK}"], 64 * (s // NSTK + 1))

        def wait_row(eng, s):
            eng.wait_ge(S[f"m_row{s % 2}"], 32 * (s // 2 + 1))

        def last(plan, kinds):
            return before(plan + [("end",)], ("end",), kinds)

        def stage1_over(eng):
            for name, kinds in (("down_done", "down"), ("kv_done", "kv"), ("res_done", "down"), ("h_hi", "ffn"),
                                ("h_lo", "ffn"), ("act_z", "proj"), ("quv", "proj"), ("q_done", "proj"), ("egap", "comb")):
                wait1(eng, name, last(plan1, (kinds,)))

        def stage2_over(eng):
            for name, kinds in (("nat_done", "d1"), ("nat_free", "d1"), ("col_lo", "k"), ("T2_hi", "xT"), ("T2_lo", "xT"),
                                ("h2_hi", "f1"), ("h2_lo", "f1"), ("o_gate", "out"), ("staged", "st")):
                wait2(eng, name, last(plan2, (kinds,)))

        def product(pe, out, lhsT, rhs, n, start=True, stop=True):
            steps = [(k, a, b) for k in range(n) for a, b in PASSES]
            for i, (k, a, b) in enumerate(steps):
                mm = pe.matmul(out, lhsT(a, k), rhs(b, k), start=start and i == 0, stop=stop and i == len(steps) - 1)
            return mm

        def tiles(i, w=P):
            return slice(i * w, (i + 1) * w)

        def landing(raw, shapes):
            at, views = 0, []
            for k, n in shapes:
                views.append(raw[:, at:at + k * n].rearrange("p (k n) -> p k n", k=k))
                at += k * n
            return views

        split1 = [wqv, wur, wg, wup, wdn, wo0]
        raw1v = landing(raw1, [(t.shape[2], t.shape[3]) for t in split1])
        scale1 = [1.0, 1.0, 1.0, 1.0, 0.5, 1.0]
        source1 = ["w_qv", "w_ur", "w_gate", "w_up", "w_down", "w_o"]
        arrived1 = [("qv_in", 32)] * 2 + [("gate_up_in", 32)] * 2 + [("down_in", 32)] * 2
        split2 = [wq1, wc1, wk1, wv1, wg1, wu1, wd1, wo1]
        raw2v = landing(raw2, [(KD, D), (KD, 2 * LAT), (1, D), (1, D), (KD, M1 * P), (KD, M1 * P), (M1, D), (KD, D)])
        source2 = ["w_q1", "w_c1", "w_k1", "w_v1", "w_gate1", "w_up1", "w_down1", "w_o1"]

        def halves2(i):
            if i in (2, 3):
                return raw2v[i][0:LAT, 0, :], split2[i][:, HI, :], split2[i][:, LO, :]
            return raw2v[i], split2[i][:, HI], split2[i][:, LO]

        bank_kv, bank_T, bank_n = bank[0], bank[1], bank[2:4]
        block = ctx.enter_context(nc.Block())

        @block.sync
        def _(sp):
            x_v = A["x"].rearrange("(n p) d -> p n d", p=P)
            sp.dma_start(x[:, 0:TPB, :], x_v[:, 0:TPB, :]).then_inc(S["x_first"], 16)
            for i in range(6):
                sp.dma_start(raw1v[i], A[source1[i]].rearrange("(k p) n -> p k n", p=P)).then_inc(S[arrived1[i][0]], 16)
                if i == 0:
                    sp.dma_start(ident[:], A["ident"]).then_inc(S["ident_in"], 16)
                if i == 1:
                    sp.dma_start(bias_z[:], A["bias_z"].partition_broadcast(P)).then_inc(S["z_bias_in"], 16)
            sp.dma_start(x[:, TPB:, :], x_v[:, TPB:, :]).then_inc(S["x_rest"], 16)
            sp.dma_start(bo0[:], A["b_o"].partition_broadcast(P)).then_inc(S["x_rest"], 16)
            sp.dma_start(lng[:], A["ln_g"].partition_broadcast(P)).then_inc(S["const_in"], 16)
            sp.dma_start(lnb[:], A["ln_b"].partition_broadcast(P)).then_inc(S["const_in"], 16)
            sp.dma_start(bdmask[:], A["head_mask"]).then_inc(S["const_in"], 16)

            stage1_over(sp)
            for i in range(8):
                if i in (2, 3):
                    sp.dma_start(raw2v[i][0:LAT, 0, :], A[source2[i]]).then_inc(S["raw2_in"], 16)
                else:
                    sp.dma_start(raw2v[i], A[source2[i]].rearrange("(k p) n -> p k n", p=P)).then_inc(S["raw2_in"], 16)
            sp.dma_start(gs1[:], A["gate_s1"]).then_inc(S["vec2_in"], 16)
            sp.dma_start(us1[:], A["up_s1"]).then_inc(S["vec2_in"], 16)
            sp.dma_start(ds1[:], A["down_s1"].partition_broadcast(P)).then_inc(S["vec2_in"], 16)
            sp.dma_start(bo1[:], A["b_o1"].partition_broadcast(P)).then_inc(S["vec2_in"], 16)
            sp.wait_ge(S["ones_set"], 2)
            for c in range(T // P):
                sp.dma_start(scr_k[:, STACK, tiles(c)], ones_row[:, 1, :]).then_inc(S["ones_stored"], 16)
                sp.dma_start(scr_q[:, STACK, tiles(c)], ones_row[:, 0, :]).then_inc(S["ones_stored"], 16)
            for step in plan2:
                if step[0] == "st":
                    _, b, which = step
                    wait2(sp, "col_lo", (("q", "k")[which], b, 1))
                    scratch, parts = ((scr_q, (HI, HI, LO)), (scr_k, (HI, LO, HI)))[which]
                    for hf in range(2):
                        for r, part in enumerate(parts):
                            sp.dma_start(scratch[hf * 8:(hf + 1) * 8, tiles(r, DH), tiles(b, BLK)],
                                         qks[:, part, hf, :].bitcast(F32)).then_inc(S["staged"], 16)

            stage2_over(sp)
            sp.wait_ge(S["ones_stored"], 2 * 16 * (T // P))
            sp.dma_start(cmask[:], A["causal"]).then_inc(S["cmask_in"], 16)
            out_v = out.rearrange("(n p) d -> p n d", p=P)
            for step in plan3:
                if step[0] == "ld":
                    _, j, p = step
                    s = j * PAIRS + p
                    if s < NSTK:
                        sp.wait_ge(S["slot_zero"], 2 * (s + 1))
                    else:
                        jj, pp = divmod(s - NSTK, PAIRS)
                        wait3(sp, "s_done", ("sxd", jj, pp, TPB * (jj + 1) - 1))
                    for e in range(2):
                        sp.dma_start(ks[64 * e:64 * e + STACK + 1, s % NSTK, 0:(j + 1) * BLK].bitcast(F32),
                                     scr_k[2 * p + e, :, 0:(j + 1) * BLK]).then_inc(S[f"stack_in{s % NSTK}"], 16)
                        sp.dma_start(qs[64 * e:64 * e + STACK + 1, s % NSTK, e, :].bitcast(F32),
                                     scr_q[2 * p + e, :, tiles(j, BLK)]).then_inc(S[f"stack_in{s % NSTK}"], 16)
                elif step[0] == "mt":
                    _, j, p = step
                    s = j * PAIRS + p
                    wait3(sp, "m_neg", step)
                    for e in range(2):
                        sp.dma_start(qs[64 * e + STACK:64 * e + STACK + 1, s % NSTK, e, :].bitcast(F32),
                                     mT[TPB * e:TPB * (e + 1), s % 2, :].bitcast(F32)).then_inc(S[f"m_row{s % 2}"], 16)
                elif step[0] == "fb":
                    _, j, i = step
                    wait3(sp, "fin_sum", step)
                    sp.dma_start(out_v[:, TPB * j + i, :], yo[:, i % 2, :]).then_inc(S[f"fin_stored{i % 2}"], 16)
            for parity in range(2):
                sp.wait_ge(S[f"fin_stored{parity}"], 16 * (T // P // 2))

        @block.tensor
        def _(pe):
            def turn(psum, src, i):
                return pe.transpose(psum, src, ident[:])

            pe.wait_ge(S["ident_in"], 16)
            for step in plan1:
                kind = step[0]
                if kind == "T":
                    _, b, k = step
                    wait1(pe, "ln_done", ("ln", b))
                    prev = before(plan1, step, ("T",))
                    if prev:
                        wait1(pe, "T_lo", prev)
                    for i in range(TPB):
                        mm = turn(bank_T[:, tiles(i)], xn1[:, i, tiles(k)], i)
                    mm.then_inc(S["T_done"], 1)
                elif kind == "proj":
                    n = step[1]
                    b, i = divmod(n, TPB)
                    if n == 0:
                        wait1(pe, "w_lo", ("w", 1))
                    wait1(pe, "T_lo", ("T", b, 1))
                    if n:
                        wait1(pe, "z_done", ("proj", n - 1))
                    if b:
                        wait1(pe, "res_done", ("down", TPB * b - 1))
                    lhs = lambda a, k: xT1[:, a, k, tiles(i)]
                    product(pe, bank_n[0][:], lhs, lambda a, k: wqv[:, a, k, :], KD)
                    product(pe, bank_n[1][:, 0:264], lhs, lambda a, k: wur[:, a, k, :], KD).then_inc(S["proj_done"], 1)
                elif kind == "ffn":
                    _, b, m = step
                    f = b * M0 + m
                    if f == 0:
                        wait1(pe, "wp_lo", ("wp", 2))
                        wait1(pe, "w_lo", ("w", 3))
                    if f >= 2:
                        wait1(pe, "h_raw", ("ffn", *divmod(f - 2, M0)))
                    rhs = lambda a, k: xT1[:, a, k, :]
                    product(pe, gu[f % 2][:, 0, :], lambda a, k: wg[:, a, k, tiles(m)], rhs, KD)
                    product(pe, gu[f % 2][:, 1, :], lambda a, k: wup[:, a, k, tiles(m)], rhs, KD).then_inc(S["gu_done"], 1)
                elif kind == "kv":
                    b = step[1]
                    for i in range(TPB):
                        n = TPB * b + i
                        wait1(pe, "quv", ("proj", n))
                        wait1(pe, "q_done", ("proj", n))
                        for hf in range(2):
                            mm = pe.matmul(bank_kv[:, tiles(hf)], qn[:, n, tiles(hf)], vn[:, b % 2, i, tiles(hf)],
                                           start=(n == 0 and hf == 0), stop=(n == T // P - 1), skip_group_check=True)
                    mm.then_inc(S["kv_done"], 1)
                elif kind == "down":
                    n = step[1]
                    b, i = divmod(n, TPB)
                    wait1(pe, "h_lo", ("ffn", b, MS))
                    wait1(pe, "z_done", ("proj", TPB * b + TPB - 1))
                    if n == 0:
                        wait1(pe, "w_lo", ("w", 4))
                    if n >= 2:
                        wait1(pe, "res_done", ("down", n - 2))
                    o = bank_n[n % 2]
                    product(pe, o[:, 0:D], lambda a, m: hT1[:, a, m, tiles(i)], lambda a, m: wdn[:, a, m, :], MS)
                    product(pe, o[:, D:], lambda a, m: hT1[:, a, MS, tiles(i)], lambda a, m: wdn[:, a, MS, :], 1)\
                        .then_inc(S["down_done"], 1)

            stage1_over(pe)
            for step in plan2:
                kind = step[0]
                if kind in ("qT", "oT", "xT"):
                    _, b, k = step
                    prev = before(plan2, step, ("qT", "oT", "xT"))
                    if prev:
                        wait2(pe, "T2_lo", prev)
                    if kind == "oT":
                        wait2(pe, "o_gate", ("out", b, 1))
                    if kind == "xT":
                        wait2(pe, "ln2_done", ("ln2", b))
                    for i in range(TPB):
                        src = qn[:, TPB * b + i, tiles(k)] if kind == "qT" else on[:, i, tiles(k)]
                        mm = turn(bank_T[:, tiles(i)], src, i)
                    mm.then_inc(S["T2_done"], 1)
                elif kind in ("out", "wo", "v", "d1"):
                    _, b, pair = step
                    u = at2["nat_done", step] - 1
                    o = bank_n[u % 2]
                    if u >= 2:
                        pe.wait_ge(S["nat_free"], u - 1)
                    if kind == "out":
                        wait2(pe, "kv_lo", ("kvx",))
                        wait2(pe, "T2_lo", ("qT", b, 1))
                    if kind == "wo":
                        wait2(pe, "T2_lo", ("oT", b, 1))
                        wait1(pe, "w_lo", ("w", 5))
                    if kind == "v":
                        wait2(pe, "col_lo", ("c", b))
                        wait2(pe, "w2_lo", ("w2", 3))
                    if kind == "d1":
                        wait2(pe, "h2_lo", ("f1", b, M1 - 1))
                        wait2(pe, "w2_lo", ("w2", 6))
                    for t in range(2):
                        i = 2 * pair + t
                        lhs = lambda a, k: qT2[:, a, k, tiles(i)]
                        if kind == "out":
                            for hf in range(2):
                                mm = product(pe, o[:, t * D + hf * P:t * D + hf * P + P],
                                             lambda a, k: qT2[:, a, hf, tiles(i)], lambda a, k: kvb[:, a, hf, :], 1)
                        elif kind == "wo":
                            mm = product(pe, o[:, tiles(t, D)], lhs, lambda a, k: wo0[:, a, k, :], KD)
                        elif kind == "v":
                            mm = product(pe, o[:, tiles(t, D)], lambda a, k: cT[0:LAT, a, tiles(i)],
                                         lambda a, k: wv1[:, a, :], 1)
                        else:
                            mm = product(pe, o[:, tiles(t, D)], lambda a, m: hT2[:, a, m, tiles(i)],
                                         lambda a, m: wd1[:, a, m, :], M1)
                    mm.then_inc(S["nat_done"], 1)
                elif kind in ("q", "c", "k"):
                    b = step[1]
                    prev = before(plan2, step, ("q", "c", "k"))
                    if prev:
                        wait2(pe, "col_lo", prev)
                    else:
                        wait2(pe, "kv_raw", ("kvx",))
                    rhs = lambda a, k: xT2[:, a, k, :]
                    if kind == "q":
                        wait2(pe, "T2_lo", ("xT", b, 1))
                        wait2(pe, "w2_lo", ("w2", 0))
                        mm = product(pe, bank[0][:], lambda a, k: wq1[:, a, k, tiles(step[2])], rhs, KD)
                    elif kind == "c":
                        wait2(pe, "w2_lo", ("w2", 1))
                        mm = product(pe, bank[0][:], lambda a, k: wc1[:, a, k, :], rhs, KD)
                    else:
                        wait2(pe, "col_lo", ("c", b))
                        wait2(pe, "w2_lo", ("w2", 2))
                        mm = product(pe, bank[0][:], lambda a, k: wk1[:, a, tiles(step[2])],
                                     lambda a, k: cT[0:LAT, a, :], 1)
                    mm.then_inc(S["col_done"], 1)
                elif kind == "f1":
                    _, b, m = step
                    f = b * M1 + m
                    if f == 0:
                        wait2(pe, "w2_lo", ("w2", 4))
                        wait2(pe, "w2p_lo", ("w2p", 5))
                    if f >= 2:
                        wait2(pe, "h2_raw", ("f1", *divmod(f - 2, M1)))
                    rhs = lambda a, k: xT2[:, a, k, :]
                    product(pe, gu[f % 2][:, 0, :], lambda a, k: wg1[:, a, k, tiles(m)], rhs, KD)
                    product(pe, gu[f % 2][:, 1, :], lambda a, k: wu1[:, a, k, tiles(m)], rhs, KD)\
                        .then_inc(S["gu2_done"], 1)

            stage2_over(pe)
            wait2(pe, "w2p_lo", ("w2p", 7))

            def misc_free(step):
                prev = before(plan3, step, ("mt", "ct", "fa", "fb"))
                if prev:
                    wait3(pe, {"mt": "m_neg", "ct": "cx_norm", "fa": "fin_lo", "fb": "fin_sum"}[prev[0]], prev)

            units = scores = 0
            for step in plan3:
                kind = step[0]
                if kind == "mx":
                    _, j, p, i, c, e = step
                    slot = (j * PAIRS + p) % NSTK
                    wait_stacks(pe, j, p)
                    w = BLK if c < j else (i + 1) * P
                    if units >= 2:
                        pe.wait_ge(S["mx_red"], units - 1)
                    pe.matmul(bank_n[units % 2][:, 0:w], qs[:, slot, e, tiles(i)], ks[:, slot, c * BLK:c * BLK + w],
                              start=True, stop=True).then_inc(S["mx_done"], 1)
                    units += 1
                elif kind == "mt":
                    _, j, p = step
                    wait3(pe, "m_all", ("mr", j, p))
                    misc_free(step)
                    pe.transpose(bank[1][0:2 * TPB, 0:P], mall[:, (j * PAIRS + p) % 2, :], ident[:])\
                        .then_inc(S["m_turned"], 1)
                elif kind in ("sx", "sxd"):
                    _, j, p, kt = step
                    slot = (j * PAIRS + p) % NSTK
                    off = max(0, kt - TPB * j) * P
                    wait_row(pe, j * PAIRS + p)
                    if scores >= 2:
                        pe.wait_ge(S["p_exp"], scores - 1)
                    for e in range(2):
                        mm = pe.matmul(gu[scores % 2][:, e, off:], ks[:, slot, tiles(kt)], qs[:, slot, e, off:],
                                       start=True, stop=True)
                    mm.then_inc(S["s_done"], 1)
                    scores += 1
                elif kind == "pv":
                    _, j, p, kt = step
                    own = ("sxd" if kt >= TPB * j else "sx", j, p, kt)
                    g = at3["s_done", own] - 1
                    off = max(0, kt - TPB * j) * P
                    wait3(pe, "p_masked" if own[0] == "sxd" else "p_exp", own)
                    if kt == 0 and (j or p):
                        wait3(pe, "cx_out", before(plan3, step, ("cx",)))
                    todo = [(e, hf) for hf in range(2) for e in range(2) if off < (hf + 1) * 2 * P]
                    for e, hf in todo:
                        lo = max(off, hf * 2 * P)
                        c = 2 * e + hf
                        mm = pe.matmul(bank[0][32 * c:32 * c + 32, lo - hf * 2 * P:2 * P], vv[:, kt, 2 * p + e, :],
                                       pr[:, g % 4, e, lo:(hf + 1) * 2 * P], start=(kt == 0),
                                       stop=(kt == TPB * j + 2 * hf + 1))
                    mm.then_inc(S["pv_done"], 1)
                elif kind == "ct":
                    _, j, p = step
                    wait3(pe, "cx_out", ("cx", j, p))
                    misc_free(step)
                    for t in range(2):
                        mm = pe.transpose(bank[1][:, tiles(t)], cxT[:, p % 2, tiles(t)], ident[:])
                    mm.then_inc(S["cx_turned"], 1)
                elif kind == "fa":
                    _, j, i = step
                    wait3(pe, "cx_norm", ("ct", j, PAIRS - 1))
                    misc_free(step)
                    for k in range(KD):
                        mm = pe.transpose(bank[1][:, tiles(k)], cx[:, j % 2, i, tiles(k)], ident[:])
                    mm.then_inc(S["fin_turned"], 1)
                elif kind == "fb":
                    _, j, i = step
                    wait3(pe, "fin_lo", ("fa", j, i))
                    misc_free(step)
                    product(pe, bank[1][:, 0:D], lambda a, k: fT[:, a, k, :], lambda a, k: wo1[:, a, k, :], KD)\
                        .then_inc(S["fin_done"], 1)

        @block.scalar
        def _(act):
            for step in plan1:
                kind = step[0]
                if kind in ("w", "wp"):
                    i = step[1]
                    act.wait_ge(S[arrived1[i][0]], arrived1[i][1])
                    act.activation(split1[i][:, HI], raw1v[i], ACT.Copy, scale=scale1[i]).then_inc(S["w_hi"], 1)
                elif kind == "T":
                    _, b, k = step
                    wait1(act, "T_done", step)
                    if b:
                        wait1(act, "gu_done", ("ffn", b - 1, MS))
                    act.activation(xT1[:, HI, k, :], bank_T[:], ACT.Copy).then_inc(S["T_hi"], 1)
                elif kind == "proj":
                    n = step[1]
                    wait1(act, "z_done", step)
                    if n >= 2:
                        wait1(act, "quv", ("proj", n - 2))
                        wait1(act, "q_done", ("proj", n - 2))
                    act.activation(ez[:, n % 2, :], z[:, n % 2, 0:D], ACT.Exp).then_inc(S["act_z"], 1)
                    act.activation(tz[:, n % 2, :], z[:, n % 2, D:3 * D], ACT.Tanh, scale=0.5).then_inc(S["act_z"], 1)
                elif kind == "ffn":
                    _, b, m = step
                    f = b * M0 + m
                    wait1(act, "gu_done", step)
                    if f >= 2:
                        wait1(act, "h_raw", ("ffn", *divmod(f - 2, M0)))
                    act.activation(tg1[:, f % 2, :], gu[f % 2][:, 0, :], ACT.Tanh, scale=0.5).then_inc(S["tanh_done"], 1)
                    wait1(act, "h_raw", step)
                    if f == 0:
                        wait1(act, "w_lo", ("w", 5))
                        wait1(act, "wp_lo", ("wp", 2))
                    if b:
                        wait1(act, "down_done", ("down", TPB * b - 1))
                    act.activation(hT1[:, HI, m, :], hr1[:, f % 2, :], ACT.Copy).then_inc(S["h_hi"], 1)
                elif kind == "comb":
                    b = step[1]
                    wait1(act, "gap", step)
                    act.activation(gate[:, 1, tiles(b, TPB)], gate[:, 0, tiles(b, TPB)], ACT.Exp).then_inc(S["egap"], 1)

            stage1_over(act)
            act.wait_ge(S["raw2_in"], 16 * 8)
            for step in plan2:
                kind = step[0]
                if kind in ("w2", "w2p"):
                    raw, hi, lo = halves2(step[1])
                    if step[1] == 6:
                        wait2(act, "down_scaled", ("w2d",))
                    act.activation(hi, raw, ACT.Copy).then_inc(S["w2_hi"], 1)
                elif kind == "kvx":
                    wait2(act, "kv_raw", step)
                    act.activation(kvb[:, HI], kvr[:], ACT.Copy).then_inc(S["kv_hi"], 1)
                elif kind in ("qT", "oT", "xT"):
                    _, b, k = step
                    wait2(act, "T2_done", step)
                    to = xT2 if kind == "xT" else qT2
                    act.activation(to[:, HI, k, :], bank_T[:], ACT.Copy).then_inc(S["T2_hi"], 1)
                elif kind in ("q", "k"):
                    _, b, hf = step
                    wait2(act, "col_done", step)
                    prev = before(plan2, step, ("st",))
                    if prev:
                        wait2(act, "staged", prev)
                    elif hf == 0:
                        wait2(act, "w2_lo", ("w2", 4))
                    act.activation(qks[:, HI, hf, :], bank[0][:], ACT.Copy).then_inc(S["col_hi"], 1)
                elif kind == "c":
                    wait2(act, "col_done", step)
                    act.activation(cT[0:LAT, HI, :], bank[0][0:LAT, :], ACT.Copy).then_inc(S["col_hi"], 1)
                elif kind == "f1":
                    _, b, m = step
                    f = b * M1 + m
                    wait2(act, "gu2_done", step)
                    if f == 0:
                        wait2(act, "scaled", ("w2s",))
                    if f >= 2:
                        wait2(act, "h2_raw", ("f1", *divmod(f - 2, M1)))
                    act.activation(tg2[:, f % 2, :], gu[f % 2][:, 0, :], ACT.Tanh, scale=gs1[:, m:m + 1])\
                        .then_inc(S["tanh2_done"], 1)
                    wait2(act, "h2_raw", step)
                    if f == 0:
                        wait2(act, "w2_lo", ("w2", 6))
                        wait2(act, "w2p_lo", ("w2p", 7))
                    if b:
                        wait2(act, "nat_done", ("d1", b - 1, 1))
                    act.activation(hT2[:, HI, m, :], hr2[:, f % 2, :], ACT.Copy).then_inc(S["h2_hi"], 1)

            stage2_over(act)
            for step in plan3:
                kind = step[0]
                if kind == "mt":
                    _, j, p = step
                    s = j * PAIRS + p
                    wait3(act, "m_turned", step)
                    if s >= 2:
                        wait_row(act, s - 2)
                    act.activation(mT[:, s % 2, :], bank[1][0:2 * TPB, 0:P], ACT.Copy, scale=-1.0)\
                        .then_inc(S["m_neg"], 1)
                elif kind in ("sx", "sxd"):
                    _, j, p, kt = step
                    g = at3["s_done", step] - 1
                    off = max(0, kt - TPB * j) * P
                    wait3(act, "s_done", step)
                    if g >= 4:
                        act.wait_ge(S["pv_done"], g - 3)
                    act.activation(pr[:, g % 4, :, off:], gu[g % 2][:, :, off:], ACT.Exp, scale=QK_SCALE)\
                        .then_inc(S["p_exp"], 1)
                elif kind == "cx":
                    _, j, p = step
                    wait3(act, "pv_done", ("pv", j, p, TPB * (j + 1) - 1))
                    s = j * PAIRS + p
                    if s >= 2:
                        wait3(act, "cx_turned", ("ct", *divmod(s - 2, PAIRS)))
                    act.activation(cxT[:, p % 2, :], bank[0][:, 0:2 * P], ACT.Copy).then_inc(S["cx_out"], 1)
                elif kind == "fa":
                    _, j, i = step
                    wait3(act, "fin_turned", step)
                    prev = before(plan3, step, ("fb",))
                    if prev:
                        wait3(act, "fin_done", prev)
                    act.activation(fT[:, HI], bank[1][:, 0:D].rearrange("p (k t) -> p k t", k=KD), ACT.Copy)\
                        .then_inc(S["fin_hi"], 1)

        @block.vector
        def _(dve):
            def normalise(which, source, to, count, sems, waits):
                stats, aggr, eps, rs, done = sems
                for i in range(count):
                    dve.bn_stats(stat[:, which, i, :], source(i)).then_inc(S[stats], 1)
                dve.wait_ge(S[stats], waits[stats])
                for i in range(count):
                    dve.bn_aggr(mvar[:, which, i, :], stat[:, which, i, :]).then_inc(S[aggr], 1)
                dve.wait_ge(S[aggr], waits[aggr])
                dve.tensor_scalar(veps[:, which, 0:count], mvar[:, which, 0:count, 1], EPS, None, ALU.add)\
                    .then_inc(S[eps], 1)
                dve.wait_ge(S[rs], waits[rs])
                for i in range(count):
                    dve.tensor_scalar(to(i), source(i), mvar[:, which, i, 0:1], rstd[:, which, i:i + 1],
                                      ALU.subtract, ALU.mult).then_inc(S[done[i]], 1)

            def normalise_gain(source, to, gain, bias, count, sems, waits):
                stats, aggr, eps, rs, centred, done = sems
                for i in range(count):
                    dve.bn_stats(stat[:, 1, i, :], source(i)).then_inc(S[stats], 1)
                dve.wait_ge(S[stats], waits[stats])
                for i in range(count):
                    dve.bn_aggr(mvar[:, 1, i, :], stat[:, 1, i, :]).then_inc(S[aggr], 1)
                dve.wait_ge(S[aggr], waits[aggr])
                dve.tensor_scalar(veps[:, 1, 0:count], mvar[:, 1, 0:count, 1], EPS, None, ALU.add).then_inc(S[eps], 1)
                for i in range(count):
                    dve.scalar_tensor_tensor(to(i), source(i), mvar[:, 1, i, 0:1], gain, ALU.subtract, ALU.mult)\
                        .then_inc(S[centred[i]], 1)
                dve.wait_ge(S[rs], waits[rs])
                for name in set(centred):
                    dve.wait_ge(S[name], waits[name])
                for i in range(count):
                    dve.scalar_tensor_tensor(to(i), to(i), rstd[:, 1, i:i + 1], bias, ALU.mult, ALU.add)\
                        .then_inc(S[done], 1)

            def low(out, raw, hi, sem, scale=1.0):
                if scale == 1.0:
                    dve.tensor_tensor(out, raw, hi, ALU.subtract).then_inc(S[sem], 1)
                else:
                    dve.scalar_tensor_tensor(out, raw, scale, hi, ALU.mult, ALU.subtract).then_inc(S[sem], 1)

            for step in plan1:
                kind = step[0]
                if kind == "ln":
                    b = step[1]
                    if b == 0:
                        dve.wait_ge(S["x_first"], 16)
                    else:
                        dve.wait_ge(S["x_rest"], 32)
                        wait1(dve, "T_done", ("T", b - 1, 1))
                        wait1(dve, "ln_done", ("ln", b - 1))
                    normalise(0, lambda i: x[:, TPB * b + i, :], lambda i: xn1[:, i, :], TPB,
                              ("stats", "aggr", "vareps", "rstd", ["ln_done"] * TPB),
                              {n: at1[n, step] for n in ("stats", "aggr", "rstd")})
                elif kind == "w":
                    i = step[1]
                    wait1(dve, "w_hi", step)
                    low(split1[i][:, LO], raw1v[i], split1[i][:, HI], "w_lo", scale1[i])
                elif kind == "T":
                    _, b, k = step
                    wait1(dve, "T_hi", step)
                    low(xT1[:, LO, k, :], bank_T[:], xT1[:, HI, k, :], "T_lo")
                elif kind == "proj":
                    n = step[1]
                    wait1(dve, "proj_done", step)
                    if n == 0:
                        dve.wait_ge(S["z_bias_in"], 16)
                    if n >= 2:
                        wait1(dve, "quv", ("proj", n - 2))
                        wait1(dve, "q_done", ("proj", n - 2))
                    dve.tensor_tensor(z[:, n % 2, 0:512], bank_n[0][:], bias_z[:, 0:512], ALU.add).then_inc(S["z_done"], 1)
                    dve.tensor_tensor(z[:, n % 2, 512:776], bank_n[1][:, 0:264], bias_z[:, 512:776], ALU.add)\
                        .then_inc(S["z_done"], 1)
                    wait1(dve, "z_done", step)
                    dve.tensor_scalar(zr[:, n % 2, :], z[:, n % 2, 0:D], 0.0, -1.0, ALU.max, ALU.add)\
                        .then_inc(S["zrelu"], 1)
                    dve.max(top[:, n, :], z[:, n % 2, 768:776]).then_inc(S["top_done"], 1)
                    wait1(dve, "act_z", step)
                    wait1(dve, "zrelu", step)
                    dve.scalar_tensor_tensor(qn[:, n, :], ez[:, n % 2, :], 1.0, zr[:, n % 2, :], ALU.min, ALU.add)\
                        .then_inc(S["q_done"], 1)
                elif kind == "ffn":
                    _, b, m = step
                    f = b * M0 + m
                    wait1(dve, "tanh_done", step)
                    dve.scalar_tensor_tensor(tg1[:, f % 2, :], tg1[:, f % 2, :], 1.0, gu[f % 2][:, 0, :],
                                             ALU.add, ALU.mult).then_inc(S["w_done"], 1)
                    if f >= 2:
                        wait1(dve, "h_lo", ("ffn", *divmod(f - 2, M0)))
                    wait1(dve, "w_done", step)
                    dve.tensor_tensor(hr1[:, f % 2, :], gu[f % 2][:, 1, :], tg1[:, f % 2, :], ALU.mult)\
                        .then_inc(S["h_raw"], 1)
                elif kind == "comb":
                    b = step[1]
                    sl = tiles(b, TPB)
                    wait1(dve, "top_done", ("proj", TPB * b + TPB - 1))
                    dve.tensor_tensor(gate[:, 0, sl], top[:, sl, 1], top[:, sl, 0], ALU.subtract).then_inc(S["gap"], 1)
                    wait1(dve, "egap", step)
                    c0 = at1["comb_step", step] - 3
                    dve.tensor_scalar(gate[:, 2, sl], gate[:, 1, sl], 1.0, None, ALU.add).then_inc(S["comb_step"], 1)
                    dve.wait_ge(S["comb_step"], c0 + 1)
                    dve.reciprocal(gate[:, 2, sl], gate[:, 2, sl]).then_inc(S["comb_step"], 1)
                    dve.wait_ge(S["comb_step"], c0 + 2)
                    dve.scalar_tensor_tensor(gate[:, 3, sl], gate[:, 1, sl], 1.0, gate[:, 2, sl], ALU.add, ALU.mult)\
                        .then_inc(S["comb_step"], 1)
                elif kind == "down":
                    n = step[1]
                    b = n // TPB
                    wait1(dve, "down_done", step)
                    wait1(dve, "comb_step", ("comb", b))
                    wait1(dve, "xb_done", ("xb", b))
                    o = bank_n[n % 2]
                    dve.scalar_tensor_tensor(x[:, n, :], o[:, D:], gate[:, 3, n:n + 1], x[:, n, :], ALU.mult, ALU.add)\
                        .then_inc(S["routed"], 1)
                    wait1(dve, "routed", step)
                    dve.tensor_tensor(x[:, n, :], o[:, 0:D], x[:, n, :], ALU.add).then_inc(S["res_done"], 1)

            stage1_over(dve)
            dve.wait_ge(S["raw2_in"], 16 * 8)
            dve.wait_ge(S["const_in"], 16 * 3)
            for step in plan2:
                kind = step[0]
                if kind == "w2":
                    raw, hi, lo = halves2(step[1])
                    wait2(dve, "w2_hi", step)
                    low(lo, raw, hi, "w2_lo")
                elif kind == "w2s":
                    dve.wait_ge(S["vec2_in"], 16 * 4)
                    s0 = at2["scaled", step] - 2
                    dve.tensor_tensor(gus1[:], gs1[:], us1[:], ALU.mult).then_inc(S["scaled"], 1)
                    dve.wait_ge(S["scaled"], s0 + 1)
                    dve.tensor_scalar(gs1[:], gs1[:], 0.5, None, ALU.mult).then_inc(S["scaled"], 1)
                elif kind == "w2d":
                    for_all = ds1[:].unsqueeze(1).broadcast_to([P, M1, D])
                    dve.scalar_tensor_tensor(raw2v[6], raw2v[6], 0.5, for_all, ALU.mult, ALU.mult)\
                        .then_inc(S["down_scaled"], 1)
                elif kind == "kvx":
                    for_both = bdmask[:].unsqueeze(1).broadcast_to([P, 2, P])
                    kv = bank_kv[:, 0:D].rearrange("p (h e) -> p h e", h=2)
                    dve.tensor_tensor(kvr[:], kv, for_both, ALU.mult).then_inc(S["kv_raw"], 1)
                    wait2(dve, "kv_hi", step)
                    wait2(dve, "kv_raw", step)
                    low(kvb[:, LO], kvr[:], kvb[:, HI], "kv_lo")
                    dve.tensor_scalar(lng[:], lng[:], 0.5, None, ALU.mult).then_inc(S["ln_halved"], 1)
                    dve.tensor_scalar(lnb[:], lnb[:], 0.5, None, ALU.mult).then_inc(S["ln_halved"], 1)
                elif kind in ("qT", "oT", "xT"):
                    _, b, k = step
                    to = xT2 if kind == "xT" else qT2
                    wait2(dve, "T2_hi", step)
                    low(to[:, LO, k, :], bank_T[:], to[:, HI, k, :], "T2_lo")
                elif kind == "out":
                    _, b, pair = step
                    o = bank_n[(at2["nat_done", step] - 1) % 2]
                    wait2(dve, "nat_done", step)
                    prev = before(plan2, step, ("out",))
                    if prev:
                        wait2(dve, "nat_free", prev)
                    if b:
                        wait2(dve, "T2_done", ("xT", b - 1, 1))
                    wait2(dve, "ln_halved", ("kvx",))
                    normalise_gain(lambda t: o[:, tiles(t, D)], lambda t: on[:, 2 * pair + t, :], lng[:], lnb[:], 2,
                                   ("o_stats", "o_aggr", "o_eps", "o_rstd", ["o_centred", "nat_free"], "o_norm"),
                                   {n: at2[n, step] for n in ("o_stats", "o_aggr", "o_rstd", "o_centred", "nat_free")})
                elif kind == "wo" or kind == "d1":
                    _, b, pair = step
                    o = bank_n[(at2["nat_done", step] - 1) % 2]
                    n = TPB * b + 2 * pair
                    wait2(dve, "nat_done", step)
                    if kind == "d1":
                        wait2(dve, "xb2_done", ("xb2", b))
                    dve.tensor_tensor(x[:, n:n + 2, :], o[:].rearrange("p (t d) -> p t d", t=2), x[:, n:n + 2, :], ALU.add)\
                        .then_inc(S["nat_free"], 1)
                elif kind == "ln2":
                    b = step[1]
                    wait2(dve, "nat_free", ("wo", b, 1))
                    wait2(dve, "T2_done", ("oT", b, 1))
                    if b:
                        wait2(dve, "ln2_done", ("ln2", b - 1))
                    normalise(2, lambda i: x[:, TPB * b + i, :], lambda i: on[:, i, :], TPB,
                              ("stats2", "aggr2", "vareps2", "rstd2", ["ln2_done"] * TPB),
                              {n: at2[n, step] for n in ("stats2", "aggr2", "rstd2")})
                elif kind in ("q", "k"):
                    hf = step[2]
                    wait2(dve, "col_hi", step)
                    low(qks[:, LO, hf, :], bank[0][:], qks[:, HI, hf, :], "col_lo")
                elif kind == "c":
                    wait2(dve, "col_hi", step)
                    low(cT[0:LAT, LO, :], bank[0][0:LAT, :], cT[0:LAT, HI, :], "col_lo")
                elif kind == "v":
                    _, b, pair = step
                    o = bank_n[(at2["nat_done", step] - 1) % 2]
                    n = TPB * b + 2 * pair
                    wait2(dve, "nat_done", step)
                    dve.wait_ge(S["vv_set"], 2)
                    dve.tensor_copy(vv[:, n:n + 2, :, 0:DH], o[:].rearrange("p (t h d) -> p t h d", t=2, h=HEADS))\
                        .then_inc(S["nat_free"], 1)
                elif kind == "f1":
                    _, b, m = step
                    f = b * M1 + m
                    wait2(dve, "tanh2_done", step)
                    dve.scalar_tensor_tensor(tg2[:, f % 2, :], tg2[:, f % 2, :], 1.0, gu[f % 2][:, 0, :],
                                             ALU.add, ALU.mult).then_inc(S["w2_done"], 1)
                    if f >= 2:
                        wait2(dve, "h2_lo", ("f1", *divmod(f - 2, M1)))
                    wait2(dve, "w2_done", step)
                    dve.scalar_tensor_tensor(hr2[:, f % 2, :], gu[f % 2][:, 1, :], gus1[:, m:m + 1], tg2[:, f % 2, :],
                                             ALU.mult, ALU.mult).then_inc(S["h2_raw"], 1)

            stage2_over(dve)
            dve.wait_ge(S["cmask_in"], 16)
            units = 0
            for step in plan3:
                kind = step[0]
                if kind == "mx":
                    _, j, p, i, c, e = step
                    scores = bank_n[units % 2]
                    dve.wait_ge(S["mx_done"], units + 1)
                    to = mxp[:, (j * PAIRS + p) % 2, TPB * e + i, c:c + 1]
                    if c < j:
                        dve.tensor_reduce(to, scores[:], AX_X, ALU.max).then_inc(S["mx_red"], 1)
                    else:
                        w = (i + 1) * P
                        if units >= 2:
                            dve.wait_ge(S["mx_red"], units - 1)
                        dve.tensor_tensor_reduce(junk[:, units % 2, 0:w], scores[:, 0:w], cmask[:, BLK - w:], 1.0, 0.0,
                                                 ALU.add, ALU.max, to).then_inc(S["mx_red"], 1)
                    units += 1
                elif kind == "mr":
                    _, j, p = step
                    s = j * PAIRS + p
                    dve.wait_ge(S["mx_red"], units)
                    if s >= 2:
                        wait3(dve, "m_turned", ("mt", *divmod(s - 2, PAIRS)))
                    dve.tensor_reduce(mall[:, s % 2, :], mxp[:, s % 2, :, 0:j + 1], AX_X, ALU.max).then_inc(S["m_all"], 1)
                elif kind == "ct":
                    _, j, p = step
                    wait3(dve, "cx_turned", step)
                    turned = bank[1][:, 0:2 * P].rearrange("p (t e h w) -> p t e h w", t=2, e=2, h=2)
                    den = bank[1][:, 0:2 * P].rearrange("p (t c w) -> p t c w", t=2, c=4)[:, :, :, DH]
                    prev = before(plan3, step, ("ct",))
                    if prev:
                        wait3(dve, "cx_norm", prev)
                    if j >= 2:
                        wait3(dve, "fin_turned", ("fa", j - 2, TPB - 1))
                    dve.reciprocal(rden[:, p % 2, :, :], den).then_inc(S["cx_rden"], 1)
                    wait3(dve, "cx_rden", step)
                    for t in range(2):
                        to = cx[:, j % 2].rearrange("p (h t) (g d) -> p t g h d", t=2, d=DH)[:, t, 2 * p:2 * p + 2]
                        scale = rden[:, p % 2, t, :].rearrange("p (e h) -> p e h", e=2).unsqueeze(3)\
                            .broadcast_to([P, 2, 2, DH])
                        dve.tensor_tensor(to, turned[:, t, :, :, 0:DH], scale, ALU.mult).then_inc(S["cx_norm"], 1)
                elif kind == "fa":
                    wait3(dve, "fin_hi", step)
                    low(fT[:, LO], bank[1][:, 0:D].rearrange("p (k t) -> p k t", k=KD), fT[:, HI], "fin_lo")
                elif kind == "fb":
                    _, j, i = step
                    n = TPB * j + i
                    wait3(dve, "fin_done", step)
                    if n >= 2:
                        dve.wait_ge(S[f"fin_stored{i % 2}"], 16 * (n // 2))
                    dve.tensor_tensor(yo[:, i % 2, :], bank[1][:, 0:D], x[:, n, :], ALU.add).then_inc(S["fin_sum"], 1)

        @block.gpsimd
        def _(pool):
            pool.memset(mhalf[:], -0.5).then_inc(S["mhalf_set"], 1)
            pool.wait_ge(S["mhalf_set"], 1)

            def power(which, count, sem_in, value, sem_out):
                pool.wait_ge(S[sem_in], value)
                pool.tensor_tensor(rstd[:, which, 0:count], veps[:, which, 0:count], mhalf[:, 0:count], ALU.pow)\
                    .then_inc(S[sem_out], 1)

            for step in plan1:
                kind = step[0]
                if kind == "ln":
                    if step[1]:
                        wait1(pool, "ln_done", ("ln", step[1] - 1))
                    power(0, TPB, "vareps", at1["vareps", step], "rstd")
                elif kind == "xb":
                    b = step[1]
                    wait1(pool, "ln_done", ("ln", b))
                    pool.wait_ge(S["x_rest"], 32)
                    sl = tiles(b, TPB)
                    pool.tensor_tensor(x[:, sl, :], x[:, sl, :], bo0[:].unsqueeze(1).broadcast_to([P, TPB, D]), ALU.add)\
                        .then_inc(S["xb_done"], 1)
                elif kind == "wp":
                    i = step[1]
                    wait1(pool, "w_hi", step)
                    pool.tensor_tensor(split1[i][:, LO], raw1v[i], split1[i][:, HI], ALU.subtract)\
                        .then_inc(S["wp_lo"], 1)
                elif kind == "proj":
                    n = step[1]
                    b, i = divmod(n, TPB)
                    if b >= 2:
                        wait1(pool, "kv_done", ("kv", b - 2))
                    wait1(pool, "act_z", step)
                    pool.tensor_tensor(tz[:, n % 2, :], tz[:, n % 2, :], z[:, n % 2, D:3 * D], ALU.mult)\
                        .then_inc(S["zt"], 1)
                    wait1(pool, "zt", step)
                    pool.tensor_tensor(vn[:, b % 2, i, :], tz[:, n % 2, 0:D], z[:, n % 2, D:2 * D], ALU.add)\
                        .then_inc(S["quv"], 1)
                    pool.tensor_tensor(un[:, n, :], tz[:, n % 2, D:], z[:, n % 2, 2 * D:3 * D], ALU.add)\
                        .then_inc(S["quv"], 1)
                elif kind == "ffn":
                    _, b, m = step
                    f = b * M0 + m
                    wait1(pool, "h_hi", step)
                    pool.tensor_tensor(hT1[:, LO, m, :], hr1[:, f % 2, :], hT1[:, HI, m, :], ALU.subtract)\
                        .then_inc(S["h_lo"], 1)

            stage1_over(pool)
            pool.memset(ones_row[:, 0], 0.0).then_inc(S["ones_set"], 1)
            pool.memset(ones_row[:, 1], 1.0).then_inc(S["ones_set"], 1)
            pool.memset(vv[:, :, :, DH + 1:], 0.0).then_inc(S["vv_set"], 1)
            pool.memset(vv[:, :, :, DH], 1.0).then_inc(S["vv_set"], 1)
            for step in plan2:
                kind = step[0]
                if kind == "w2p":
                    raw, hi, lo = halves2(step[1])
                    wait2(pool, "w2_hi", step)
                    pool.tensor_tensor(lo, raw, hi, ALU.subtract).then_inc(S["w2p_lo"], 1)
                elif kind == "out":
                    _, b, pair = step
                    prev = before(plan2, step, ("out",))
                    if prev:
                        wait2(pool, "nat_free", prev)
                    power(1, 2, "o_eps", at2["o_eps", step], "o_rstd")
                    wait2(pool, "o_norm", step)
                    sl = slice(2 * pair, 2 * pair + 2)
                    n = TPB * b + 2 * pair
                    pool.tensor_tensor(on[:, sl, :], on[:, sl, :], un[:, n:n + 2, :], ALU.mult).then_inc(S["o_gate"], 1)
                elif kind == "ln2":
                    b = step[1]
                    if b:
                        wait2(pool, "ln2_done", ("ln2", b - 1))
                    power(2, TPB, "vareps2", at2["vareps2", step], "rstd2")
                elif kind == "xb2":
                    b = step[1]
                    pool.wait_ge(S["vec2_in"], 16 * 4)
                    wait2(pool, "ln2_done", ("ln2", b))
                    sl = tiles(b, TPB)
                    pool.tensor_tensor(x[:, sl, :], x[:, sl, :], bo1[:].unsqueeze(1).broadcast_to([P, TPB, D]), ALU.add)\
                        .then_inc(S["xb2_done"], 1)
                elif kind == "f1":
                    _, b, m = step
                    f = b * M1 + m
                    wait2(pool, "h2_hi", step)
                    pool.tensor_tensor(hT2[:, LO, m, :], hr2[:, f % 2, :], hT2[:, HI, m, :], ALU.subtract)\
                        .then_inc(S["h2_lo"], 1)

            stage2_over(pool)
            for slot in range(NSTK):
                pool.memset(ks[:, slot, :].bitcast(F32), 0.0).then_inc(S["slot_zero"], 1)
                pool.memset(qs[:, slot].bitcast(F32), 0.0).then_inc(S["slot_zero"], 1)
            for step in plan3:
                if step[0] == "sxd":
                    _, j, p, kt = step
                    g = at3["s_done", step] - 1
                    off = (kt - TPB * j) * P
                    square = pr[:, g % 4, :, off:off + P]
                    wait3(pool, "p_exp", step)
                    pool.affine_select(out=square, in_=square, compare_op=ALU.is_ge, fill=0.0, base=0,
                                       pattern=[[0, 2], [1, P]], channel_multiplier=-1).then_inc(S["p_masked"], 1)


def kernel(**inputs):
    import numpy as np
    import concourse.bacc as bacc
    from concourse.bass_utils import run_bass_kernel_spmd

    a = {k: np.asarray(v) for k, v in inputs.items()}

    def padded(w, axis):
        pad = [(0, 0)] * w.ndim
        pad[axis] = (0, M1 * P - w.shape[axis])
        return np.pad(w, pad)

    keys = np.arange(BLK)[None, :] - (BLK - P)
    lanes = np.arange(P)
    f32 = np.float32
    laid = {
        "x": a["L0_attn_x"].reshape(T, D),
        "w_qv": np.concatenate([a["L0_attn_Wqk"], a["L0_attn_Wv"]], 1),
        "w_ur": np.concatenate([a["L0_attn_Wu"], a["L0_ffn_router_weight"].T], 1),
        "bias_z": np.concatenate([a["L0_attn_bqk"], a["L0_attn_bv"], a["L0_attn_bu"], np.zeros(NR, f32)]),
        "w_gate": np.concatenate([a["L0_ffn_sh_gate"], a["L0_ffn_r_gate"]], 0).T,
        "w_up": np.concatenate([a["L0_ffn_sh_up"], a["L0_ffn_r_up"]], 0).T,
        "w_down": np.concatenate([a["L0_ffn_sh_down"], a["L0_ffn_r_down"]], 1).T,
        "w_o": a["L0_attn_Wo"],
        "b_o": a["L0_attn_bo"],
        "ln_g": a["L0_attn_ln_g"],
        "ln_b": a["L0_attn_ln_b"],
        "w_q1": a["L1_attn_W_q"].T,
        "w_c1": np.concatenate([a["L1_attn_W_dkv"], a["L1_attn_W_dkv"]], 0).T,
        "w_k1": a["L1_attn_W_uk"].T,
        "w_v1": a["L1_attn_W_uv"].T,
        "w_gate1": padded(a["L1_ffn_gate_w"], 0).T,
        "w_up1": padded(a["L1_ffn_up_w"], 0).T,
        "w_down1": padded(a["L1_ffn_down_w"], 1).T,
        "w_o1": a["L1_attn_W_o_w"].T,
        "gate_s1": padded(a["L1_ffn_gate_s"], 0).reshape(M1, P).T,
        "up_s1": padded(a["L1_ffn_up_s"], 0).reshape(M1, P).T,
        "down_s1": a["L1_ffn_down_s"],
        "b_o1": a["L1_attn_W_o_b"],
        "ident": np.eye(P, dtype=f32),
        "head_mask": np.where(lanes[:, None] // DH == lanes[None, :] // DH, f32(0.5), f32(0.0)),
        "causal": np.where(keys > lanes[:, None], f32(NEG), f32(0.0)),
    }
    nc = bacc.Bacc("TRN2", target_bir_lowering=False, num_devices=1)
    arrays, aps = {}, {}
    for name, value in laid.items():
        value = np.ascontiguousarray(value)
        arrays[f"in_{name}"] = value
        aps[name] = nc.dram_tensor(f"in_{name}", value.shape, mybir.dt.from_np(value.dtype), kind="ExternalInput").ap()
    out = nc.dram_tensor("out_y", (T, D), F32, kind="ExternalOutput").ap()
    build(nc, aps, out)
    r = run_bass_kernel_spmd(nc, [arrays], core_ids=[0])
    return np.asarray(r.results[0]["out_y"]).reshape(1, T, D)
```

```python
from contextlib import ExitStack

import concourse.bass as bass
from concourse import mybir

F32 = mybir.dt.float32
F32R = mybir.dt.float32r
BF16 = mybir.dt.bfloat16
ALU = mybir.AluOpType
ACT = mybir.ActivationFunctionType
AX_X = mybir.AxisListType.X

P = 128
T = 2048
D = 256
HEADS = 16
DH = D // HEADS
BLK = 512
NB = T // BLK
TPB = BLK // P
KD = D // P
INTER = 1024
MS = INTER // P
M0 = MS + 1
NR = 8
LAT = 64
M1 = 6
EPS = 1e-5
PAIRS = HEADS // 2
STACK = 3 * DH
QK_SCALE = 1.0 / DH ** 0.5
HI, LO = 0, 1
PASSES = ((HI, HI), (HI, LO), (LO, HI))
NEG = -1e30
RIGHT = "right"
LEADS, LAG = (6, 8, 12, 12), 2
NSTK = 3
RAW1 = KD * 512 + KD * 264 + KD * D + 2 * KD * M0 * P + M0 * D
RAW2 = KD * D + KD * 2 * LAT + 2 * D + 2 * KD * M1 * P + M1 * D + KD * D


def tally(plan, signals):
    count, table = {}, {}
    for step in plan:
        for name, n in signals[step[0]]:
            count[name] = count.get(name, 0) + n
            table[name, step] = count[name]
    return table


def stage1_plan():
    plan = [("ln", 0), ("w", 0), ("w", 1), ("T", 0, 0), ("T", 0, 1), ("wp", 2), ("proj", 0), ("w", 3), ("proj", 1),
            ("proj", 2), ("w", 4), ("proj", 3), ("w", 5), ("xb", 0)]
    for b in range(NB):
        for i in range(TPB):
            if b:
                plan.append(("proj", TPB * b + i))
            plan += [("ffn", b, 2 * i), ("ffn", b, 2 * i + 1)]
            if i == 1 and b + 1 < NB:
                plan += [("ln", b + 1), ("xb", b + 1)]
        if b + 1 < NB:
            plan += [("T", b + 1, 0), ("ffn", b, MS), ("comb", b), ("kv", b), ("T", b + 1, 1)]
            plan += [("down", TPB * b + i) for i in range(TPB)]
    b = NB - 1
    plan.remove(("ffn", b, 2 * TPB - 1))
    plan += [("kv", b), ("ffn", b, 2 * TPB - 1), ("kvx",), ("qT", 0, 0), ("ffn", b, MS), ("comb", b), ("qT", 0, 1)]
    plan += [("out", 0, 0), ("out", 0, 1)] + [("down", TPB * b + i) for i in range(3)]
    plan += [("oT", 0, 0), ("down", T // P - 1), ("oT", 0, 1), ("wo", 0, 0), ("wo", 0, 1), ("ln2", 0), ("into2",)]
    return plan


SIGNALS1 = {
    "into2": [("ones_set", 2), ("vv_set", 2)], "into3": [("slot_zero", 2)], "spare": [("slot_zero", 4)],
    "w": [("w_hi", 1), ("w_lo", 1)],
    "wp": [("w_hi", 1), ("wp_lo", 1)],
    "ln": [("stats", TPB), ("aggr", TPB), ("vareps", 1), ("rstd", 1), ("ln_done", TPB)],
    "xb": [("xb_done", 1)],
    "T": [("T_done", 1), ("T_hi", 1), ("T_lo", 1)],
    "proj": [("proj_done", 1), ("z_done", 2), ("top_done", 1), ("zrelu", 1), ("act_z", 2), ("q_done", 1), ("zt", 1), ("quv", 2)],
    "ffn": [("gu_done", 1), ("tanh_done", 1), ("w_done", 1), ("h_raw", 1), ("h_hi", 1), ("h_lo", 1)],
    "kv": [("kv_done", 1)],
    "comb": [("gap", 1), ("egap", 1), ("comb_step", 3)],
    "down": [("down_done", 1), ("routed", 1), ("res_done", 1)],
}


def stage2_plan(head):
    def chain(b):
        return {"qT": [("qT", b, 0)], "qT'": [("qT", b, 1)], "out": [("out", b, 0)], "out'": [("out", b, 1)],
                "oT": [("oT", b, 0)], "oT'": [("oT", b, 1)], "wo": [("wo", b, 0)],
                "wo'": [("wo", b, 1), ("ln2", b), ("xb2", b)], "xT": [("xT", b, 0)], "xT'": [("xT", b, 1)]}

    plan = [("xb2", 0), ("xT", 0, 0), ("w2", 0), ("xT", 0, 1), ("w2", 1), ("w2", 2), ("w2", 3), ("w2s",), ("w2p", 5), ("w2", 4)]
    for b in range(NB):
        nxt = chain(b + 1) if b + 1 < NB else dict.fromkeys(chain(0), [])
        plan += [("q", b, 0)] + nxt["qT"]
        if b == 0:
            plan += [("w2d",), ("w2", 6), ("w2p", 7)]
        plan += [("f1", b, 0), ("q", b, 1), ("st", b, 0)] + nxt["qT'"]
        plan += [("f1", b, 1), ("c", b)] + nxt["out"] + nxt["out'"]
        if b == NB - 1:
            plan += [("spare",)]
        plan += [("f1", b, 2), ("k", b, 0), ("f1", b, 3), ("k", b, 1), ("st", b, 1)] + nxt["oT"]
        plan += [("f1", b, 4)] + nxt["oT'"] + nxt["wo"] + [("f1", b, 5)] + nxt["wo'"]
        plan += [("v", b, 0), ("v", b, 1)]
        if b == NB - 1:
            plan += head
        plan += [("d1", b, 0), ("d1", b, 1)] + nxt["xT"] + nxt["xT'"]
    plan += [("into3",)]
    return plan


SIGNALS2 = {
    "w2": [("w2_hi", 1), ("w2_lo", 1)],
    "w2p": [("w2_hi", 1), ("w2p_lo", 1)],
    "w2s": [("scaled", 2)],
    "w2d": [("down_scaled", 1)],
    "kvx": [("kv_raw", 1), ("kv_hi", 1), ("kv_lo", 1), ("ln_halved", 2)],
    "qT": [("T2_done", 1), ("T2_hi", 1), ("T2_lo", 1)],
    "oT": [("T2_done", 1), ("T2_hi", 1), ("T2_lo", 1)],
    "xT": [("T2_done", 1), ("T2_hi", 1), ("T2_lo", 1)],
    "out": [("nat_done", 1), ("o_stats", 2), ("o_aggr", 2), ("o_eps", 1), ("o_rstd", 1), ("o_centred", 1),
            ("o_norm", 2), ("o_gate", 1), ("nat_free", 1)],
    "wo": [("nat_done", 1), ("nat_free", 1)],
    "ln2": [("stats2", TPB), ("aggr2", TPB), ("vareps2", 1), ("rstd2", 1), ("ln2_done", TPB)],
    "xb2": [("xb2_done", 1)],
    "q": [("col_done", 1), ("col_hi", 1), ("col_lo", 1)],
    "k": [("col_done", 1), ("col_hi", 1), ("col_lo", 1)],
    "c": [("col_done", 1), ("col_hi", 1), ("col_lo", 1)],
    "v": [("nat_done", 1), ("nat_free", 1)],
    "f1": [("gu2_done", 1), ("tanh2_done", 1), ("w2_done", 1), ("h2_raw", 1), ("h2_hi", 1), ("h2_lo", 1)],
    "st": [("staged", 16 * 6)],
    "d1": [("nat_done", 1), ("nat_free", 1)],
}


def stage3_plan():
    steps = [(j, p) for j in range(NB) for p in range(PAIRS)]
    maxima, ends, begins, turn = [], [], [], []
    for n, s in enumerate(steps):
        begins.append(len(maxima))
        if n < NSTK:
            maxima.append(("ld", *s))
        for n, unit in enumerate((i, c, e) for i in range(TPB) for c in range(s[0] + 1) for e in range(2)):
            maxima.append(("mx", *s, *unit))
            if n == 3:
                maxima += turn
        turn = [("mt", *s)]
        maxima.append(("mr", *s))
        ends.append(len(maxima) + 6)
    maxima += turn
    plan, done, products, extras = [], 0, [], []
    for n, s in enumerate(steps):
        count = TPB * (s[0] + 1)
        for kt in range(count):
            after = ends[n + 1] - ends[n] if n + 1 < len(steps) else 0
            goal = min(len(maxima), ends[n] + LEADS[s[0]] + kt * after // count)
            if n + NSTK < len(steps):
                goal = min(goal, begins[n + NSTK])
            goal = max(done, goal)
            half = max((done + goal) // 2, min(goal, ends[n]))
            plan += maxima[done:half]
            plan.append(("sxd" if kt >= TPB * s[0] else "sx", *s, kt))
            if kt == count - 1 and n + NSTK < len(steps):
                plan.append(("ld", *steps[n + NSTK]))
            plan += maxima[half:goal]
            done = goal
            products.append(("pv", *s, kt))
            if len(products) > LAG:
                step = products.pop(0)
                plan.append(step)
                if step[3] == TPB * (step[1] + 1) - 1:
                    plan.append(("cx", *step[1:3]))
                    extras.append(("ct", *step[1:3]))
                    if step[2] == PAIRS - 1:
                        extras += [(kind, step[1], i) for i in range(TPB) for kind in ("fa", "fb")]
                elif extras:
                    plan.append(extras.pop(0))
    plan += products + extras
    plan += [("cx", *steps[-1]), ("ct", *steps[-1])] + [(k, NB - 1, i) for i in range(TPB) for k in ("fa", "fb")]
    return plan


SIGNALS3 = {
    "ld": [],
    "mx": [("mx_done", 1), ("mx_red", 1)],
    "mr": [("m_all", 1)],
    "mt": [("m_turned", 1), ("m_neg", 1)],
    "sx": [("s_done", 1), ("p_exp", 1)],
    "sxd": [("s_done", 1), ("p_exp", 1), ("p_masked", 1)],
    "pv": [("pv_done", 1)],
    "cx": [("cx_out", 1)],
    "ct": [("cx_turned", 1), ("cx_rden", 1), ("cx_norm", 2)],
    "fa": [("fin_turned", 1), ("fin_hi", 1), ("fin_lo", 1)],
    "fb": [("fin_done", 1), ("fin_sum", 1)],
}


def build(nc, A, out):
    plan3 = stage3_plan()
    cut = min(plan3.index(("sxd", 0, 0, 0)), plan3.index(("ld", 0, 2)))
    plan = stage1_plan() + stage2_plan(plan3[:cut]) + plan3[cut:]
    at = tally(plan, {**SIGNALS1, **SIGNALS2, **SIGNALS3})

    def before(step, kinds, n=1):
        where = plan.index(step) if step else len(plan)
        for s in reversed(plan[:where]):
            if s[0] in kinds:
                n -= 1
                if n == 0:
                    return s
        return None

    ctx = ExitStack()
    with ctx:
        def sb(name, shape, dt=F32, scope=ctx, side=None):
            return scope.enter_context(nc.sbuf_tensor(name, shape, dt, side=side))

        x = sb("x_res", [P, T // P, D])
        ident = sb("ident", [P, P])
        mvar = sb("mvar", [P, 3, TPB, 2])
        stat = sb("stat", [P, 3, TPB, 6])
        rstd = sb("rstd_c", [P, 3, TPB])
        veps = sb("veps_c", [P, 3, TPB])
        mhalf = sb("mhalf", [P, TPB])
        s12 = ExitStack()
        qn = sb("qn", [P, T // P, D], F32, s12, RIGHT)
        un = sb("un", [P, T // P, D], F32, s12, RIGHT)
        lng = sb("lng", [P, D], F32, s12, RIGHT)
        bdmask = sb("bdmask", [P, P], F32, s12, RIGHT)
        lnb = sb("lnb", [P, D], F32, s12, RIGHT)
        wo0 = sb("wo0", [P, 2, KD, D], F32R, s12, RIGHT)
        kvr = sb("kvr", [P, 2, P], F32, s12, RIGHT)
        kvb = sb("kvb", [P, 2, 2, P], F32R, s12, RIGHT)
        wqv = sb("wqv", [P, 2, KD, 512], F32R, s12, RIGHT)
        xn1 = sb("xn1", [P, TPB, D], F32, s12, RIGHT)
        qT2 = wqv
        on = xn1
        s1, raw_scope = ExitStack(), ExitStack()
        wur = sb("wur", [P, 2, KD, 264], F32R, s1)
        wg = sb("wg", [P, 2, KD, M0 * P], F32R, s1)
        wup = sb("wup", [P, 2, KD, M0 * P], F32R, s1)
        wdn = sb("wdn", [P, 2, M0, D], F32R, s1)
        bias_z = sb("bias_z", [P, 776], F32, s1)
        bo0 = sb("bo0", [P, D], F32, s1)
        xT1 = sb("xT1", [P, 2, KD, BLK], F32R, s1)
        z = sb("z", [P, 2, 776], F32, s1)
        zr = sb("zr", [P, 2, D], F32, s1)
        ez = sb("ez", [P, 2, D], F32, s1)
        tz = sb("tz", [P, 2, 2 * D], F32, s1)
        vn = sb("vn", [P, 2, TPB, D], F32, s1)
        tg1 = sb("tg1", [P, 2, BLK], F32, s1)
        hr1 = sb("hr1", [P, 2, BLK], F32, s1)
        raw1 = sb("raw1", [P, RAW1], F32, raw_scope)
        raw_scope.close()
        hT1 = sb("hT1", [P, 2, M0, BLK], F32R, s1)
        top = sb("top", [P, T // P, 8], F32, s1)
        gate = sb("gate", [P, 4, T // P], F32, s1)
        s1.close()
        s23 = ExitStack()
        vv = sb("vv", [P, T // P, HEADS, 32], F32, s23)
        wo1 = sb("wo1", [P, 2, KD, D], F32R, s23)
        s2, raw2_scope = ExitStack(), ExitStack()
        wq1 = sb("wq1", [P, 2, KD, D], F32R, s2)
        wc1 = sb("wc1", [P, 2, KD, 2 * LAT], F32R, s2)
        wk1 = sb("wk1", [LAT, 2, D], F32R, s2)
        wv1 = sb("wv1", [LAT, 2, D], F32R, s2)
        wg1 = sb("wg1", [P, 2, KD, M1 * P], F32R, s2)
        wu1 = sb("wu1", [P, 2, KD, M1 * P], F32R, s2)
        wd1 = sb("wd1", [P, 2, M1, D], F32R, s2)
        ones_row = sb("ones_row", [HEADS, 2, P], F32, s2)
        gs1 = sb("gs1", [P, M1], F32, s2)
        us1 = sb("us1", [P, M1], F32, s2)
        gus1 = sb("gus1", [P, M1], F32, s2)
        ds1 = sb("ds1", [P, D], F32, s2)
        bo1 = sb("bo1", [P, D], F32, s2)
        xT2 = sb("xT2", [P, 2, KD, BLK], F32R, s2)
        cT = sb("cT", [P, 2, BLK], F32R, s2)
        tg2 = sb("tg2", [P, 2, BLK], F32, s2)
        hr2 = sb("hr2", [P, 2, BLK], F32, s2)
        raw2 = sb("raw2", [P, RAW2], F32, raw2_scope)
        raw2_scope.close()
        qks = sb("qks", [P, 2, 2, BLK], F32R, s2)
        hT2 = sb("hT2", [P, 2, M1, BLK], F32R, s2)
        s2.close()
        s12.close()
        early = ExitStack()
        ks01 = sb("ks01", [P, 2, T], F32R, early, RIGHT)
        qs = sb("qs", [P, NSTK, 2, BLK], F32R, early, RIGHT)
        cmask = sb("cmask", [P, BLK], F32, early, RIGHT)
        junk = sb("junk", [P, 2, BLK], BF16, early, RIGHT)
        mT = sb("mT", [2 * TPB, 2, P], F32R, early, RIGHT)
        mxp = sb("mxp", [P, 2, 2 * TPB, NB], F32, early, RIGHT)
        mall = sb("mall", [P, 2, 2 * TPB], F32, early, RIGHT)
        ks2 = sb("ks2", [P, T], F32R, s23)
        ks = [ks01[:, 0, :], ks01[:, 1, :], ks2[:]]
        pr = sb("pr", [P, 4, 2, BLK], F32, s23)
        cxT = sb("cxT", [P, 2, 2 * P], F32, s23)
        rden = sb("rden", [P, 2, 2, 4], F32, s23)
        cx = sb("cx", [P, 2, TPB, D], F32, s23)
        fT = sb("fT", [P, 2, KD, P], F32R, s23)
        yo = sb("yo", [P, 2, D], F32, s23)
        s23.close()
        early.close()

        bank = [ctx.enter_context(nc.psum_tensor(f"bank{i}", [P, 512], F32)) for i in range(4)]
        pairA = ctx.enter_context(nc.psum_tensor("pairA", [P, 2, 512], F32))
        pairB = ctx.enter_context(nc.psum_tensor("pairB", [P, 2, 512], F32))
        gu = [pairA, pairB]

        scr_q = nc.dram_tensor("scr_q", [HEADS, STACK + 1, T], F32, kind="Internal").ap()
        scr_k = nc.dram_tensor("scr_k", [HEADS, STACK + 1, T], F32, kind="Internal").ap()

        names = {n for sig in (SIGNALS1, SIGNALS2, SIGNALS3) for v in sig.values() for n, _ in v}
        names |= {"x_first", "x_rest", "z_bias_in", "qv_in", "gate_up_in", "down_in", "const_in", "mhalf_set",
                  "small2_in", "large2_in", "vec2_in", "ones_set", "ones_stored", "vv_set", "cmask_in", "ident_in", "slot_zero"}
        names |= {f"stack_in{i}" for i in range(NSTK)} | {f"{n}{i}" for n in ("m_row", "fin_stored") for i in range(2)}
        S = {n: ctx.enter_context(nc.semaphore(n)) for n in sorted(names)}

        def wait(eng, name, step):
            eng.wait_ge(S[name], at[name, step])

        def wait_stacks(eng, j, p):
            s = j * PAIRS + p
            eng.wait_ge(S[f"stack_in{s % NSTK}"], 64 * (s // NSTK + 1))

        def wait_row(eng, s):
            eng.wait_ge(S[f"m_row{s % 2}"], 32 * (s // 2 + 1))

        def last(kind):
            return before(None, (kind,))

        def stage1_over(eng):
            for name, kinds in (("down_done", "down"), ("kv_done", "kv"), ("res_done", "down"), ("h_hi", "ffn"),
                                ("h_lo", "ffn"), ("act_z", "proj"), ("quv", "proj"), ("q_done", "proj"), ("egap", "comb")):
                wait(eng, name, last(kinds))

        def stage2_over(eng):
            for name, kinds in (("nat_done", "d1"), ("nat_free", "d1"), ("col_lo", "k"), ("T2_hi", "xT"), ("T2_lo", "xT"),
                                ("h2_hi", "f1"), ("h2_lo", "f1"), ("o_gate", "out"), ("staged", "st")):
                wait(eng, name, last(kinds))

        def product(pe, out, lhsT, rhs, n, start=True, stop=True):
            steps = [(k, a, b) for k in range(n) for a, b in PASSES]
            for i, (k, a, b) in enumerate(steps):
                mm = pe.matmul(out, lhsT(a, k), rhs(b, k), start=start and i == 0, stop=stop and i == len(steps) - 1)
            return mm

        def tiles(i, w=P):
            return slice(i * w, (i + 1) * w)

        def landing(raw, shapes):
            at, views = 0, []
            for k, n in shapes:
                views.append(raw[:, at:at + k * n].rearrange("p (k n) -> p k n", k=k))
                at += k * n
            return views

        split1 = [wqv, wur, wg, wup, wdn, wo0]
        raw1v = landing(raw1, [(t.shape[2], t.shape[3]) for t in split1])
        scale1 = [1.0, 1.0, 1.0, 1.0, 0.5, 1.0]
        source1 = ["w_qv", "w_ur", "w_gate", "w_up", "w_down", "w_o"]
        arrived1 = [("qv_in", 32)] * 2 + [("gate_up_in", 32)] * 2 + [("down_in", 32)] * 2
        split2 = [wq1, wc1, wk1, wv1, wg1, wu1, wd1, wo1]
        raw2v = landing(raw2, [(KD, D), (KD, 2 * LAT), (1, D), (1, D), (KD, M1 * P), (KD, M1 * P), (M1, D), (KD, D)])
        arrived2 = [("small2_in", 64)] * 4 + [("large2_in", 64)] * 4
        source2 = ["w_q1", "w_c1", "w_k1", "w_v1", "w_gate1", "w_up1", "w_down1", "w_o1"]

        def halves2(i):
            if i in (2, 3):
                return raw2v[i][0:LAT, 0, :], split2[i][:, HI, :], split2[i][:, LO, :]
            return raw2v[i], split2[i][:, HI], split2[i][:, LO]

        bank_kv, bank_T, bank_n = bank[0], bank[1], bank[2:4]
        shared_free = {"T": "T_lo", "qT": "T2_lo", "oT": "T2_lo", "xT": "T2_lo",
                       "mt": "m_neg", "ct": "cx_norm", "fa": "fin_lo", "fb": "fin_sum"}
        nat_free = {"proj": "z_done", "down": "res_done", "out": "nat_free", "wo": "nat_free", "v": "nat_free",
                    "d1": "nat_free", "mx": "mx_red"}
        turn_of = {"down": "down_done", "mx": "mx_done"}

        def nat_bank(step):
            return None if step[0] == "proj" else (at[turn_of.get(step[0], "nat_done"), step] - 1) % 2

        nat_users = {}
        holder = [None, None]
        for s in plan:
            if s[0] in nat_free:
                mine = (0, 1) if nat_bank(s) is None else (nat_bank(s),)
                nat_users[s] = [h for i, h in enumerate(holder) if i in mine and h]
                for i in mine:
                    holder[i] = s

        def wait_nat(pe, step):
            for user in nat_users[step]:
                wait(pe, nat_free[user[0]], user)

        def wait_shared(pe, step):
            prev = before(step, tuple(shared_free))
            if prev:
                wait(pe, shared_free[prev[0]], prev)

        block = ctx.enter_context(nc.Block())

        @block.sync
        def _(sp):
            x_v = A["x"].rearrange("(n p) d -> p n d", p=P)
            sp.dma_start(x[:, 0:TPB, :], x_v[:, 0:TPB, :]).then_inc(S["x_first"], 16)
            for i in range(6):
                sp.dma_start(raw1v[i], A[source1[i]].rearrange("(k p) n -> p k n", p=P)).then_inc(S[arrived1[i][0]], 16)
                if i == 0:
                    sp.dma_start(ident[:], A["ident"]).then_inc(S["ident_in"], 16)
                if i == 1:
                    sp.dma_start(bias_z[:], A["bias_z"].partition_broadcast(P)).then_inc(S["z_bias_in"], 16)
            sp.dma_start(x[:, TPB:, :], x_v[:, TPB:, :]).then_inc(S["x_rest"], 16)
            sp.dma_start(bo0[:], A["b_o"].partition_broadcast(P)).then_inc(S["x_rest"], 16)
            sp.dma_start(lng[:], A["ln_g"].partition_broadcast(P)).then_inc(S["const_in"], 16)
            sp.dma_start(lnb[:], A["ln_b"].partition_broadcast(P)).then_inc(S["const_in"], 16)
            sp.dma_start(bdmask[:], A["head_mask"]).then_inc(S["const_in"], 16)

            stage1_over(sp)
            for i in range(8):
                to = raw2v[i][0:LAT, 0, :] if i in (2, 3) else raw2v[i]
                source = A[source2[i]] if i in (2, 3) else A[source2[i]].rearrange("(k p) n -> p k n", p=P)
                sp.dma_start(to, source).then_inc(S[arrived2[i][0]], 16)
            sp.dma_start(gs1[:], A["gate_s1"]).then_inc(S["vec2_in"], 16)
            sp.dma_start(us1[:], A["up_s1"]).then_inc(S["vec2_in"], 16)
            sp.dma_start(ds1[:], A["down_s1"].partition_broadcast(P)).then_inc(S["vec2_in"], 16)
            sp.dma_start(bo1[:], A["b_o1"].partition_broadcast(P)).then_inc(S["vec2_in"], 16)
            sp.wait_ge(S["ones_set"], 2)
            for c in range(T // P):
                sp.dma_start(scr_k[:, STACK, tiles(c)], ones_row[:, 1, :]).then_inc(S["ones_stored"], 16)
                sp.dma_start(scr_q[:, STACK, tiles(c)], ones_row[:, 0, :]).then_inc(S["ones_stored"], 16)
            out_v = out.rearrange("(n p) d -> p n d", p=P)
            for step in plan:
                if step[0] == "st":
                    _, b, which = step
                    wait(sp, "col_lo", (("q", "k")[which], b, 1))
                    scratch, parts = ((scr_q, (HI, HI, LO)), (scr_k, (HI, LO, HI)))[which]
                    for hf in range(2):
                        for r, part in enumerate(parts):
                            sp.dma_start(scratch[hf * 8:(hf + 1) * 8, tiles(r, DH), tiles(b, BLK)],
                                         qks[:, part, hf, :].bitcast(F32)).then_inc(S["staged"], 16)

                elif step[0] == "ld":
                    _, j, p = step
                    s = j * PAIRS + p
                    if s == 0:
                        wait(sp, "staged", last("st"))
                        sp.wait_ge(S["ones_stored"], 2 * 16 * (T // P))
                        wait(sp, "o_gate", last("out"))
                        sp.dma_start(cmask[:], A["causal"]).then_inc(S["cmask_in"], 16)
                    if s < NSTK:
                        sp.wait_ge(S["slot_zero"], 2 * (s + 1))
                    else:
                        jj, pp = divmod(s - NSTK, PAIRS)
                        wait(sp, "s_done", ("sxd", jj, pp, TPB * (jj + 1) - 1))
                    for e in range(2):
                        sp.dma_start(ks[s % NSTK][64 * e:64 * e + STACK + 1, 0:(j + 1) * BLK].bitcast(F32),
                                     scr_k[2 * p + e, :, 0:(j + 1) * BLK]).then_inc(S[f"stack_in{s % NSTK}"], 16)
                        sp.dma_start(qs[64 * e:64 * e + STACK + 1, s % NSTK, e, :].bitcast(F32),
                                     scr_q[2 * p + e, :, tiles(j, BLK)]).then_inc(S[f"stack_in{s % NSTK}"], 16)
                elif step[0] == "mt":
                    _, j, p = step
                    s = j * PAIRS + p
                    wait(sp, "m_neg", step)
                    for e in range(2):
                        sp.dma_start(qs[64 * e + STACK:64 * e + STACK + 1, s % NSTK, e, :].bitcast(F32),
                                     mT[TPB * e:TPB * (e + 1), s % 2, :].bitcast(F32)).then_inc(S[f"m_row{s % 2}"], 16)
                elif step[0] == "fb":
                    _, j, i = step
                    wait(sp, "fin_sum", step)
                    sp.dma_start(out_v[:, TPB * j + i, :], yo[:, i % 2, :]).then_inc(S[f"fin_stored{i % 2}"], 16)
            for parity in range(2):
                sp.wait_ge(S[f"fin_stored{parity}"], 16 * (T // P // 2))

        @block.tensor
        def _(pe):
            def turn(psum, src, i):
                return pe.transpose(psum, src, ident[:])

            pe.wait_ge(S["ident_in"], 16)
            scores = 0
            for step in plan:
                kind = step[0]
                if kind == "into2":
                    stage1_over(pe)
                elif kind == "into3":
                    stage2_over(pe)
                    wait(pe, "w2p_lo", ("w2p", 7))
                elif kind == "T":
                    _, b, k = step
                    wait(pe, "ln_done", ("ln", b))
                    wait_shared(pe, step)
                    for i in range(TPB):
                        mm = turn(bank_T[:, tiles(i)], xn1[:, i, tiles(k)], i)
                    mm.then_inc(S["T_done"], 1)
                elif kind == "proj":
                    n = step[1]
                    b, i = divmod(n, TPB)
                    if n == 0:
                        wait(pe, "w_lo", ("w", 1))
                    wait(pe, "T_lo", ("T", b, 1))
                    wait_nat(pe, step)
                    lhs = lambda a, k: xT1[:, a, k, tiles(i)]
                    product(pe, bank_n[0][:], lhs, lambda a, k: wqv[:, a, k, :], KD)
                    product(pe, bank_n[1][:, 0:264], lhs, lambda a, k: wur[:, a, k, :], KD).then_inc(S["proj_done"], 1)
                elif kind == "ffn":
                    _, b, m = step
                    f = b * M0 + m
                    if f == 0:
                        wait(pe, "wp_lo", ("wp", 2))
                        wait(pe, "w_lo", ("w", 3))
                    if f >= 2:
                        wait(pe, "h_raw", ("ffn", *divmod(f - 2, M0)))
                    rhs = lambda a, k: xT1[:, a, k, :]
                    product(pe, gu[f % 2][:, 0, :], lambda a, k: wg[:, a, k, tiles(m)], rhs, KD)
                    product(pe, gu[f % 2][:, 1, :], lambda a, k: wup[:, a, k, tiles(m)], rhs, KD).then_inc(S["gu_done"], 1)
                elif kind == "kv":
                    b = step[1]
                    for i in range(TPB):
                        n = TPB * b + i
                        wait(pe, "quv", ("proj", n))
                        wait(pe, "q_done", ("proj", n))
                        for hf in range(2):
                            mm = pe.matmul(bank_kv[:, tiles(hf)], qn[:, n, tiles(hf)], vn[:, b % 2, i, tiles(hf)],
                                           start=(n == 0 and hf == 0), stop=(n == T // P - 1), skip_group_check=True)
                    mm.then_inc(S["kv_done"], 1)
                elif kind == "down":
                    n = step[1]
                    b, i = divmod(n, TPB)
                    wait(pe, "h_lo", ("ffn", b, MS))
                    wait_nat(pe, step)
                    if n == 0:
                        wait(pe, "w_lo", ("w", 4))
                    o = bank_n[n % 2]
                    product(pe, o[:, 0:D], lambda a, m: hT1[:, a, m, tiles(i)], lambda a, m: wdn[:, a, m, :], MS)
                    product(pe, o[:, D:], lambda a, m: hT1[:, a, MS, tiles(i)], lambda a, m: wdn[:, a, MS, :], 1)\
                        .then_inc(S["down_done"], 1)

                elif kind in ("qT", "oT", "xT"):
                    _, b, k = step
                    wait_shared(pe, step)
                    if kind == "oT":
                        wait(pe, "o_gate", ("out", b, 1))
                    if kind == "xT":
                        wait(pe, "ln2_done", ("ln2", b))
                    for i in range(TPB):
                        src = qn[:, TPB * b + i, tiles(k)] if kind == "qT" else on[:, i, tiles(k)]
                        mm = turn(bank_T[:, tiles(i)], src, i)
                    mm.then_inc(S["T2_done"], 1)
                elif kind in ("out", "wo", "v", "d1"):
                    _, b, pair = step
                    o = bank_n[nat_bank(step)]
                    wait_nat(pe, step)
                    if kind == "out":
                        wait(pe, "kv_lo", ("kvx",))
                        wait(pe, "T2_lo", ("qT", b, 1))
                    if kind == "wo":
                        wait(pe, "T2_lo", ("oT", b, 1))
                        wait(pe, "w_lo", ("w", 5))
                    if kind == "v":
                        wait(pe, "col_lo", ("c", b))
                        wait(pe, "w2_lo", ("w2", 3))
                    if kind == "d1":
                        wait(pe, "h2_lo", ("f1", b, M1 - 1))
                        wait(pe, "w2_lo", ("w2", 6))
                    for t in range(2):
                        i = 2 * pair + t
                        lhs = lambda a, k: qT2[:, a, k, tiles(i)]
                        if kind == "out":
                            for hf in range(2):
                                mm = product(pe, o[:, t * D + hf * P:t * D + hf * P + P],
                                             lambda a, k: qT2[:, a, hf, tiles(i)], lambda a, k: kvb[:, a, hf, :], 1)
                        elif kind == "wo":
                            mm = product(pe, o[:, tiles(t, D)], lhs, lambda a, k: wo0[:, a, k, :], KD)
                        elif kind == "v":
                            mm = product(pe, o[:, tiles(t, D)], lambda a, k: cT[0:LAT, a, tiles(i)],
                                         lambda a, k: wv1[:, a, :], 1)
                        else:
                            mm = product(pe, o[:, tiles(t, D)], lambda a, m: hT2[:, a, m, tiles(i)],
                                         lambda a, m: wd1[:, a, m, :], M1)
                    mm.then_inc(S["nat_done"], 1)
                elif kind in ("q", "c", "k"):
                    b = step[1]
                    prev = before(step, ("q", "c", "k"))
                    if prev:
                        wait(pe, "col_lo", prev)
                    else:
                        wait(pe, "kv_raw", ("kvx",))
                    rhs = lambda a, k: xT2[:, a, k, :]
                    if kind == "q":
                        wait(pe, "T2_lo", ("xT", b, 1))
                        wait(pe, "w2_lo", ("w2", 0))
                        mm = product(pe, bank[0][:], lambda a, k: wq1[:, a, k, tiles(step[2])], rhs, KD)
                    elif kind == "c":
                        wait(pe, "w2_lo", ("w2", 1))
                        mm = product(pe, bank[0][:], lambda a, k: wc1[:, a, k, :], rhs, KD)
                    else:
                        wait(pe, "col_lo", ("c", b))
                        wait(pe, "w2_lo", ("w2", 2))
                        mm = product(pe, bank[0][:], lambda a, k: wk1[:, a, tiles(step[2])],
                                     lambda a, k: cT[0:LAT, a, :], 1)
                    mm.then_inc(S["col_done"], 1)
                elif kind == "f1":
                    _, b, m = step
                    f = b * M1 + m
                    if f == 0:
                        wait(pe, "w2_lo", ("w2", 4))
                        wait(pe, "w2p_lo", ("w2p", 5))
                    if f >= 2:
                        wait(pe, "h2_raw", ("f1", *divmod(f - 2, M1)))
                    rhs = lambda a, k: xT2[:, a, k, :]
                    product(pe, gu[f % 2][:, 0, :], lambda a, k: wg1[:, a, k, tiles(m)], rhs, KD)
                    product(pe, gu[f % 2][:, 1, :], lambda a, k: wu1[:, a, k, tiles(m)], rhs, KD)\
                        .then_inc(S["gu2_done"], 1)

                elif kind == "mx":
                    _, j, p, i, c, e = step
                    slot = (j * PAIRS + p) % NSTK
                    wait_stacks(pe, j, p)
                    w = BLK if c < j else (i + 1) * P
                    wait_nat(pe, step)
                    pe.matmul(bank_n[nat_bank(step)][:, 0:w], qs[:, slot, e, tiles(i)], ks[slot][:, c * BLK:c * BLK + w],
                              start=True, stop=True).then_inc(S["mx_done"], 1)
                elif kind == "mt":
                    _, j, p = step
                    wait(pe, "m_all", ("mr", j, p))
                    wait_shared(pe, step)
                    pe.transpose(bank[1][0:2 * TPB, 0:P], mall[:, (j * PAIRS + p) % 2, :], ident[:])\
                        .then_inc(S["m_turned"], 1)
                elif kind in ("sx", "sxd"):
                    _, j, p, kt = step
                    slot = (j * PAIRS + p) % NSTK
                    off = max(0, kt - TPB * j) * P
                    wait_row(pe, j * PAIRS + p)
                    if scores >= 2:
                        pe.wait_ge(S["p_exp"], scores - 1)
                    for e in range(2):
                        mm = pe.matmul(gu[scores % 2][:, e, off:], ks[slot][:, tiles(kt)], qs[:, slot, e, off:],
                                       start=True, stop=True)
                    mm.then_inc(S["s_done"], 1)
                    scores += 1
                elif kind == "pv":
                    _, j, p, kt = step
                    own = ("sxd" if kt >= TPB * j else "sx", j, p, kt)
                    g = at["s_done", own] - 1
                    off = max(0, kt - TPB * j) * P
                    wait(pe, "p_masked" if own[0] == "sxd" else "p_exp", own)
                    if kt == 0 and (j or p):
                        wait(pe, "cx_out", before(step, ("cx",)))
                    todo = [(e, hf) for hf in range(2) for e in range(2) if off < (hf + 1) * 2 * P]
                    for e, hf in todo:
                        lo = max(off, hf * 2 * P)
                        c = 2 * e + hf
                        mm = pe.matmul(bank[0][32 * c:32 * c + 32, lo - hf * 2 * P:2 * P], vv[:, kt, 2 * p + e, :],
                                       pr[:, g % 4, e, lo:(hf + 1) * 2 * P], start=(kt == 0),
                                       stop=(kt == TPB * j + 2 * hf + 1))
                    mm.then_inc(S["pv_done"], 1)
                elif kind == "ct":
                    _, j, p = step
                    wait(pe, "cx_out", ("cx", j, p))
                    wait_shared(pe, step)
                    for t in range(2):
                        mm = pe.transpose(bank[1][:, tiles(t)], cxT[:, p % 2, tiles(t)], ident[:])
                    mm.then_inc(S["cx_turned"], 1)
                elif kind == "fa":
                    _, j, i = step
                    wait(pe, "cx_norm", ("ct", j, PAIRS - 1))
                    wait_shared(pe, step)
                    for k in range(KD):
                        mm = pe.transpose(bank[1][:, tiles(k)], cx[:, j % 2, i, tiles(k)], ident[:])
                    mm.then_inc(S["fin_turned"], 1)
                elif kind == "fb":
                    _, j, i = step
                    wait(pe, "fin_lo", ("fa", j, i))
                    wait_shared(pe, step)
                    product(pe, bank[1][:, 0:D], lambda a, k: fT[:, a, k, :], lambda a, k: wo1[:, a, k, :], KD)\
                        .then_inc(S["fin_done"], 1)

        @block.scalar
        def _(act):
            for step in plan:
                kind = step[0]
                if kind == "into2":
                    stage1_over(act)
                elif kind == "into3":
                    stage2_over(act)
                elif kind in ("w", "wp"):
                    i = step[1]
                    act.wait_ge(S[arrived1[i][0]], arrived1[i][1])
                    act.activation(split1[i][:, HI], raw1v[i], ACT.Copy, scale=scale1[i]).then_inc(S["w_hi"], 1)
                elif kind == "T":
                    _, b, k = step
                    wait(act, "T_done", step)
                    if b:
                        wait(act, "gu_done", ("ffn", b - 1, MS))
                    act.activation(xT1[:, HI, k, :], bank_T[:], ACT.Copy).then_inc(S["T_hi"], 1)
                elif kind == "proj":
                    n = step[1]
                    wait(act, "z_done", step)
                    if n >= 2:
                        wait(act, "quv", ("proj", n - 2))
                        wait(act, "q_done", ("proj", n - 2))
                    act.activation(ez[:, n % 2, :], z[:, n % 2, 0:D], ACT.Exp).then_inc(S["act_z"], 1)
                    act.activation(tz[:, n % 2, :], z[:, n % 2, D:3 * D], ACT.Tanh, scale=0.5).then_inc(S["act_z"], 1)
                elif kind == "ffn":
                    _, b, m = step
                    f = b * M0 + m
                    wait(act, "gu_done", step)
                    if f >= 2:
                        wait(act, "h_raw", ("ffn", *divmod(f - 2, M0)))
                    act.activation(tg1[:, f % 2, :], gu[f % 2][:, 0, :], ACT.Tanh, scale=0.5).then_inc(S["tanh_done"], 1)
                    wait(act, "h_raw", step)
                    if f == 0:
                        wait(act, "w_lo", ("w", 5))
                        wait(act, "wp_lo", ("wp", 2))
                    if b:
                        wait(act, "down_done", ("down", TPB * b - 1))
                    act.activation(hT1[:, HI, m, :], hr1[:, f % 2, :], ACT.Copy).then_inc(S["h_hi"], 1)
                elif kind == "comb":
                    b = step[1]
                    wait(act, "gap", step)
                    act.activation(gate[:, 1, tiles(b, TPB)], gate[:, 0, tiles(b, TPB)], ACT.Exp).then_inc(S["egap"], 1)

                elif kind in ("w2", "w2p"):
                    raw, hi, lo = halves2(step[1])
                    act.wait_ge(S[arrived2[step[1]][0]], arrived2[step[1]][1])
                    if step[1] == 6:
                        wait(act, "down_scaled", ("w2d",))
                    act.activation(hi, raw, ACT.Copy).then_inc(S["w2_hi"], 1)
                elif kind == "kvx":
                    wait(act, "kv_raw", step)
                    act.activation(kvb[:, HI], kvr[:], ACT.Copy).then_inc(S["kv_hi"], 1)
                elif kind in ("qT", "oT", "xT"):
                    _, b, k = step
                    wait(act, "T2_done", step)
                    if kind == "qT" and b == 0:
                        wait(act, "proj_done", last("proj"))
                    to = xT2 if kind == "xT" else qT2
                    act.activation(to[:, HI, k, :], bank_T[:], ACT.Copy).then_inc(S["T2_hi"], 1)
                elif kind in ("q", "k"):
                    _, b, hf = step
                    wait(act, "col_done", step)
                    prev = before(step, ("st",))
                    if prev:
                        wait(act, "staged", prev)
                    elif hf == 0:
                        wait(act, "w2_lo", ("w2", 4))
                    act.activation(qks[:, HI, hf, :], bank[0][:], ACT.Copy).then_inc(S["col_hi"], 1)
                elif kind == "c":
                    wait(act, "col_done", step)
                    act.activation(cT[0:LAT, HI, :], bank[0][0:LAT, :], ACT.Copy).then_inc(S["col_hi"], 1)
                elif kind == "f1":
                    _, b, m = step
                    f = b * M1 + m
                    wait(act, "gu2_done", step)
                    if f == 0:
                        wait(act, "scaled", ("w2s",))
                    if f >= 2:
                        wait(act, "h2_raw", ("f1", *divmod(f - 2, M1)))
                    act.activation(tg2[:, f % 2, :], gu[f % 2][:, 0, :], ACT.Tanh, scale=gs1[:, m:m + 1])\
                        .then_inc(S["tanh2_done"], 1)
                    wait(act, "h2_raw", step)
                    if f == 0:
                        wait(act, "w2_lo", ("w2", 6))
                        wait(act, "w2p_lo", ("w2p", 7))
                    if b:
                        wait(act, "nat_done", ("d1", b - 1, 1))
                    act.activation(hT2[:, HI, m, :], hr2[:, f % 2, :], ACT.Copy).then_inc(S["h2_hi"], 1)

                elif kind == "mt":
                    _, j, p = step
                    s = j * PAIRS + p
                    if s == 0:
                        wait(act, "nat_free", last("out"))
                    wait(act, "m_turned", step)
                    if s >= 2:
                        wait_row(act, s - 2)
                    act.activation(mT[:, s % 2, :], bank[1][0:2 * TPB, 0:P], ACT.Copy, scale=-1.0)\
                        .then_inc(S["m_neg"], 1)
                elif kind in ("sx", "sxd"):
                    _, j, p, kt = step
                    g = at["s_done", step] - 1
                    off = max(0, kt - TPB * j) * P
                    wait(act, "s_done", step)
                    if g >= 4:
                        act.wait_ge(S["pv_done"], g - 3)
                    act.activation(pr[:, g % 4, :, off:], gu[g % 2][:, :, off:], ACT.Exp, scale=QK_SCALE)\
                        .then_inc(S["p_exp"], 1)
                elif kind == "cx":
                    _, j, p = step
                    wait(act, "pv_done", ("pv", j, p, TPB * (j + 1) - 1))
                    s = j * PAIRS + p
                    if s >= 2:
                        wait(act, "cx_turned", ("ct", *divmod(s - 2, PAIRS)))
                    act.activation(cxT[:, p % 2, :], bank[0][:, 0:2 * P], ACT.Copy).then_inc(S["cx_out"], 1)
                elif kind == "fa":
                    _, j, i = step
                    wait(act, "fin_turned", step)
                    prev = before(step, ("fb",))
                    if prev:
                        wait(act, "fin_done", prev)
                    act.activation(fT[:, HI], bank[1][:, 0:D].rearrange("p (k t) -> p k t", k=KD), ACT.Copy)\
                        .then_inc(S["fin_hi"], 1)

        @block.vector
        def _(dve):
            def normalise(which, source, to, count, sems, waits):
                stats, aggr, eps, rs, done = sems
                for i in range(count):
                    dve.bn_stats(stat[:, which, i, :], source(i)).then_inc(S[stats], 1)
                dve.wait_ge(S[stats], waits[stats])
                for i in range(count):
                    dve.bn_aggr(mvar[:, which, i, :], stat[:, which, i, :]).then_inc(S[aggr], 1)
                dve.wait_ge(S[aggr], waits[aggr])
                dve.tensor_scalar(veps[:, which, 0:count], mvar[:, which, 0:count, 1], EPS, None, ALU.add)\
                    .then_inc(S[eps], 1)
                dve.wait_ge(S[rs], waits[rs])
                for i in range(count):
                    dve.tensor_scalar(to(i), source(i), mvar[:, which, i, 0:1], rstd[:, which, i:i + 1],
                                      ALU.subtract, ALU.mult).then_inc(S[done[i]], 1)

            def normalise_gain(source, to, gain, bias, count, sems, waits):
                stats, aggr, eps, rs, centred, done = sems
                for i in range(count):
                    dve.bn_stats(stat[:, 1, i, :], source(i)).then_inc(S[stats], 1)
                dve.wait_ge(S[stats], waits[stats])
                for i in range(count):
                    dve.bn_aggr(mvar[:, 1, i, :], stat[:, 1, i, :]).then_inc(S[aggr], 1)
                dve.wait_ge(S[aggr], waits[aggr])
                dve.tensor_scalar(veps[:, 1, 0:count], mvar[:, 1, 0:count, 1], EPS, None, ALU.add).then_inc(S[eps], 1)
                for i in range(count):
                    dve.scalar_tensor_tensor(to(i), source(i), mvar[:, 1, i, 0:1], gain, ALU.subtract, ALU.mult)\
                        .then_inc(S[centred[i]], 1)
                dve.wait_ge(S[rs], waits[rs])
                for name in set(centred):
                    dve.wait_ge(S[name], waits[name])
                for i in range(count):
                    dve.scalar_tensor_tensor(to(i), to(i), rstd[:, 1, i:i + 1], bias, ALU.mult, ALU.add)\
                        .then_inc(S[done], 1)

            def low(out, raw, hi, sem, scale=1.0):
                if scale == 1.0:
                    dve.tensor_tensor(out, raw, hi, ALU.subtract).then_inc(S[sem], 1)
                else:
                    dve.scalar_tensor_tensor(out, raw, scale, hi, ALU.mult, ALU.subtract).then_inc(S[sem], 1)

            for step in plan:
                kind = step[0]
                if kind == "into2":
                    stage1_over(dve)
                elif kind == "into3":
                    stage2_over(dve)
                elif kind == "ln":
                    b = step[1]
                    if b == 0:
                        dve.wait_ge(S["x_first"], 16)
                    else:
                        dve.wait_ge(S["x_rest"], 32)
                        wait(dve, "T_done", ("T", b - 1, 1))
                        wait(dve, "ln_done", ("ln", b - 1))
                    normalise(0, lambda i: x[:, TPB * b + i, :], lambda i: xn1[:, i, :], TPB,
                              ("stats", "aggr", "vareps", "rstd", ["ln_done"] * TPB),
                              {n: at[n, step] for n in ("stats", "aggr", "rstd")})
                elif kind == "w":
                    i = step[1]
                    wait(dve, "w_hi", step)
                    low(split1[i][:, LO], raw1v[i], split1[i][:, HI], "w_lo", scale1[i])
                elif kind == "T":
                    _, b, k = step
                    wait(dve, "T_hi", step)
                    low(xT1[:, LO, k, :], bank_T[:], xT1[:, HI, k, :], "T_lo")
                elif kind == "proj":
                    n = step[1]
                    wait(dve, "proj_done", step)
                    if n == 0:
                        dve.wait_ge(S["z_bias_in"], 16)
                    if n >= 2:
                        wait(dve, "quv", ("proj", n - 2))
                        wait(dve, "q_done", ("proj", n - 2))
                    dve.tensor_tensor(z[:, n % 2, 0:512], bank_n[0][:], bias_z[:, 0:512], ALU.add).then_inc(S["z_done"], 1)
                    dve.tensor_tensor(z[:, n % 2, 512:776], bank_n[1][:, 0:264], bias_z[:, 512:776], ALU.add)\
                        .then_inc(S["z_done"], 1)
                    wait(dve, "z_done", step)
                    dve.tensor_scalar(zr[:, n % 2, :], z[:, n % 2, 0:D], 0.0, -1.0, ALU.max, ALU.add)\
                        .then_inc(S["zrelu"], 1)
                    dve.max(top[:, n, :], z[:, n % 2, 768:776]).then_inc(S["top_done"], 1)
                    wait(dve, "act_z", step)
                    wait(dve, "zrelu", step)
                    dve.scalar_tensor_tensor(qn[:, n, :], ez[:, n % 2, :], 1.0, zr[:, n % 2, :], ALU.min, ALU.add)\
                        .then_inc(S["q_done"], 1)
                elif kind == "ffn":
                    _, b, m = step
                    f = b * M0 + m
                    wait(dve, "tanh_done", step)
                    dve.scalar_tensor_tensor(tg1[:, f % 2, :], tg1[:, f % 2, :], 1.0, gu[f % 2][:, 0, :],
                                             ALU.add, ALU.mult).then_inc(S["w_done"], 1)
                    if f >= 2:
                        wait(dve, "h_lo", ("ffn", *divmod(f - 2, M0)))
                    wait(dve, "w_done", step)
                    dve.tensor_tensor(hr1[:, f % 2, :], gu[f % 2][:, 1, :], tg1[:, f % 2, :], ALU.mult)\
                        .then_inc(S["h_raw"], 1)
                elif kind == "comb":
                    b = step[1]
                    sl = tiles(b, TPB)
                    wait(dve, "top_done", ("proj", TPB * b + TPB - 1))
                    dve.tensor_tensor(gate[:, 0, sl], top[:, sl, 1], top[:, sl, 0], ALU.subtract).then_inc(S["gap"], 1)
                    wait(dve, "egap", step)
                    c0 = at["comb_step", step] - 3
                    dve.tensor_scalar(gate[:, 2, sl], gate[:, 1, sl], 1.0, None, ALU.add).then_inc(S["comb_step"], 1)
                    dve.wait_ge(S["comb_step"], c0 + 1)
                    dve.reciprocal(gate[:, 2, sl], gate[:, 2, sl]).then_inc(S["comb_step"], 1)
                    dve.wait_ge(S["comb_step"], c0 + 2)
                    dve.scalar_tensor_tensor(gate[:, 3, sl], gate[:, 1, sl], 1.0, gate[:, 2, sl], ALU.add, ALU.mult)\
                        .then_inc(S["comb_step"], 1)
                elif kind == "down":
                    n = step[1]
                    b = n // TPB
                    wait(dve, "down_done", step)
                    wait(dve, "comb_step", ("comb", b))
                    wait(dve, "xb_done", ("xb", b))
                    o = bank_n[n % 2]
                    dve.scalar_tensor_tensor(x[:, n, :], o[:, D:], gate[:, 3, n:n + 1], x[:, n, :], ALU.mult, ALU.add)\
                        .then_inc(S["routed"], 1)
                    wait(dve, "routed", step)
                    dve.tensor_tensor(x[:, n, :], o[:, 0:D], x[:, n, :], ALU.add).then_inc(S["res_done"], 1)

                elif kind == "w2":
                    raw, hi, lo = halves2(step[1])
                    wait(dve, "w2_hi", step)
                    low(lo, raw, hi, "w2_lo")
                elif kind == "w2s":
                    dve.wait_ge(S["vec2_in"], 16 * 4)
                    s0 = at["scaled", step] - 2
                    dve.tensor_tensor(gus1[:], gs1[:], us1[:], ALU.mult).then_inc(S["scaled"], 1)
                    dve.wait_ge(S["scaled"], s0 + 1)
                    dve.tensor_scalar(gs1[:], gs1[:], 0.5, None, ALU.mult).then_inc(S["scaled"], 1)
                elif kind == "w2d":
                    dve.wait_ge(S["large2_in"], 16 * 4)
                    dve.wait_ge(S["vec2_in"], 16 * 4)
                    for_all = ds1[:].unsqueeze(1).broadcast_to([P, M1, D])
                    dve.scalar_tensor_tensor(raw2v[6], raw2v[6], 0.5, for_all, ALU.mult, ALU.mult)\
                        .then_inc(S["down_scaled"], 1)
                elif kind == "kvx":
                    for_both = bdmask[:].unsqueeze(1).broadcast_to([P, 2, P])
                    wait(dve, "kv_done", last("kv"))
                    dve.wait_ge(S["const_in"], 16 * 3)
                    kv = bank_kv[:, 0:D].rearrange("p (h e) -> p h e", h=2)
                    dve.tensor_tensor(kvr[:], kv, for_both, ALU.mult).then_inc(S["kv_raw"], 1)
                    wait(dve, "kv_hi", step)
                    wait(dve, "kv_raw", step)
                    low(kvb[:, LO], kvr[:], kvb[:, HI], "kv_lo")
                    dve.tensor_scalar(lng[:], lng[:], 0.5, None, ALU.mult).then_inc(S["ln_halved"], 1)
                    dve.tensor_scalar(lnb[:], lnb[:], 0.5, None, ALU.mult).then_inc(S["ln_halved"], 1)
                elif kind in ("qT", "oT", "xT"):
                    _, b, k = step
                    to = xT2 if kind == "xT" else qT2
                    wait(dve, "T2_hi", step)
                    low(to[:, LO, k, :], bank_T[:], to[:, HI, k, :], "T2_lo")
                elif kind == "out":
                    _, b, pair = step
                    o = bank_n[nat_bank(step)]
                    wait(dve, "nat_done", step)
                    prev = before(step, ("out",))
                    if prev:
                        wait(dve, "nat_free", prev)
                    wait(dve, *(("T2_done", ("xT", b - 1, 1)) if b else ("T_done", last("T"))))
                    wait(dve, "ln_halved", ("kvx",))
                    normalise_gain(lambda t: o[:, tiles(t, D)], lambda t: on[:, 2 * pair + t, :], lng[:], lnb[:], 2,
                                   ("o_stats", "o_aggr", "o_eps", "o_rstd", ["o_centred", "nat_free"], "o_norm"),
                                   {n: at[n, step] for n in ("o_stats", "o_aggr", "o_rstd", "o_centred", "nat_free")})
                elif kind == "wo" or kind == "d1":
                    _, b, pair = step
                    o = bank_n[nat_bank(step)]
                    n = TPB * b + 2 * pair
                    wait(dve, "nat_done", step)
                    wait(dve, *(("xb2_done", ("xb2", b)) if kind == "d1" else ("res_done", ("down", TPB * b + TPB - 1))))
                    dve.tensor_tensor(x[:, n:n + 2, :], o[:].rearrange("p (t d) -> p t d", t=2), x[:, n:n + 2, :], ALU.add)\
                        .then_inc(S["nat_free"], 1)
                elif kind == "ln2":
                    b = step[1]
                    wait(dve, "nat_free", ("wo", b, 1))
                    wait(dve, "T2_done", ("oT", b, 1))
                    if b:
                        wait(dve, "ln2_done", ("ln2", b - 1))
                    normalise(2, lambda i: x[:, TPB * b + i, :], lambda i: on[:, i, :], TPB,
                              ("stats2", "aggr2", "vareps2", "rstd2", ["ln2_done"] * TPB),
                              {n: at[n, step] for n in ("stats2", "aggr2", "rstd2")})
                elif kind in ("q", "k"):
                    hf = step[2]
                    wait(dve, "col_hi", step)
                    low(qks[:, LO, hf, :], bank[0][:], qks[:, HI, hf, :], "col_lo")
                elif kind == "c":
                    wait(dve, "col_hi", step)
                    low(cT[0:LAT, LO, :], bank[0][0:LAT, :], cT[0:LAT, HI, :], "col_lo")
                elif kind == "v":
                    _, b, pair = step
                    o = bank_n[nat_bank(step)]
                    n = TPB * b + 2 * pair
                    wait(dve, "nat_done", step)
                    dve.wait_ge(S["vv_set"], 2)
                    dve.tensor_copy(vv[:, n:n + 2, :, 0:DH], o[:].rearrange("p (t h d) -> p t h d", t=2, h=HEADS))\
                        .then_inc(S["nat_free"], 1)
                elif kind == "f1":
                    _, b, m = step
                    f = b * M1 + m
                    wait(dve, "tanh2_done", step)
                    dve.scalar_tensor_tensor(tg2[:, f % 2, :], tg2[:, f % 2, :], 1.0, gu[f % 2][:, 0, :],
                                             ALU.add, ALU.mult).then_inc(S["w2_done"], 1)
                    if f >= 2:
                        wait(dve, "h2_lo", ("f1", *divmod(f - 2, M1)))
                    wait(dve, "w2_done", step)
                    dve.scalar_tensor_tensor(hr2[:, f % 2, :], gu[f % 2][:, 1, :], gus1[:, m:m + 1], tg2[:, f % 2, :],
                                             ALU.mult, ALU.mult).then_inc(S["h2_raw"], 1)

                elif kind == "mx":
                    _, j, p, i, c, e = step
                    units = at["mx_done", step] - 1
                    scores = bank_n[nat_bank(step)]
                    if units == 0:
                        dve.wait_ge(S["cmask_in"], 16)
                        wait(dve, "o_gate", last("out"))
                    wait(dve, "mx_done", step)
                    to = mxp[:, (j * PAIRS + p) % 2, TPB * e + i, c:c + 1]
                    if c < j:
                        dve.tensor_reduce(to, scores[:], AX_X, ALU.max).then_inc(S["mx_red"], 1)
                    else:
                        w = (i + 1) * P
                        if units >= 2:
                            dve.wait_ge(S["mx_red"], units - 1)
                        dve.tensor_tensor_reduce(junk[:, units % 2, 0:w], scores[:, 0:w], cmask[:, BLK - w:], 1.0, 0.0,
                                                 ALU.add, ALU.max, to).then_inc(S["mx_red"], 1)
                elif kind == "mr":
                    _, j, p = step
                    s = j * PAIRS + p
                    wait(dve, "mx_red", ("mx", j, p, TPB - 1, j, 1))
                    if s >= 2:
                        wait(dve, "m_turned", ("mt", *divmod(s - 2, PAIRS)))
                    dve.tensor_reduce(mall[:, s % 2, :], mxp[:, s % 2, :, 0:j + 1], AX_X, ALU.max).then_inc(S["m_all"], 1)
                elif kind == "ct":
                    _, j, p = step
                    wait(dve, "cx_turned", step)
                    turned = bank[1][:, 0:2 * P].rearrange("p (t e h w) -> p t e h w", t=2, e=2, h=2)
                    den = bank[1][:, 0:2 * P].rearrange("p (t c w) -> p t c w", t=2, c=4)[:, :, :, DH]
                    prev = before(step, ("ct",))
                    if prev:
                        wait(dve, "cx_norm", prev)
                    if j >= 2:
                        wait(dve, "fin_turned", ("fa", j - 2, TPB - 1))
                    dve.reciprocal(rden[:, p % 2, :, :], den).then_inc(S["cx_rden"], 1)
                    wait(dve, "cx_rden", step)
                    for t in range(2):
                        to = cx[:, j % 2].rearrange("p (h t) (g d) -> p t g h d", t=2, d=DH)[:, t, 2 * p:2 * p + 2]
                        scale = rden[:, p % 2, t, :].rearrange("p (e h) -> p e h", e=2).unsqueeze(3)\
                            .broadcast_to([P, 2, 2, DH])
                        dve.tensor_tensor(to, turned[:, t, :, :, 0:DH], scale, ALU.mult).then_inc(S["cx_norm"], 1)
                elif kind == "fa":
                    wait(dve, "fin_hi", step)
                    low(fT[:, LO], bank[1][:, 0:D].rearrange("p (k t) -> p k t", k=KD), fT[:, HI], "fin_lo")
                elif kind == "fb":
                    _, j, i = step
                    n = TPB * j + i
                    wait(dve, "fin_done", step)
                    if n >= 2:
                        dve.wait_ge(S[f"fin_stored{i % 2}"], 16 * (n // 2))
                    dve.tensor_tensor(yo[:, i % 2, :], bank[1][:, 0:D], x[:, n, :], ALU.add).then_inc(S["fin_sum"], 1)

        @block.gpsimd
        def _(pool):
            pool.memset(mhalf[:], -0.5).then_inc(S["mhalf_set"], 1)
            pool.wait_ge(S["mhalf_set"], 1)

            def power(which, count, sem_in, value, sem_out):
                pool.wait_ge(S[sem_in], value)
                pool.tensor_tensor(rstd[:, which, 0:count], veps[:, which, 0:count], mhalf[:, 0:count], ALU.pow)\
                    .then_inc(S[sem_out], 1)

            for step in plan:
                kind = step[0]
                if kind == "into2":
                    stage1_over(pool)
                    pool.memset(ones_row[:, 0], 0.0).then_inc(S["ones_set"], 1)
                    pool.memset(ones_row[:, 1], 1.0).then_inc(S["ones_set"], 1)
                    pool.memset(vv[:, :, :, DH + 1:], 0.0).then_inc(S["vv_set"], 1)
                    pool.memset(vv[:, :, :, DH], 1.0).then_inc(S["vv_set"], 1)
                elif kind == "spare":
                    wait(pool, "T2_done", ("qT", NB - 1, 1))
                    wait(pool, "o_gate", last("out"))
                    for slot in range(2):
                        pool.memset(ks[slot].bitcast(F32), 0.0).then_inc(S["slot_zero"], 1)
                        pool.memset(qs[:, slot].bitcast(F32), 0.0).then_inc(S["slot_zero"], 1)
                elif kind == "into3":
                    stage2_over(pool)
                    pool.memset(ks[2].bitcast(F32), 0.0).then_inc(S["slot_zero"], 1)
                    pool.memset(qs[:, 2].bitcast(F32), 0.0).then_inc(S["slot_zero"], 1)
                elif kind == "ln":
                    if step[1]:
                        wait(pool, "ln_done", ("ln", step[1] - 1))
                    power(0, TPB, "vareps", at["vareps", step], "rstd")
                elif kind == "xb":
                    b = step[1]
                    wait(pool, "ln_done", ("ln", b))
                    pool.wait_ge(S["x_rest"], 32)
                    sl = tiles(b, TPB)
                    pool.tensor_tensor(x[:, sl, :], x[:, sl, :], bo0[:].unsqueeze(1).broadcast_to([P, TPB, D]), ALU.add)\
                        .then_inc(S["xb_done"], 1)
                elif kind == "wp":
                    i = step[1]
                    wait(pool, "w_hi", step)
                    pool.tensor_tensor(split1[i][:, LO], raw1v[i], split1[i][:, HI], ALU.subtract)\
                        .then_inc(S["wp_lo"], 1)
                elif kind == "proj":
                    n = step[1]
                    b, i = divmod(n, TPB)
                    if b >= 2:
                        wait(pool, "kv_done", ("kv", b - 2))
                    wait(pool, "act_z", step)
                    pool.tensor_tensor(tz[:, n % 2, :], tz[:, n % 2, :], z[:, n % 2, D:3 * D], ALU.mult)\
                        .then_inc(S["zt"], 1)
                    wait(pool, "zt", step)
                    pool.tensor_tensor(vn[:, b % 2, i, :], tz[:, n % 2, 0:D], z[:, n % 2, D:2 * D], ALU.add)\
                        .then_inc(S["quv"], 1)
                    pool.tensor_tensor(un[:, n, :], tz[:, n % 2, D:], z[:, n % 2, 2 * D:3 * D], ALU.add)\
                        .then_inc(S["quv"], 1)
                elif kind == "ffn":
                    _, b, m = step
                    f = b * M0 + m
                    wait(pool, "h_hi", step)
                    pool.tensor_tensor(hT1[:, LO, m, :], hr1[:, f % 2, :], hT1[:, HI, m, :], ALU.subtract)\
                        .then_inc(S["h_lo"], 1)
                elif kind == "w2p":
                    raw, hi, lo = halves2(step[1])
                    wait(pool, "w2_hi", step)
                    pool.tensor_tensor(lo, raw, hi, ALU.subtract).then_inc(S["w2p_lo"], 1)
                elif kind == "out":
                    _, b, pair = step
                    prev = before(step, ("out",))
                    if prev:
                        wait(pool, "nat_free", prev)
                    power(1, 2, "o_eps", at["o_eps", step], "o_rstd")
                    if pair == 0:
                        wait(pool, "quv", ("proj", TPB * b + TPB - 1))
                    wait(pool, "o_norm", step)
                    sl = slice(2 * pair, 2 * pair + 2)
                    n = TPB * b + 2 * pair
                    pool.tensor_tensor(on[:, sl, :], on[:, sl, :], un[:, n:n + 2, :], ALU.mult).then_inc(S["o_gate"], 1)
                elif kind == "ln2":
                    b = step[1]
                    if b:
                        wait(pool, "ln2_done", ("ln2", b - 1))
                    power(2, TPB, "vareps2", at["vareps2", step], "rstd2")
                elif kind == "xb2":
                    b = step[1]
                    pool.wait_ge(S["vec2_in"], 16 * 4)
                    wait(pool, "ln2_done", ("ln2", b))
                    sl = tiles(b, TPB)
                    pool.tensor_tensor(x[:, sl, :], x[:, sl, :], bo1[:].unsqueeze(1).broadcast_to([P, TPB, D]), ALU.add)\
                        .then_inc(S["xb2_done"], 1)
                elif kind == "f1":
                    _, b, m = step
                    f = b * M1 + m
                    wait(pool, "h2_hi", step)
                    pool.tensor_tensor(hT2[:, LO, m, :], hr2[:, f % 2, :], hT2[:, HI, m, :], ALU.subtract)\
                        .then_inc(S["h2_lo"], 1)
                elif kind == "sxd":
                    _, j, p, kt = step
                    g = at["s_done", step] - 1
                    off = (kt - TPB * j) * P
                    square = pr[:, g % 4, :, off:off + P]
                    wait(pool, "p_exp", step)
                    pool.affine_select(out=square, in_=square, compare_op=ALU.is_ge, fill=0.0, base=0,
                                       pattern=[[0, 2], [1, P]], channel_multiplier=-1).then_inc(S["p_masked"], 1)


def kernel(**inputs):
    import numpy as np
    import concourse.bacc as bacc
    from concourse.bass_utils import run_bass_kernel_spmd

    a = {k: np.asarray(v) for k, v in inputs.items()}

    def padded(w, axis):
        pad = [(0, 0)] * w.ndim
        pad[axis] = (0, M1 * P - w.shape[axis])
        return np.pad(w, pad)

    keys = np.arange(BLK)[None, :] - (BLK - P)
    lanes = np.arange(P)
    f32 = np.float32
    laid = {
        "x": a["L0_attn_x"].reshape(T, D),
        "w_qv": np.concatenate([a["L0_attn_Wqk"], a["L0_attn_Wv"]], 1),
        "w_ur": np.concatenate([a["L0_attn_Wu"], a["L0_ffn_router_weight"].T], 1),
        "bias_z": np.concatenate([a["L0_attn_bqk"], a["L0_attn_bv"], a["L0_attn_bu"], np.zeros(NR, f32)]),
        "w_gate": np.concatenate([a["L0_ffn_sh_gate"], a["L0_ffn_r_gate"]], 0).T,
        "w_up": np.concatenate([a["L0_ffn_sh_up"], a["L0_ffn_r_up"]], 0).T,
        "w_down": np.concatenate([a["L0_ffn_sh_down"], a["L0_ffn_r_down"]], 1).T,
        "w_o": a["L0_attn_Wo"],
        "b_o": a["L0_attn_bo"],
        "ln_g": a["L0_attn_ln_g"],
        "ln_b": a["L0_attn_ln_b"],
        "w_q1": a["L1_attn_W_q"].T,
        "w_c1": np.concatenate([a["L1_attn_W_dkv"], a["L1_attn_W_dkv"]], 0).T,
        "w_k1": a["L1_attn_W_uk"].T,
        "w_v1": a["L1_attn_W_uv"].T,
        "w_gate1": padded(a["L1_ffn_gate_w"], 0).T,
        "w_up1": padded(a["L1_ffn_up_w"], 0).T,
        "w_down1": padded(a["L1_ffn_down_w"], 1).T,
        "w_o1": a["L1_attn_W_o_w"].T,
        "gate_s1": padded(a["L1_ffn_gate_s"], 0).reshape(M1, P).T,
        "up_s1": padded(a["L1_ffn_up_s"], 0).reshape(M1, P).T,
        "down_s1": a["L1_ffn_down_s"],
        "b_o1": a["L1_attn_W_o_b"],
        "ident": np.eye(P, dtype=f32),
        "head_mask": np.where(lanes[:, None] // DH == lanes[None, :] // DH, f32(0.5), f32(0.0)),
        "causal": np.where(keys > lanes[:, None], f32(NEG), f32(0.0)),
    }
    nc = bacc.Bacc("TRN2", target_bir_lowering=False, num_devices=1)
    arrays, aps = {}, {}
    for name, value in laid.items():
        value = np.ascontiguousarray(value)
        arrays[f"in_{name}"] = value
        aps[name] = nc.dram_tensor(f"in_{name}", value.shape, mybir.dt.from_np(value.dtype), kind="ExternalInput").ap()
    out = nc.dram_tensor("out_y", (T, D), F32, kind="ExternalOutput").ap()
    build(nc, aps, out)
    r = run_bass_kernel_spmd(nc, [arrays], core_ids=[0])
    return np.asarray(r.results[0]["out_y"]).reshape(1, T, D)
```

```python
from contextlib import ExitStack

import concourse.bass as bass
from concourse import mybir

F32 = mybir.dt.float32
F32R = mybir.dt.float32r
BF16 = mybir.dt.bfloat16
ALU = mybir.AluOpType
ACT = mybir.ActivationFunctionType
AX_X = mybir.AxisListType.X

P = 128
T = 2048
D = 256
HEADS = 16
DH = D // HEADS
BLK = 512
NB = T // BLK
TPB = BLK // P
KD = D // P
INTER = 1024
MS = INTER // P
M0 = MS + 1
NR = 8
LAT = 64
M1 = 6
EPS = 1e-5
PAIRS = HEADS // 2
STACK = 3 * DH
QK_SCALE = 1.0 / DH ** 0.5
HI, LO = 0, 1
PASSES = ((HI, HI), (HI, LO), (LO, HI))
NEG = -1e30
RIGHT = "right"
LEADS = (8, 8, 8, 8)
LAG = 3
EARLY = 3
STAGED = 16 * 6
NSTK = 4
RAW1 = KD * 512 + KD * 264 + KD * D + 2 * KD * M0 * P + M0 * D
RAW2 = KD * D + KD * 2 * LAT + 2 * D + 2 * KD * M1 * P + M1 * D + KD * D


def tally(plan, signals):
    count, table = {}, {}
    for step in plan:
        for name, n in signals[step[0]]:
            count[name] = count.get(name, 0) + n
            table[name, step] = count[name]
    return table


def stage1_plan():
    plan = [("ln", 0), ("w", 0), ("w", 1), ("T", 0, 0), ("T", 0, 1), ("wp", 2), ("proj", 0), ("w", 3), ("proj", 1),
            ("proj", 2), ("w", 4), ("proj", 3), ("w", 5), ("xb", 0)]
    for b in range(NB):
        for i in range(TPB):
            if b and i:
                plan.append(("proj", TPB * b + i))
            plan += [("ffn", b, 2 * i), ("ffn", b, 2 * i + 1)]
            if i == 1 and b + 1 < NB:
                plan += [("ln", b + 1), ("xb", b + 1)]
        if b + 1 < NB:
            plan += [("T", b + 1, 0), ("T", b + 1, 1), ("ffn", b, MS), ("comb", b), ("kv", b)]
            plan += [("proj", TPB * (b + 1))]
            plan += [("down", TPB * b + i) for i in range(TPB)]
    b = NB - 1
    plan.remove(("ffn", b, 2 * TPB - 1))
    plan += [("kv", b), ("qT", 0, 0), ("ffn", b, 2 * TPB - 1), ("kvx",), ("qT", 0, 1), ("ffn", b, MS), ("comb", b)]
    plan += [("out", 0, 0), ("out", 0, 1)] + [("down", TPB * b + i) for i in range(3)]
    plan += [("oT", 0, 0), ("down", T // P - 1), ("oT", 0, 1), ("wo", 0, 0), ("wo", 0, 1), ("ln2", 0), ("into2",)]
    return plan


SIGNALS1 = {
    "into2": [("ones_set", 2), ("vv_set", 2)], "into3": [("slot_zero", 3)], "spare": [("slot_zero", 5)],
    "w": [("w_hi", 1), ("w_lo", 1)],
    "wp": [("w_hi", 1), ("wp_lo", 1)],
    "ln": [("stats", TPB), ("aggr", TPB), ("vareps", 1), ("rstd", 1), ("ln_done", TPB)],
    "xb": [("xb_done", 1)],
    "T": [("T_done", 1), ("T_hi", 1), ("T_lo", 1)],
    "proj": [("proj_done", 1), ("z_done", 2), ("top_done", 1), ("zrelu", 1), ("act_z", 2), ("q_done", 1), ("zt", 1), ("quv", 2)],
    "ffn": [("gu_done", 1), ("tanh_done", 1), ("w_done", 1), ("h_raw", 1), ("h_hi", 1), ("h_lo", 1)],
    "kv": [("kv_done", 1)],
    "comb": [("gap", 1), ("egap", 1), ("comb_step", 3)],
    "down": [("down_done", 1), ("routed", 1), ("res_done", 1)],
}


def stage2_plan():
    def chain(b):
        return {"qT": [("qT", b, 0)], "qT'": [("qT", b, 1)], "out": [("out", b, 0)], "out'": [("out", b, 1)],
                "oT": [("oT", b, 0)], "oT'": [("oT", b, 1)], "wo": [("wo", b, 0)],
                "wo'": [("wo", b, 1), ("ln2", b), ("xb2", b)], "xT": [("xT", b, 0)], "xT'": [("xT", b, 1)]}

    plan = [("xb2", 0), ("xT", 0, 0), ("w2", 0), ("xT", 0, 1), ("w2", 1), ("w2", 2), ("w2", 3), ("w2s",), ("w2p", 5), ("w2", 4)]
    for b in range(NB):
        nxt = chain(b + 1) if b + 1 < NB else dict.fromkeys(chain(0), [])
        plan += [("q", b, 0)] + nxt["qT"]
        if b == 0:
            plan += [("w2d",), ("w2", 6), ("w2p", 7)]
        plan += [("f1", b, 0), ("q", b, 1), ("st", b, 0)] + nxt["qT'"]
        plan += [("f1", b, 1), ("c", b)] + nxt["out"] + nxt["out'"]
        plan += [("f1", b, 2), ("v", b, 0), ("f1", b, 3), ("k", b, 0)] + nxt["oT"] + [("f1", b, 4), ("k", b, 1)]
        plan += [("st", b, 1)] + nxt["oT'"] + [("f1", b, 5)] + nxt["wo"] + nxt["wo'"] + [("v", b, 1)]
        if b == NB - 2:
            plan += [("spare",)] + [("ld", 0, p) for p in range(EARLY)]
        plan += [("d1", b, 0)]
        plan += nxt["xT"] + [("d1", b, 1)] + nxt["xT'"]
    return plan


SIGNALS2 = {
    "w2": [("w2_hi", 1), ("w2_lo", 1)],
    "w2p": [("w2_hi", 1), ("w2p_lo", 1)],
    "w2s": [("scaled", 2)],
    "w2d": [("down_scaled", 1)],
    "kvx": [("kv_raw", 1), ("kv_hi", 1), ("kv_lo", 1), ("ln_halved", 2)],
    "qT": [("T2_done", 1), ("T2_hi", 1), ("T2_lo", 1)],
    "oT": [("T2_done", 1), ("T2_hi", 1), ("T2_lo", 1)],
    "xT": [("T2_done", 1), ("T2_hi", 1), ("T2_lo", 1)],
    "out": [("nat_done", 1), ("o_stats", 2), ("o_aggr", 2), ("o_eps", 1), ("o_rstd", 1), ("o_centred", 1),
            ("o_norm", 2), ("o_gate", 1), ("nat_free", 1)],
    "wo": [("nat_done", 1), ("nat_free", 1)],
    "ln2": [("stats2", TPB), ("aggr2", TPB), ("vareps2", 1), ("rstd2", 1), ("ln2_done", TPB)],
    "xb2": [("xb2_done", 1)],
    "q": [("col_done", 1), ("col_hi", 1), ("col_lo", 1)],
    "k": [("col_done", 1), ("col_hi", 1), ("col_lo", 1)],
    "c": [("col_done", 1), ("col_hi", 1), ("col_lo", 1)],
    "v": [("nat_done", 1), ("nat_free", 1)],
    "f1": [("gu2_done", 1), ("tanh2_done", 1), ("w2_done", 1), ("h2_raw", 1), ("h2_hi", 1), ("h2_lo", 1)],
    "st": [],
    "d1": [("nat_done", 1), ("nat_free", 1)],
}


def stage3_plan():
    steps = [(j, p) for j in range(NB) for p in range(PAIRS)]
    maxima, ends, begins, turn = [], [], [], []
    for n, s in enumerate(steps):
        begins.append(len(maxima))
        if n < NSTK:
            maxima.append(("ld", *s))
        for u, unit in enumerate((i, c, e) for i in range(TPB) for c in range(s[0] + 1) for e in range(2)):
            maxima.append(("mx", *s, *unit))
            if u == 3:
                maxima += turn
        turn = [("mt", *s)]
        maxima.append(("mr", *s))
        ends.append(len(maxima) + 6)
    maxima += turn
    plan, done, products, extras = [], 0, [], []
    for n, s in enumerate(steps):
        count = TPB * (s[0] + 1)
        for kt in range(count):
            after = ends[n + 1] - ends[n] if n + 1 < len(steps) else 0
            goal = min(len(maxima), ends[n] + LEADS[s[0]] + kt * after // count)
            if n + NSTK < len(steps):
                goal = min(goal, begins[n + NSTK])
            goal = max(done, goal)
            half = max((done + goal) // 2, min(goal, ends[n]))
            plan += maxima[done:half]
            plan.append(("sxd" if kt >= TPB * s[0] else "sx", *s, kt))
            if kt == count - 1 and n + NSTK < len(steps):
                plan.append(("ld", *steps[n + NSTK]))
            plan += maxima[half:goal]
            done = goal
            products.append(("pv", *s, kt))
            if len(products) > LAG:
                step = products.pop(0)
                plan.append(step)
                if step[3] == TPB * (step[1] + 1) - 1:
                    plan.append(("cx", *step[1:3]))
                    extras.append(("ct", *step[1:3]))
                    if step[2] == PAIRS - 1:
                        extras += [(kind, step[1], i) for i in range(TPB) for kind in ("fa", "fb")]
                elif extras:
                    plan.append(extras.pop(0))
    plan += products + extras
    plan += [("cx", *steps[-1]), ("ct", *steps[-1]), ("fa", NB - 1, 0)]
    for i in range(TPB):
        plan += [("fa", NB - 1, i + 1)] * (i + 1 < TPB) + [("fb", NB - 1, i)]
    return plan


def whole_plan():
    plan2, plan3 = stage2_plan(), stage3_plan()
    loads = [s for s in plan3 if s[0] == "ld" and s[1] == 0 and s[2] < NSTK]
    first = [("sxd", 0, 0, kt) for kt in range(TPB)]
    plan3 = [s for s in plan3 if s not in loads + first]
    cut = plan3.index(("mx", 0, EARLY, 0, 0, 0))
    head = [s for s in plan3[:cut] if s[0] in ("mx", "mr", "mt")]
    plan3 = [s for s in plan3 if s not in head]
    b = NB - 1

    def take(n):
        return [head.pop(0) for _ in range(min(n, len(head)))]

    hooks = [("q", b, 1), ("f1", b, 0), ("f1", b, 1), ("f1", b, 2), ("c", b), ("v", b, 0), ("f1", b, 3), ("k", b, 0),
             ("f1", b, 4), ("k", b, 1), ("f1", b, 5), ("v", b, 1)]
    plan = []
    for s in plan2:
        if s == ("d1", b, 1):
            plan.append(first[0])
        plan.append(s)
        if s in hooks:
            plan += take(2)
        if s == ("v", b, 1):
            plan += take(len(head))
    return stage1_plan() + plan + [("into3",)] + loads[EARLY:] + first[1:] + plan3


SIGNALS3 = {
    "ld": [],
    "mx": [("mx_done", 1), ("mx_red", 1)],
    "mr": [("m_all", 1)],
    "mt": [("m_turned", 1), ("m_neg", 1)],
    "sx": [("s_done", 1), ("p_exp", 1)],
    "sxd": [("s_done", 1), ("p_exp", 1), ("p_masked", 1)],
    "pv": [("pv_done", 1)],
    "cx": [("cx_out", 1)],
    "ct": [("cx_turned", 1), ("cx_rden", 1), ("cx_norm", 2)],
    "fa": [("fin_turned", 1), ("fin_hi", 1), ("fin_lo", 1)],
    "fb": [("fin_done", 1), ("fin_sum", 1)],
}


def build(nc, A, out):
    plan = whole_plan()
    at = tally(plan, {**SIGNALS1, **SIGNALS2, **SIGNALS3})

    def before(step, kinds, n=1):
        where = plan.index(step) if step else len(plan)
        for s in reversed(plan[:where]):
            if s[0] in kinds:
                n -= 1
                if n == 0:
                    return s
        return None

    ctx = ExitStack()
    with ctx:
        def sb(name, shape, dt=F32, scope=ctx, side=None):
            return scope.enter_context(nc.sbuf_tensor(name, shape, dt, side=side))

        x = sb("x_res", [P, T // P, D])
        ident = sb("ident", [P, P])
        mvar = sb("mvar", [P, 3, TPB, 2])
        stat = sb("stat", [P, 3, TPB, 6])
        rstd = sb("rstd_c", [P, 3, TPB])
        veps = sb("veps_c", [P, 3, TPB])
        mhalf = sb("mhalf", [P, TPB])
        s12 = ExitStack()
        qn = sb("qn", [P, T // P, D], F32, s12, RIGHT)
        un = sb("un", [P, T // P, D], F32, s12, RIGHT)
        lng = sb("lng", [P, D], F32, s12, RIGHT)
        bdmask = sb("bdmask", [P, P], F32, s12, RIGHT)
        lnb = sb("lnb", [P, D], F32, s12, RIGHT)
        wo0 = sb("wo0", [P, 2, KD, D], F32R, s12, RIGHT)
        kvr = sb("kvr", [P, 2, P], F32, s12, RIGHT)
        kvb = sb("kvb", [P, 2, 2, P], F32R, s12, RIGHT)
        wqv = sb("wqv", [P, 2, KD, 512], F32R, s12, RIGHT)
        xn1 = sb("xn1", [P, TPB, D], F32, s12, RIGHT)
        qT2 = wqv
        on = xn1
        s1, raw_scope = ExitStack(), ExitStack()
        wur = sb("wur", [P, 2, KD, 264], F32R, s1)
        wg = sb("wg", [P, 2, KD, M0 * P], F32R, s1)
        wup = sb("wup", [P, 2, KD, M0 * P], F32R, s1)
        wdn = sb("wdn", [P, 2, M0, D], F32R, s1)
        bias_z = sb("bias_z", [P, 776], F32, s1)
        bo0 = sb("bo0", [P, D], F32, s1)
        xT1 = sb("xT1", [P, 2, KD, BLK], F32R, s1)
        z = sb("z", [P, 2, 776], F32, s1)
        zr = sb("zr", [P, 2, D], F32, s1)
        ez = sb("ez", [P, 2, D], F32, s1)
        tz = sb("tz", [P, 2, 2 * D], F32, s1)
        vn = sb("vn", [P, 2, TPB, D], F32, s1)
        tg1 = sb("tg1", [P, 2, BLK], F32, s1)
        hr1 = sb("hr1", [P, 2, BLK], F32, s1)
        raw1 = sb("raw1", [P, RAW1], F32, raw_scope)
        raw_scope.close()
        hT1 = sb("hT1", [P, 2, M0, BLK], F32R, s1)
        top = sb("top", [P, T // P, 8], F32, s1)
        gate = sb("gate", [P, 4, T // P], F32, s1)
        s1.close()
        s23 = ExitStack()
        vv = sb("vv", [P, T // P, HEADS, 32], F32, s23)
        wo1 = sb("wo1", [P, 2, KD, D], F32R, s23)
        s2, raw2_scope = ExitStack(), ExitStack()
        wq1 = sb("wq1", [P, 2, KD, D], F32R, s2)
        wc1 = sb("wc1", [P, 2, KD, 2 * LAT], F32R, s2)
        wk1 = sb("wk1", [LAT, 2, D], F32R, s2)
        wv1 = sb("wv1", [LAT, 2, D], F32R, s2)
        wg1 = sb("wg1", [P, 2, KD, M1 * P], F32R, s2)
        wu1 = sb("wu1", [P, 2, KD, M1 * P], F32R, s2)
        wd1 = sb("wd1", [P, 2, M1, D], F32R, s2)
        ones_row = sb("ones_row", [HEADS, 2, P], F32, s2)
        gs1 = sb("gs1", [P, M1], F32, s2)
        us1 = sb("us1", [P, M1], F32, s2)
        gus1 = sb("gus1", [P, M1], F32, s2)
        ds1 = sb("ds1", [P, D], F32, s2)
        bo1 = sb("bo1", [P, D], F32, s2)
        xT2 = sb("xT2", [P, 2, KD, BLK], F32R, s2)
        cT = sb("cT", [P, 2, BLK], F32R, s2)
        tg2 = sb("tg2", [P, 2, BLK], F32, s2)
        hr2 = sb("hr2", [P, 2, BLK], F32, s2)
        raw2 = sb("raw2", [P, RAW2], F32, raw2_scope)
        raw2_scope.close()
        qks = sb("qks", [P, 2, 2, BLK], F32R, s2)
        hT2 = sb("hT2", [P, 2, M1, BLK], F32R, s2)
        s2.close()
        s12.close()
        early = ExitStack()
        ks01 = sb("ks01", [P, 2, T], F32R, early, RIGHT)
        qs02 = sb("qs02", [P, 3, 2, BLK], F32R, early, RIGHT)
        cmask = sb("cmask", [P, BLK], F32, early, RIGHT)
        junk = sb("junk", [P, 2, BLK], BF16, early, RIGHT)
        mT = sb("mT", [2 * TPB, 2, P], F32R, early, RIGHT)
        mxp = sb("mxp", [P, 2, 2 * TPB, NB], F32, early, RIGHT)
        mall = sb("mall", [P, 2, 2 * TPB], F32, early, RIGHT)
        pr = sb("pr", [P, 4, 2, BLK], F32, early, RIGHT)
        ks23 = sb("ks23", [P, 2, T], F32R, s23)
        qs3 = sb("qs3", [P, 2, BLK], F32R, s23)
        ks = [ks23[:, 0, :], ks23[:, 1, :], ks01[:, 0, :], ks01[:, 1, :]]

        def k_stack(j, p):
            return ks[p % NSTK] if j else ks01[:, p % 2, tiles(p // 2, BLK)]

        qs = [qs02[:, 0], qs02[:, 1], qs02[:, 2], qs3[:]]
        cxT = sb("cxT", [P, 2, 2 * P], F32, s23)
        rden = sb("rden", [P, 2, 2, 4], F32, s23)
        cx = sb("cx", [P, 2, TPB, D], F32, s23)
        fT = sb("fT", [P, 2, 2, KD, P], F32R, s23)
        yo = sb("yo", [P, 2, D], F32, s23)
        s23.close()
        early.close()

        bank = [ctx.enter_context(nc.psum_tensor(f"bank{i}", [P, 512], F32)) for i in range(4)]
        pairA = ctx.enter_context(nc.psum_tensor("pairA", [P, 2, 512], F32))
        pairB = ctx.enter_context(nc.psum_tensor("pairB", [P, 2, 512], F32))
        gu = [pairA, pairB]

        scr_q = nc.dram_tensor("scr_q", [HEADS, STACK + 1, T], F32, kind="Internal").ap()
        scr_k = nc.dram_tensor("scr_k", [HEADS, STACK + 1, T], F32, kind="Internal").ap()

        names = {n for sig in (SIGNALS1, SIGNALS2, SIGNALS3) for v in sig.values() for n, _ in v}
        names |= {"x_first", "x_rest", "z_bias_in", "qv_in", "gate_up_in", "down_in", "const_in", "mhalf_set",
                  "small2_in", "large2_in", "vec2_in", "ones_set", "ones_stored", "vv_set", "cmask_in", "ident_in", "slot_zero"}
        names |= {f"staged{b}{which}" for b in range(NB) for which in range(2)}
        names |= {f"stack_in{i}" for i in range(NSTK)} | {f"{n}{i}" for n in ("m_row", "fin_stored") for i in range(2)}
        S = {n: ctx.enter_context(nc.semaphore(n)) for n in sorted(names)}

        def wait(eng, name, step):
            eng.wait_ge(S[name], at[name, step])

        def wait_stacks(eng, j, p):
            s = j * PAIRS + p
            eng.wait_ge(S[f"stack_in{s % NSTK}"], 64 * (s // NSTK + 1))

        def wait_row(eng, s):
            eng.wait_ge(S[f"m_row{s % 2}"], 32 * (s // 2 + 1))

        def last(kind):
            return before(None, (kind,))

        def stage1_over(eng):
            for name, kinds in (("down_done", "down"), ("kv_done", "kv"), ("res_done", "down"), ("h_hi", "ffn"),
                                ("h_lo", "ffn"), ("act_z", "proj"), ("quv", "proj"), ("q_done", "proj"), ("egap", "comb")):
                wait(eng, name, last(kinds))

        def stage2_over(eng):
            for name, kinds in (("nat_done", "d1"), ("nat_free", "d1"), ("col_lo", "k"), ("T2_hi", "xT"), ("T2_lo", "xT"),
                                ("h2_hi", "f1"), ("h2_lo", "f1"), ("o_gate", "out")):
                wait(eng, name, last(kinds))
            for which in range(2):
                eng.wait_ge(S[f"staged{NB - 1}{which}"], STAGED)

        def product(pe, out, lhsT, rhs, n, start=True, stop=True):
            steps = [(k, a, b) for k in range(n) for a, b in PASSES]
            for i, (k, a, b) in enumerate(steps):
                mm = pe.matmul(out, lhsT(a, k), rhs(b, k), start=start and i == 0, stop=stop and i == len(steps) - 1)
            return mm

        def tiles(i, w=P):
            return slice(i * w, (i + 1) * w)

        def landing(raw, shapes):
            at, views = 0, []
            for k, n in shapes:
                views.append(raw[:, at:at + k * n].rearrange("p (k n) -> p k n", k=k))
                at += k * n
            return views

        split1 = [wqv, wur, wg, wup, wdn, wo0]
        raw1v = landing(raw1, [(t.shape[2], t.shape[3]) for t in split1])
        scale1 = [1.0, 1.0, 1.0, 1.0, 0.5, 1.0]
        source1 = ["w_qv", "w_ur", "w_gate", "w_up", "w_down", "w_o"]
        arrived1 = [("qv_in", 32)] * 2 + [("gate_up_in", 32)] * 2 + [("down_in", 32)] * 2
        split2 = [wq1, wc1, wk1, wv1, wg1, wu1, wd1, wo1]
        raw2v = landing(raw2, [(KD, D), (KD, 2 * LAT), (1, D), (1, D), (KD, M1 * P), (KD, M1 * P), (M1, D), (KD, D)])
        arrived2 = [("small2_in", 64)] * 4 + [("large2_in", 64)] * 4
        source2 = ["w_q1", "w_c1", "w_k1", "w_v1", "w_gate1", "w_up1", "w_down1", "w_o1"]

        def halves2(i):
            if i in (2, 3):
                return raw2v[i][0:LAT, 0, :], split2[i][:, HI, :], split2[i][:, LO, :]
            return raw2v[i], split2[i][:, HI], split2[i][:, LO]

        bank_kv, bank_n = bank[0], bank[2:4]
        bank_free = {"T": "T_lo", "qT": "T2_lo", "oT": "T2_lo", "xT": "T2_lo", "proj": "z_done", "down": "res_done",
                     "out": "nat_free", "wo": "nat_free", "v": "nat_free", "d1": "nat_free",
                     "mx": "mx_red", "mt": "m_neg", "ct": "cx_norm", "fa": "fin_lo", "fb": "fin_sum"}
        banks_of, before_in_bank = {}, {}
        holder, rounds = {}, {2: 0, 3: 0}
        for s in plan:
            if s[0] in ("T", "qT", "oT", "xT") and s[2] == 0:
                banks_of[s] = (1,)
            elif s[0] == "proj":
                banks_of[s] = (2, 3)
            elif s[0] in ("T", "qT", "oT", "xT", "down", "out", "wo", "v", "d1"):
                banks_of[s] = (2 + rounds[2] % 2,)
                rounds[2] += 1
            elif s[0] in bank_free:
                banks_of[s] = (1 + rounds[3] % 3,)
                rounds[3] += 1
            else:
                continue
            before_in_bank[s] = [holder[i] for i in banks_of[s] if i in holder]
            holder.update({i: s for i in banks_of[s]})

        def bank_of(step):
            return bank[banks_of[step][0]]

        def wait_bank(pe, step):
            for user in before_in_bank[step]:
                wait(pe, bank_free[user[0]], user)

        block = ctx.enter_context(nc.Block())

        @block.sync
        def _(sp):
            x_v = A["x"].rearrange("(n p) d -> p n d", p=P)
            sp.dma_start(x[:, 0:TPB, :], x_v[:, 0:TPB, :]).then_inc(S["x_first"], 16)
            for i in range(6):
                sp.dma_start(raw1v[i], A[source1[i]].rearrange("(k p) n -> p k n", p=P)).then_inc(S[arrived1[i][0]], 16)
                if i == 0:
                    sp.dma_start(ident[:], A["ident"]).then_inc(S["ident_in"], 16)
                if i == 1:
                    sp.dma_start(bias_z[:], A["bias_z"].partition_broadcast(P)).then_inc(S["z_bias_in"], 16)
            sp.dma_start(x[:, TPB:, :], x_v[:, TPB:, :]).then_inc(S["x_rest"], 16)
            sp.dma_start(bo0[:], A["b_o"].partition_broadcast(P)).then_inc(S["x_rest"], 16)
            sp.dma_start(lng[:], A["ln_g"].partition_broadcast(P)).then_inc(S["const_in"], 16)
            sp.dma_start(lnb[:], A["ln_b"].partition_broadcast(P)).then_inc(S["const_in"], 16)
            sp.dma_start(bdmask[:], A["head_mask"]).then_inc(S["const_in"], 16)

            stage1_over(sp)
            for i in range(8):
                to = raw2v[i][0:LAT, 0, :] if i in (2, 3) else raw2v[i]
                source = A[source2[i]] if i in (2, 3) else A[source2[i]].rearrange("(k p) n -> p k n", p=P)
                sp.dma_start(to, source).then_inc(S[arrived2[i][0]], 16)
            sp.dma_start(gs1[:], A["gate_s1"]).then_inc(S["vec2_in"], 16)
            sp.dma_start(us1[:], A["up_s1"]).then_inc(S["vec2_in"], 16)
            sp.dma_start(ds1[:], A["down_s1"].partition_broadcast(P)).then_inc(S["vec2_in"], 16)
            sp.dma_start(bo1[:], A["b_o1"].partition_broadcast(P)).then_inc(S["vec2_in"], 16)
            sp.wait_ge(S["ones_set"], 2)
            for c in range(T // P):
                sp.dma_start(scr_k[:, STACK, tiles(c)], ones_row[:, 1, :]).then_inc(S["ones_stored"], 16)
                sp.dma_start(scr_q[:, STACK, tiles(c)], ones_row[:, 0, :]).then_inc(S["ones_stored"], 16)
            out_v = out.rearrange("(n p) d -> p n d", p=P)
            for step in plan:
                if step[0] == "st":
                    _, b, which = step
                    wait(sp, "col_lo", (("q", "k")[which], b, 1))
                    scratch, parts = ((scr_q, (HI, HI, LO)), (scr_k, (HI, LO, HI)))[which]
                    for hf in range(2):
                        for r, part in enumerate(parts):
                            sp.dma_start(scratch[hf * 8:(hf + 1) * 8, tiles(r, DH), tiles(b, BLK)],
                                         qks[:, part, hf, :].bitcast(F32)).then_inc(S[f"staged{b}{which}"], 16)

                elif step[0] == "ld":
                    _, j, p = step
                    s = j * PAIRS + p
                    if p == 0:
                        for which in range(2):
                            sp.wait_ge(S[f"staged{j}{which}"], STAGED)
                    if s == 0:
                        sp.wait_ge(S["ones_stored"], 2 * 16 * (T // P))
                        wait(sp, "o_gate", last("out"))
                        sp.dma_start(cmask[:], A["causal"]).then_inc(S["cmask_in"], 16)
                    if s < NSTK:
                        sp.wait_ge(S["slot_zero"], (2, 4, 5, 6)[s])
                    else:
                        jj, pp = divmod(s - NSTK, PAIRS)
                        wait(sp, "s_done", ("sxd", jj, pp, TPB * (jj + 1) - 1))
                    if s == PAIRS:
                        sp.wait_ge(S["slot_zero"], 8)
                    for e in range(2):
                        sp.dma_start(k_stack(j, p)[64 * e:64 * e + STACK + 1, 0:(j + 1) * BLK].bitcast(F32),
                                     scr_k[2 * p + e, :, 0:(j + 1) * BLK]).then_inc(S[f"stack_in{s % NSTK}"], 16)
                        sp.dma_start(qs[s % NSTK][64 * e:64 * e + STACK + 1, e, :].bitcast(F32),
                                     scr_q[2 * p + e, :, tiles(j, BLK)]).then_inc(S[f"stack_in{s % NSTK}"], 16)
                elif step[0] == "mt":
                    _, j, p = step
                    s = j * PAIRS + p
                    wait(sp, "m_neg", step)
                    for e in range(2):
                        sp.dma_start(qs[s % NSTK][64 * e + STACK:64 * e + STACK + 1, e, :].bitcast(F32),
                                     mT[TPB * e:TPB * (e + 1), s % 2, :].bitcast(F32)).then_inc(S[f"m_row{s % 2}"], 16)
                elif step[0] == "fb":
                    _, j, i = step
                    wait(sp, "fin_sum", step)
                    sp.dma_start(out_v[:, TPB * j + i, :], yo[:, i % 2, :]).then_inc(S[f"fin_stored{i % 2}"], 16)
            for parity in range(2):
                sp.wait_ge(S[f"fin_stored{parity}"], 16 * (T // P // 2))

        @block.tensor
        def _(pe):
            pe.wait_ge(S["ident_in"], 16)
            scores = 0
            for step in plan:
                kind = step[0]
                if kind == "into2":
                    stage1_over(pe)
                elif kind == "into3":
                    stage2_over(pe)
                    wait(pe, "w2p_lo", ("w2p", 7))
                elif kind == "T":
                    _, b, k = step
                    wait(pe, "ln_done", ("ln", b))
                    wait_bank(pe, step)
                    for i in range(TPB):
                        mm = pe.transpose(bank_of(step)[:, tiles(i)], xn1[:, i, tiles(k)], ident[:])
                    mm.then_inc(S["T_done"], 1)
                elif kind == "proj":
                    n = step[1]
                    b, i = divmod(n, TPB)
                    if n == 0:
                        wait(pe, "w_lo", ("w", 1))
                    wait(pe, "T_lo", ("T", b, 1))
                    wait_bank(pe, step)
                    lhs = lambda a, k: xT1[:, a, k, tiles(i)]
                    product(pe, bank_n[0][:], lhs, lambda a, k: wqv[:, a, k, :], KD)
                    product(pe, bank_n[1][:, 0:264], lhs, lambda a, k: wur[:, a, k, :], KD).then_inc(S["proj_done"], 1)
                elif kind == "ffn":
                    _, b, m = step
                    f = b * M0 + m
                    if f == 0:
                        wait(pe, "wp_lo", ("wp", 2))
                        wait(pe, "w_lo", ("w", 3))
                    if f >= 2:
                        wait(pe, "h_raw", ("ffn", *divmod(f - 2, M0)))
                    rhs = lambda a, k: xT1[:, a, k, :]
                    product(pe, gu[f % 2][:, 0, :], lambda a, k: wg[:, a, k, tiles(m)], rhs, KD)
                    product(pe, gu[f % 2][:, 1, :], lambda a, k: wup[:, a, k, tiles(m)], rhs, KD).then_inc(S["gu_done"], 1)
                elif kind == "kv":
                    b = step[1]
                    for i in range(TPB):
                        n = TPB * b + i
                        wait(pe, "quv", ("proj", n))
                        wait(pe, "q_done", ("proj", n))
                        for hf in range(2):
                            mm = pe.matmul(bank_kv[:, tiles(hf)], qn[:, n, tiles(hf)], vn[:, b % 2, i, tiles(hf)],
                                           start=(n == 0 and hf == 0), stop=(n == T // P - 1), skip_group_check=True)
                    mm.then_inc(S["kv_done"], 1)
                elif kind == "down":
                    n = step[1]
                    b, i = divmod(n, TPB)
                    wait(pe, "h_lo", ("ffn", b, MS))
                    wait_bank(pe, step)
                    if n == 0:
                        wait(pe, "w_lo", ("w", 4))
                    o = bank_of(step)
                    product(pe, o[:, 0:D], lambda a, m: hT1[:, a, m, tiles(i)], lambda a, m: wdn[:, a, m, :], MS)
                    product(pe, o[:, D:], lambda a, m: hT1[:, a, MS, tiles(i)], lambda a, m: wdn[:, a, MS, :], 1)\
                        .then_inc(S["down_done"], 1)

                elif kind in ("qT", "oT", "xT"):
                    _, b, k = step
                    wait_bank(pe, step)
                    if kind == "oT":
                        wait(pe, "o_gate", ("out", b, 1))
                    if kind == "xT":
                        wait(pe, "ln2_done", ("ln2", b))
                    for i in range(TPB):
                        src = qn[:, TPB * b + i, tiles(k)] if kind == "qT" else on[:, i, tiles(k)]
                        mm = pe.transpose(bank_of(step)[:, tiles(i)], src, ident[:])
                    mm.then_inc(S["T2_done"], 1)
                elif kind in ("out", "wo", "v", "d1"):
                    _, b, pair = step
                    o = bank_of(step)
                    wait_bank(pe, step)
                    if kind == "out":
                        wait(pe, "kv_lo", ("kvx",))
                        wait(pe, "T2_lo", ("qT", b, 1))
                    if kind == "wo":
                        wait(pe, "T2_lo", ("oT", b, 1))
                        wait(pe, "w_lo", ("w", 5))
                    if kind == "v":
                        wait(pe, "col_lo", ("c", b))
                        wait(pe, "w2_lo", ("w2", 3))
                    if kind == "d1":
                        wait(pe, "h2_lo", ("f1", b, M1 - 1))
                        wait(pe, "w2_lo", ("w2", 6))
                    for t in range(2):
                        i = 2 * pair + t
                        lhs = lambda a, k: qT2[:, a, k, tiles(i)]
                        if kind == "out":
                            for hf in range(2):
                                mm = product(pe, o[:, t * D + hf * P:t * D + hf * P + P],
                                             lambda a, k: qT2[:, a, hf, tiles(i)], lambda a, k: kvb[:, a, hf, :], 1)
                        elif kind == "wo":
                            mm = product(pe, o[:, tiles(t, D)], lhs, lambda a, k: wo0[:, a, k, :], KD)
                        elif kind == "v":
                            mm = product(pe, o[:, tiles(t, D)], lambda a, k: cT[0:LAT, a, tiles(i)],
                                         lambda a, k: wv1[:, a, :], 1)
                        else:
                            mm = product(pe, o[:, tiles(t, D)], lambda a, m: hT2[:, a, m, tiles(i)],
                                         lambda a, m: wd1[:, a, m, :], M1)
                    mm.then_inc(S["nat_done"], 1)
                elif kind in ("q", "c", "k"):
                    b = step[1]
                    prev = before(step, ("q", "c", "k"))
                    if prev:
                        wait(pe, "col_lo", prev)
                    else:
                        wait(pe, "kv_raw", ("kvx",))
                    rhs = lambda a, k: xT2[:, a, k, :]
                    if kind == "q":
                        wait(pe, "T2_lo", ("xT", b, 1))
                        wait(pe, "w2_lo", ("w2", 0))
                        mm = product(pe, bank[0][:], lambda a, k: wq1[:, a, k, tiles(step[2])], rhs, KD)
                    elif kind == "c":
                        wait(pe, "w2_lo", ("w2", 1))
                        mm = product(pe, bank[0][:], lambda a, k: wc1[:, a, k, :], rhs, KD)
                    else:
                        wait(pe, "col_lo", ("c", b))
                        wait(pe, "w2_lo", ("w2", 2))
                        mm = product(pe, bank[0][:], lambda a, k: wk1[:, a, tiles(step[2])],
                                     lambda a, k: cT[0:LAT, a, :], 1)
                    mm.then_inc(S["col_done"], 1)
                elif kind == "f1":
                    _, b, m = step
                    f = b * M1 + m
                    if f == 0:
                        wait(pe, "w2_lo", ("w2", 4))
                        wait(pe, "w2p_lo", ("w2p", 5))
                    if f >= 2:
                        wait(pe, "h2_raw", ("f1", *divmod(f - 2, M1)))
                    rhs = lambda a, k: xT2[:, a, k, :]
                    product(pe, gu[f % 2][:, 0, :], lambda a, k: wg1[:, a, k, tiles(m)], rhs, KD)
                    product(pe, gu[f % 2][:, 1, :], lambda a, k: wu1[:, a, k, tiles(m)], rhs, KD)\
                        .then_inc(S["gu2_done"], 1)

                elif kind == "mx":
                    _, j, p, i, c, e = step
                    slot = (j * PAIRS + p) % NSTK
                    wait_stacks(pe, j, p)
                    w = BLK if c < j else (i + 1) * P
                    wait_bank(pe, step)
                    pe.matmul(bank_of(step)[:, 0:w], qs[slot][:, e, tiles(i)], k_stack(j, p)[:, c * BLK:c * BLK + w],
                              start=True, stop=True).then_inc(S["mx_done"], 1)
                elif kind == "mt":
                    _, j, p = step
                    wait(pe, "m_all", ("mr", j, p))
                    wait_bank(pe, step)
                    pe.transpose(bank_of(step)[0:2 * TPB, 0:P], mall[:, (j * PAIRS + p) % 2, :], ident[:])\
                        .then_inc(S["m_turned"], 1)
                elif kind in ("sx", "sxd"):
                    _, j, p, kt = step
                    slot = (j * PAIRS + p) % NSTK
                    off = max(0, kt - TPB * j) * P
                    wait_row(pe, j * PAIRS + p)
                    if scores >= 2:
                        pe.wait_ge(S["p_exp"], scores - 1)
                    else:
                        wait(pe, "h2_raw", last("f1"))
                    for e in range(2):
                        mm = pe.matmul(gu[scores % 2][:, e, off:], k_stack(j, p)[:, tiles(kt)], qs[slot][:, e, off:],
                                       start=True, stop=True)
                    mm.then_inc(S["s_done"], 1)
                    scores += 1
                elif kind == "pv":
                    _, j, p, kt = step
                    own = ("sxd" if kt >= TPB * j else "sx", j, p, kt)
                    g = at["s_done", own] - 1
                    off = max(0, kt - TPB * j) * P
                    wait(pe, "p_masked" if own[0] == "sxd" else "p_exp", own)
                    if kt == 0 and (j or p):
                        wait(pe, "cx_out", before(step, ("cx",)))
                    elif kt == 0:
                        wait(pe, "col_lo", last("k"))
                        wait(pe, "nat_free", last("v"))
                    todo = [(e, hf) for hf in range(2) for e in range(2) if off < (hf + 1) * 2 * P]
                    for e, hf in todo:
                        lo = max(off, hf * 2 * P)
                        c = 2 * e + hf
                        mm = pe.matmul(bank[0][32 * c:32 * c + 32, lo - hf * 2 * P:2 * P], vv[:, kt, 2 * p + e, :],
                                       pr[:, g % 4, e, lo:(hf + 1) * 2 * P], start=(kt == 0),
                                       stop=(kt == TPB * j + 2 * hf + 1))
                    mm.then_inc(S["pv_done"], 1)
                elif kind == "ct":
                    _, j, p = step
                    wait(pe, "cx_out", ("cx", j, p))
                    wait_bank(pe, step)
                    for t in range(2):
                        mm = pe.transpose(bank_of(step)[:, tiles(t)], cxT[:, p % 2, tiles(t)], ident[:])
                    mm.then_inc(S["cx_turned"], 1)
                elif kind == "fa":
                    _, j, i = step
                    wait(pe, "cx_norm", ("ct", j, PAIRS - 1))
                    wait_bank(pe, step)
                    for k in range(KD):
                        mm = pe.transpose(bank_of(step)[:, tiles(k)], cx[:, j % 2, i, tiles(k)], ident[:])
                    mm.then_inc(S["fin_turned"], 1)
                elif kind == "fb":
                    _, j, i = step
                    wait(pe, "fin_lo", ("fa", j, i))
                    wait_bank(pe, step)
                    o = bank_of(step)
                    product(pe, o[:, 0:D], lambda a, k: fT[:, i % 2, a, k, :], lambda a, k: wo1[:, a, k, :], KD)\
                        .then_inc(S["fin_done"], 1)

        @block.scalar
        def _(act):
            for step in plan:
                kind = step[0]
                if kind == "into2":
                    stage1_over(act)
                elif kind == "into3":
                    stage2_over(act)
                elif kind in ("w", "wp"):
                    i = step[1]
                    act.wait_ge(S[arrived1[i][0]], arrived1[i][1])
                    act.activation(split1[i][:, HI], raw1v[i], ACT.Copy, scale=scale1[i]).then_inc(S["w_hi"], 1)
                elif kind == "T":
                    _, b, k = step
                    wait(act, "T_done", step)
                    if b:
                        wait(act, "gu_done", ("ffn", b - 1, MS))
                    act.activation(xT1[:, HI, k, :], bank_of(step)[:], ACT.Copy).then_inc(S["T_hi"], 1)
                elif kind == "proj":
                    n = step[1]
                    wait(act, "z_done", step)
                    if n >= 2:
                        wait(act, "quv", ("proj", n - 2))
                        wait(act, "q_done", ("proj", n - 2))
                    act.activation(ez[:, n % 2, :], z[:, n % 2, 0:D], ACT.Exp).then_inc(S["act_z"], 1)
                    act.activation(tz[:, n % 2, :], z[:, n % 2, D:3 * D], ACT.Tanh, scale=0.5).then_inc(S["act_z"], 1)
                elif kind == "ffn":
                    _, b, m = step
                    f = b * M0 + m
                    wait(act, "gu_done", step)
                    if f >= 2:
                        wait(act, "h_raw", ("ffn", *divmod(f - 2, M0)))
                    act.activation(tg1[:, f % 2, :], gu[f % 2][:, 0, :], ACT.Tanh, scale=0.5).then_inc(S["tanh_done"], 1)
                    wait(act, "h_raw", step)
                    if f == 0:
                        wait(act, "w_lo", ("w", 5))
                        wait(act, "wp_lo", ("wp", 2))
                    if b:
                        wait(act, "down_done", ("down", TPB * b - 1))
                    act.activation(hT1[:, HI, m, :], hr1[:, f % 2, :], ACT.Copy).then_inc(S["h_hi"], 1)
                elif kind == "comb":
                    b = step[1]
                    wait(act, "gap", step)
                    act.activation(gate[:, 1, tiles(b, TPB)], gate[:, 0, tiles(b, TPB)], ACT.Exp).then_inc(S["egap"], 1)

                elif kind in ("w2", "w2p"):
                    raw, hi, lo = halves2(step[1])
                    act.wait_ge(S[arrived2[step[1]][0]], arrived2[step[1]][1])
                    if step[1] == 6:
                        wait(act, "down_scaled", ("w2d",))
                    act.activation(hi, raw, ACT.Copy).then_inc(S["w2_hi"], 1)
                elif kind == "kvx":
                    wait(act, "kv_raw", step)
                    act.activation(kvb[:, HI], kvr[:], ACT.Copy).then_inc(S["kv_hi"], 1)
                elif kind in ("qT", "oT", "xT"):
                    _, b, k = step
                    wait(act, "T2_done", step)
                    if kind == "qT" and b == 0:
                        wait(act, "proj_done", last("proj"))
                    to = xT2 if kind == "xT" else qT2
                    act.activation(to[:, HI, k, :], bank_of(step)[:], ACT.Copy).then_inc(S["T2_hi"], 1)
                elif kind in ("q", "k"):
                    _, b, hf = step
                    wait(act, "col_done", step)
                    prev = before(step, ("st",))
                    if prev:
                        act.wait_ge(S["staged{}{}".format(*prev[1:])], STAGED)
                    elif hf == 0:
                        wait(act, "w2_lo", ("w2", 4))
                    act.activation(qks[:, HI, hf, :], bank[0][:], ACT.Copy).then_inc(S["col_hi"], 1)
                elif kind == "c":
                    wait(act, "col_done", step)
                    act.activation(cT[0:LAT, HI, :], bank[0][0:LAT, :], ACT.Copy).then_inc(S["col_hi"], 1)
                elif kind == "f1":
                    _, b, m = step
                    f = b * M1 + m
                    wait(act, "gu2_done", step)
                    if f == 0:
                        wait(act, "scaled", ("w2s",))
                    if f >= 2:
                        wait(act, "h2_raw", ("f1", *divmod(f - 2, M1)))
                    act.activation(tg2[:, f % 2, :], gu[f % 2][:, 0, :], ACT.Tanh, scale=gs1[:, m:m + 1])\
                        .then_inc(S["tanh2_done"], 1)
                    wait(act, "h2_raw", step)
                    if f == 0:
                        wait(act, "w2_lo", ("w2", 6))
                        wait(act, "w2p_lo", ("w2p", 7))
                    if b:
                        wait(act, "nat_done", ("d1", b - 1, 1))
                    act.activation(hT2[:, HI, m, :], hr2[:, f % 2, :], ACT.Copy).then_inc(S["h2_hi"], 1)

                elif kind == "mt":
                    _, j, p = step
                    s = j * PAIRS + p
                    if s == 0:
                        wait(act, "nat_free", last("out"))
                    wait(act, "m_turned", step)
                    if s >= 2:
                        wait_row(act, s - 2)
                    act.activation(mT[:, s % 2, :], bank_of(step)[0:2 * TPB, 0:P], ACT.Copy, scale=-1.0)\
                        .then_inc(S["m_neg"], 1)
                elif kind in ("sx", "sxd"):
                    _, j, p, kt = step
                    g = at["s_done", step] - 1
                    off = max(0, kt - TPB * j) * P
                    wait(act, "s_done", step)
                    if g == 0:
                        wait(act, "nat_free", last("wo"))
                        wait(act, "nat_done", last("wo"))
                    if g >= 4:
                        act.wait_ge(S["pv_done"], g - 3)
                    act.activation(pr[:, g % 4, :, off:], gu[g % 2][:, :, off:], ACT.Exp, scale=QK_SCALE)\
                        .then_inc(S["p_exp"], 1)
                elif kind == "cx":
                    _, j, p = step
                    wait(act, "pv_done", ("pv", j, p, TPB * (j + 1) - 1))
                    s = j * PAIRS + p
                    if s >= 2:
                        wait(act, "cx_turned", ("ct", *divmod(s - 2, PAIRS)))
                    act.activation(cxT[:, p % 2, :], bank[0][:, 0:2 * P], ACT.Copy).then_inc(S["cx_out"], 1)
                elif kind == "fa":
                    _, j, i = step
                    wait(act, "fin_turned", step)
                    prev = before(step, ("fb",)) if i < 2 else ("fb", j, i - 2)
                    if prev:
                        wait(act, "fin_done", prev)
                    act.activation(fT[:, i % 2, HI], bank_of(step)[:, 0:D].rearrange("p (k t) -> p k t", k=KD), ACT.Copy)\
                        .then_inc(S["fin_hi"], 1)

        @block.vector
        def _(dve):
            def normalise(which, source, to, count, sems, waits):
                stats, aggr, eps, rs, done = sems
                for i in range(count):
                    dve.bn_stats(stat[:, which, i, :], source(i)).then_inc(S[stats], 1)
                dve.wait_ge(S[stats], waits[stats])
                for i in range(count):
                    dve.bn_aggr(mvar[:, which, i, :], stat[:, which, i, :]).then_inc(S[aggr], 1)
                dve.wait_ge(S[aggr], waits[aggr])
                dve.tensor_scalar(veps[:, which, 0:count], mvar[:, which, 0:count, 1], EPS, None, ALU.add)\
                    .then_inc(S[eps], 1)
                dve.wait_ge(S[rs], waits[rs])
                for i in range(count):
                    dve.tensor_scalar(to(i), source(i), mvar[:, which, i, 0:1], rstd[:, which, i:i + 1],
                                      ALU.subtract, ALU.mult).then_inc(S[done[i]], 1)

            def normalise_gain(source, to, gain, bias, count, sems, waits):
                stats, aggr, eps, rs, centred, done = sems
                for i in range(count):
                    dve.bn_stats(stat[:, 1, i, :], source(i)).then_inc(S[stats], 1)
                dve.wait_ge(S[stats], waits[stats])
                for i in range(count):
                    dve.bn_aggr(mvar[:, 1, i, :], stat[:, 1, i, :]).then_inc(S[aggr], 1)
                dve.wait_ge(S[aggr], waits[aggr])
                dve.tensor_scalar(veps[:, 1, 0:count], mvar[:, 1, 0:count, 1], EPS, None, ALU.add).then_inc(S[eps], 1)
                for i in range(count):
                    dve.scalar_tensor_tensor(to(i), source(i), mvar[:, 1, i, 0:1], gain, ALU.subtract, ALU.mult)\
                        .then_inc(S[centred[i]], 1)
                dve.wait_ge(S[rs], waits[rs])
                for name in set(centred):
                    dve.wait_ge(S[name], waits[name])
                for i in range(count):
                    dve.scalar_tensor_tensor(to(i), to(i), rstd[:, 1, i:i + 1], bias, ALU.mult, ALU.add)\
                        .then_inc(S[done], 1)

            def low(out, raw, hi, sem, scale=1.0):
                if scale == 1.0:
                    dve.tensor_tensor(out, raw, hi, ALU.subtract).then_inc(S[sem], 1)
                else:
                    dve.scalar_tensor_tensor(out, raw, scale, hi, ALU.mult, ALU.subtract).then_inc(S[sem], 1)

            for step in plan:
                kind = step[0]
                if kind == "into2":
                    stage1_over(dve)
                elif kind == "into3":
                    stage2_over(dve)
                elif kind == "ln":
                    b = step[1]
                    if b == 0:
                        dve.wait_ge(S["x_first"], 16)
                    else:
                        dve.wait_ge(S["x_rest"], 32)
                        wait(dve, "T_done", ("T", b - 1, 1))
                        wait(dve, "ln_done", ("ln", b - 1))
                    normalise(0, lambda i: x[:, TPB * b + i, :], lambda i: xn1[:, i, :], TPB,
                              ("stats", "aggr", "vareps", "rstd", ["ln_done"] * TPB),
                              {n: at[n, step] for n in ("stats", "aggr", "rstd")})
                elif kind == "w":
                    i = step[1]
                    wait(dve, "w_hi", step)
                    low(split1[i][:, LO], raw1v[i], split1[i][:, HI], "w_lo", scale1[i])
                elif kind == "T":
                    _, b, k = step
                    wait(dve, "T_hi", step)
                    low(xT1[:, LO, k, :], bank_of(step)[:], xT1[:, HI, k, :], "T_lo")
                elif kind == "proj":
                    n = step[1]
                    wait(dve, "proj_done", step)
                    if n == 0:
                        dve.wait_ge(S["z_bias_in"], 16)
                    if n >= 2:
                        wait(dve, "quv", ("proj", n - 2))
                        wait(dve, "q_done", ("proj", n - 2))
                    dve.tensor_tensor(z[:, n % 2, 0:512], bank_n[0][:], bias_z[:, 0:512], ALU.add).then_inc(S["z_done"], 1)
                    dve.tensor_tensor(z[:, n % 2, 512:776], bank_n[1][:, 0:264], bias_z[:, 512:776], ALU.add)\
                        .then_inc(S["z_done"], 1)
                    wait(dve, "z_done", step)
                    dve.tensor_scalar(zr[:, n % 2, :], z[:, n % 2, 0:D], 0.0, -1.0, ALU.max, ALU.add)\
                        .then_inc(S["zrelu"], 1)
                    dve.max(top[:, n, :], z[:, n % 2, 768:776]).then_inc(S["top_done"], 1)
                    wait(dve, "act_z", step)
                    wait(dve, "zrelu", step)
                    dve.scalar_tensor_tensor(qn[:, n, :], ez[:, n % 2, :], 1.0, zr[:, n % 2, :], ALU.min, ALU.add)\
                        .then_inc(S["q_done"], 1)
                elif kind == "ffn":
                    _, b, m = step
                    f = b * M0 + m
                    wait(dve, "tanh_done", step)
                    dve.scalar_tensor_tensor(tg1[:, f % 2, :], tg1[:, f % 2, :], 1.0, gu[f % 2][:, 0, :],
                                             ALU.add, ALU.mult).then_inc(S["w_done"], 1)
                    if f >= 2:
                        wait(dve, "h_lo", ("ffn", *divmod(f - 2, M0)))
                    wait(dve, "w_done", step)
                    dve.tensor_tensor(hr1[:, f % 2, :], gu[f % 2][:, 1, :], tg1[:, f % 2, :], ALU.mult)\
                        .then_inc(S["h_raw"], 1)
                elif kind == "comb":
                    b = step[1]
                    sl = tiles(b, TPB)
                    wait(dve, "top_done", ("proj", TPB * b + TPB - 1))
                    dve.tensor_tensor(gate[:, 0, sl], top[:, sl, 1], top[:, sl, 0], ALU.subtract).then_inc(S["gap"], 1)
                    wait(dve, "egap", step)
                    c0 = at["comb_step", step] - 3
                    dve.tensor_scalar(gate[:, 2, sl], gate[:, 1, sl], 1.0, None, ALU.add).then_inc(S["comb_step"], 1)
                    dve.wait_ge(S["comb_step"], c0 + 1)
                    dve.reciprocal(gate[:, 2, sl], gate[:, 2, sl]).then_inc(S["comb_step"], 1)
                    dve.wait_ge(S["comb_step"], c0 + 2)
                    dve.scalar_tensor_tensor(gate[:, 3, sl], gate[:, 1, sl], 1.0, gate[:, 2, sl], ALU.add, ALU.mult)\
                        .then_inc(S["comb_step"], 1)
                elif kind == "down":
                    n = step[1]
                    b = n // TPB
                    wait(dve, "down_done", step)
                    wait(dve, "comb_step", ("comb", b))
                    wait(dve, "xb_done", ("xb", b))
                    o = bank_of(step)
                    dve.scalar_tensor_tensor(x[:, n, :], o[:, D:], gate[:, 3, n:n + 1], x[:, n, :], ALU.mult, ALU.add)\
                        .then_inc(S["routed"], 1)
                    wait(dve, "routed", step)
                    dve.tensor_tensor(x[:, n, :], o[:, 0:D], x[:, n, :], ALU.add).then_inc(S["res_done"], 1)

                elif kind == "w2":
                    raw, hi, lo = halves2(step[1])
                    wait(dve, "w2_hi", step)
                    low(lo, raw, hi, "w2_lo")
                elif kind == "w2s":
                    dve.wait_ge(S["vec2_in"], 16 * 4)
                    s0 = at["scaled", step] - 2
                    dve.tensor_tensor(gus1[:], gs1[:], us1[:], ALU.mult).then_inc(S["scaled"], 1)
                    dve.wait_ge(S["scaled"], s0 + 1)
                    dve.tensor_scalar(gs1[:], gs1[:], 0.5, None, ALU.mult).then_inc(S["scaled"], 1)
                elif kind == "w2d":
                    dve.wait_ge(S["large2_in"], 16 * 4)
                    dve.wait_ge(S["vec2_in"], 16 * 4)
                    for_all = ds1[:].unsqueeze(1).broadcast_to([P, M1, D])
                    dve.scalar_tensor_tensor(raw2v[6], raw2v[6], 0.5, for_all, ALU.mult, ALU.mult)\
                        .then_inc(S["down_scaled"], 1)
                elif kind == "kvx":
                    for_both = bdmask[:].unsqueeze(1).broadcast_to([P, 2, P])
                    wait(dve, "kv_done", last("kv"))
                    dve.wait_ge(S["const_in"], 16 * 3)
                    kv = bank_kv[:, 0:D].rearrange("p (h e) -> p h e", h=2)
                    dve.tensor_tensor(kvr[:], kv, for_both, ALU.mult).then_inc(S["kv_raw"], 1)
                    wait(dve, "kv_hi", step)
                    wait(dve, "kv_raw", step)
                    low(kvb[:, LO], kvr[:], kvb[:, HI], "kv_lo")
                    dve.tensor_scalar(lng[:], lng[:], 0.5, None, ALU.mult).then_inc(S["ln_halved"], 1)
                    dve.tensor_scalar(lnb[:], lnb[:], 0.5, None, ALU.mult).then_inc(S["ln_halved"], 1)
                elif kind in ("qT", "oT", "xT"):
                    _, b, k = step
                    to = xT2 if kind == "xT" else qT2
                    wait(dve, "T2_hi", step)
                    low(to[:, LO, k, :], bank_of(step)[:], to[:, HI, k, :], "T2_lo")
                elif kind == "out":
                    _, b, pair = step
                    o = bank_of(step)
                    wait(dve, "nat_done", step)
                    prev = before(step, ("out",))
                    if prev:
                        wait(dve, "nat_free", prev)
                    wait(dve, *(("T2_done", ("xT", b - 1, 1)) if b else ("T_done", last("T"))))
                    wait(dve, "ln_halved", ("kvx",))
                    normalise_gain(lambda t: o[:, tiles(t, D)], lambda t: on[:, 2 * pair + t, :], lng[:], lnb[:], 2,
                                   ("o_stats", "o_aggr", "o_eps", "o_rstd", ["o_centred", "nat_free"], "o_norm"),
                                   {n: at[n, step] for n in ("o_stats", "o_aggr", "o_rstd", "o_centred", "nat_free")})
                elif kind == "wo" or kind == "d1":
                    _, b, pair = step
                    o = bank_of(step)
                    n = TPB * b + 2 * pair
                    wait(dve, "nat_done", step)
                    wait(dve, *(("xb2_done", ("xb2", b)) if kind == "d1" else ("res_done", ("down", TPB * b + TPB - 1))))
                    dve.tensor_tensor(x[:, n:n + 2, :], o[:].rearrange("p (t d) -> p t d", t=2), x[:, n:n + 2, :], ALU.add)\
                        .then_inc(S["nat_free"], 1)
                elif kind == "ln2":
                    b = step[1]
                    wait(dve, "nat_free", ("wo", b, 1))
                    wait(dve, "T2_done", ("oT", b, 1))
                    if b:
                        wait(dve, "ln2_done", ("ln2", b - 1))
                    normalise(2, lambda i: x[:, TPB * b + i, :], lambda i: on[:, i, :], TPB,
                              ("stats2", "aggr2", "vareps2", "rstd2", ["ln2_done"] * TPB),
                              {n: at[n, step] for n in ("stats2", "aggr2", "rstd2")})
                elif kind in ("q", "k"):
                    hf = step[2]
                    wait(dve, "col_hi", step)
                    low(qks[:, LO, hf, :], bank[0][:], qks[:, HI, hf, :], "col_lo")
                elif kind == "c":
                    wait(dve, "col_hi", step)
                    low(cT[0:LAT, LO, :], bank[0][0:LAT, :], cT[0:LAT, HI, :], "col_lo")
                elif kind == "v":
                    _, b, pair = step
                    o = bank_of(step)
                    n = TPB * b + 2 * pair
                    wait(dve, "nat_done", step)
                    dve.wait_ge(S["vv_set"], 2)
                    dve.tensor_copy(vv[:, n:n + 2, :, 0:DH], o[:].rearrange("p (t h d) -> p t h d", t=2, h=HEADS))\
                        .then_inc(S["nat_free"], 1)
                elif kind == "f1":
                    _, b, m = step
                    f = b * M1 + m
                    wait(dve, "tanh2_done", step)
                    dve.scalar_tensor_tensor(tg2[:, f % 2, :], tg2[:, f % 2, :], 1.0, gu[f % 2][:, 0, :],
                                             ALU.add, ALU.mult).then_inc(S["w2_done"], 1)
                    if f >= 2:
                        wait(dve, "h2_lo", ("f1", *divmod(f - 2, M1)))
                    wait(dve, "w2_done", step)
                    dve.scalar_tensor_tensor(hr2[:, f % 2, :], gu[f % 2][:, 1, :], gus1[:, m:m + 1], tg2[:, f % 2, :],
                                             ALU.mult, ALU.mult).then_inc(S["h2_raw"], 1)

                elif kind == "mx":
                    _, j, p, i, c, e = step
                    units = at["mx_done", step] - 1
                    scores = bank_of(step)
                    if units == 0:
                        dve.wait_ge(S["cmask_in"], 16)
                        wait(dve, "o_gate", last("out"))
                    wait(dve, "mx_done", step)
                    to = mxp[:, (j * PAIRS + p) % 2, TPB * e + i, c:c + 1]
                    if c < j:
                        dve.tensor_reduce(to, scores[:], AX_X, ALU.max).then_inc(S["mx_red"], 1)
                    else:
                        w = (i + 1) * P
                        if units >= 2:
                            dve.wait_ge(S["mx_red"], units - 1)
                        dve.tensor_tensor_reduce(junk[:, units % 2, 0:w], scores[:, 0:w], cmask[:, BLK - w:], 1.0, 0.0,
                                                 ALU.add, ALU.max, to).then_inc(S["mx_red"], 1)
                elif kind == "mr":
                    _, j, p = step
                    s = j * PAIRS + p
                    wait(dve, "mx_red", ("mx", j, p, TPB - 1, j, 1))
                    if s >= 2:
                        wait(dve, "m_turned", ("mt", *divmod(s - 2, PAIRS)))
                    dve.tensor_reduce(mall[:, s % 2, :], mxp[:, s % 2, :, 0:j + 1], AX_X, ALU.max).then_inc(S["m_all"], 1)
                elif kind == "ct":
                    _, j, p = step
                    wait(dve, "cx_turned", step)
                    turned = bank_of(step)[:, 0:2 * P].rearrange("p (t e h w) -> p t e h w", t=2, e=2, h=2)
                    den = bank_of(step)[:, 0:2 * P].rearrange("p (t c w) -> p t c w", t=2, c=4)[:, :, :, DH]
                    prev = before(step, ("ct",))
                    if prev:
                        wait(dve, "cx_norm", prev)
                    if j >= 2:
                        wait(dve, "fin_turned", ("fa", j - 2, TPB - 1))
                    dve.reciprocal(rden[:, p % 2, :, :], den).then_inc(S["cx_rden"], 1)
                    wait(dve, "cx_rden", step)
                    for t in range(2):
                        to = cx[:, j % 2].rearrange("p (h t) (g d) -> p t g h d", t=2, d=DH)[:, t, 2 * p:2 * p + 2]
                        scale = rden[:, p % 2, t, :].rearrange("p (e h) -> p e h", e=2).unsqueeze(3)\
                            .broadcast_to([P, 2, 2, DH])
                        dve.tensor_tensor(to, turned[:, t, :, :, 0:DH], scale, ALU.mult).then_inc(S["cx_norm"], 1)
                elif kind == "fa":
                    i = step[2]
                    wait(dve, "fin_hi", step)
                    low(fT[:, i % 2, LO], bank_of(step)[:, 0:D].rearrange("p (k t) -> p k t", k=KD), fT[:, i % 2, HI], "fin_lo")
                elif kind == "fb":
                    _, j, i = step
                    n = TPB * j + i
                    wait(dve, "fin_done", step)
                    if n >= 2:
                        dve.wait_ge(S[f"fin_stored{i % 2}"], 16 * (n // 2))
                    o = bank_of(step)
                    dve.tensor_tensor(yo[:, i % 2, :], o[:, 0:D], x[:, n, :], ALU.add).then_inc(S["fin_sum"], 1)

        @block.gpsimd
        def _(pool):
            pool.memset(mhalf[:], -0.5).then_inc(S["mhalf_set"], 1)
            pool.wait_ge(S["mhalf_set"], 1)

            def power(which, count, sem_in, value, sem_out):
                pool.wait_ge(S[sem_in], value)
                pool.tensor_tensor(rstd[:, which, 0:count], veps[:, which, 0:count], mhalf[:, 0:count], ALU.pow)\
                    .then_inc(S[sem_out], 1)

            for step in plan:
                kind = step[0]
                if kind == "into2":
                    stage1_over(pool)
                    pool.memset(ones_row[:, 0], 0.0).then_inc(S["ones_set"], 1)
                    pool.memset(ones_row[:, 1], 1.0).then_inc(S["ones_set"], 1)
                    pool.memset(vv[:, :, :, DH + 1:], 0.0).then_inc(S["vv_set"], 1)
                    pool.memset(vv[:, :, :, DH], 1.0).then_inc(S["vv_set"], 1)
                elif kind == "spare":
                    wait(pool, "T2_done", ("qT", NB - 1, 1))
                    wait(pool, "o_gate", last("out"))
                    for slot in range(2):
                        pool.memset(ks01[:, slot].bitcast(F32), 0.0).then_inc(S["slot_zero"], 1)
                        pool.memset(qs[slot].bitcast(F32), 0.0).then_inc(S["slot_zero"], 1)
                    pool.memset(qs[2].bitcast(F32), 0.0).then_inc(S["slot_zero"], 1)
                elif kind == "into3":
                    stage2_over(pool)
                    pool.memset(qs[3].bitcast(F32), 0.0).then_inc(S["slot_zero"], 1)
                    for slot in range(2):
                        pool.memset(ks23[:, slot].bitcast(F32), 0.0).then_inc(S["slot_zero"], 1)
                elif kind == "ln":
                    if step[1]:
                        wait(pool, "ln_done", ("ln", step[1] - 1))
                    power(0, TPB, "vareps", at["vareps", step], "rstd")
                elif kind == "xb":
                    b = step[1]
                    wait(pool, "ln_done", ("ln", b))
                    pool.wait_ge(S["x_rest"], 32)
                    sl = tiles(b, TPB)
                    pool.tensor_tensor(x[:, sl, :], x[:, sl, :], bo0[:].unsqueeze(1).broadcast_to([P, TPB, D]), ALU.add)\
                        .then_inc(S["xb_done"], 1)
                elif kind == "wp":
                    i = step[1]
                    wait(pool, "w_hi", step)
                    pool.tensor_tensor(split1[i][:, LO], raw1v[i], split1[i][:, HI], ALU.subtract)\
                        .then_inc(S["wp_lo"], 1)
                elif kind == "proj":
                    n = step[1]
                    b, i = divmod(n, TPB)
                    if b >= 2:
                        wait(pool, "kv_done", ("kv", b - 2))
                    wait(pool, "act_z", step)
                    pool.tensor_tensor(tz[:, n % 2, :], tz[:, n % 2, :], z[:, n % 2, D:3 * D], ALU.mult)\
                        .then_inc(S["zt"], 1)
                    wait(pool, "zt", step)
                    pool.tensor_tensor(vn[:, b % 2, i, :], tz[:, n % 2, 0:D], z[:, n % 2, D:2 * D], ALU.add)\
                        .then_inc(S["quv"], 1)
                    pool.tensor_tensor(un[:, n, :], tz[:, n % 2, D:], z[:, n % 2, 2 * D:3 * D], ALU.add)\
                        .then_inc(S["quv"], 1)
                elif kind == "ffn":
                    _, b, m = step
                    f = b * M0 + m
                    wait(pool, "h_hi", step)
                    pool.tensor_tensor(hT1[:, LO, m, :], hr1[:, f % 2, :], hT1[:, HI, m, :], ALU.subtract)\
                        .then_inc(S["h_lo"], 1)
                elif kind == "w2p":
                    raw, hi, lo = halves2(step[1])
                    wait(pool, "w2_hi", step)
                    pool.tensor_tensor(lo, raw, hi, ALU.subtract).then_inc(S["w2p_lo"], 1)
                elif kind == "out":
                    _, b, pair = step
                    prev = before(step, ("out",))
                    if prev:
                        wait(pool, "nat_free", prev)
                    power(1, 2, "o_eps", at["o_eps", step], "o_rstd")
                    if pair == 0:
                        wait(pool, "quv", ("proj", TPB * b + TPB - 1))
                    wait(pool, "o_norm", step)
                    sl = slice(2 * pair, 2 * pair + 2)
                    n = TPB * b + 2 * pair
                    pool.tensor_tensor(on[:, sl, :], on[:, sl, :], un[:, n:n + 2, :], ALU.mult).then_inc(S["o_gate"], 1)
                elif kind == "ln2":
                    b = step[1]
                    if b:
                        wait(pool, "ln2_done", ("ln2", b - 1))
                    power(2, TPB, "vareps2", at["vareps2", step], "rstd2")
                elif kind == "xb2":
                    b = step[1]
                    pool.wait_ge(S["vec2_in"], 16 * 4)
                    wait(pool, "ln2_done", ("ln2", b))
                    sl = tiles(b, TPB)
                    pool.tensor_tensor(x[:, sl, :], x[:, sl, :], bo1[:].unsqueeze(1).broadcast_to([P, TPB, D]), ALU.add)\
                        .then_inc(S["xb2_done"], 1)
                elif kind == "f1":
                    _, b, m = step
                    f = b * M1 + m
                    wait(pool, "h2_hi", step)
                    pool.tensor_tensor(hT2[:, LO, m, :], hr2[:, f % 2, :], hT2[:, HI, m, :], ALU.subtract)\
                        .then_inc(S["h2_lo"], 1)
                elif kind == "sxd":
                    _, j, p, kt = step
                    g = at["s_done", step] - 1
                    off = (kt - TPB * j) * P
                    square = pr[:, g % 4, :, off:off + P]
                    wait(pool, "p_exp", step)
                    pool.affine_select(out=square, in_=square, compare_op=ALU.is_ge, fill=0.0, base=0,
                                       pattern=[[0, 2], [1, P]], channel_multiplier=-1).then_inc(S["p_masked"], 1)


def kernel(**inputs):
    import numpy as np
    import concourse.bacc as bacc
    from concourse.bass_utils import run_bass_kernel_spmd

    a = {k: np.asarray(v) for k, v in inputs.items()}

    def padded(w, axis):
        pad = [(0, 0)] * w.ndim
        pad[axis] = (0, M1 * P - w.shape[axis])
        return np.pad(w, pad)

    keys = np.arange(BLK)[None, :] - (BLK - P)
    lanes = np.arange(P)
    f32 = np.float32
    laid = {
        "x": a["L0_attn_x"].reshape(T, D),
        "w_qv": np.concatenate([a["L0_attn_Wqk"], a["L0_attn_Wv"]], 1),
        "w_ur": np.concatenate([a["L0_attn_Wu"], a["L0_ffn_router_weight"].T], 1),
        "bias_z": np.concatenate([a["L0_attn_bqk"], a["L0_attn_bv"], a["L0_attn_bu"], np.zeros(NR, f32)]),
        "w_gate": np.concatenate([a["L0_ffn_sh_gate"], a["L0_ffn_r_gate"]], 0).T,
        "w_up": np.concatenate([a["L0_ffn_sh_up"], a["L0_ffn_r_up"]], 0).T,
        "w_down": np.concatenate([a["L0_ffn_sh_down"], a["L0_ffn_r_down"]], 1).T,
        "w_o": a["L0_attn_Wo"],
        "b_o": a["L0_attn_bo"],
        "ln_g": a["L0_attn_ln_g"],
        "ln_b": a["L0_attn_ln_b"],
        "w_q1": a["L1_attn_W_q"].T,
        "w_c1": np.concatenate([a["L1_attn_W_dkv"], a["L1_attn_W_dkv"]], 0).T,
        "w_k1": a["L1_attn_W_uk"].T,
        "w_v1": a["L1_attn_W_uv"].T,
        "w_gate1": padded(a["L1_ffn_gate_w"], 0).T,
        "w_up1": padded(a["L1_ffn_up_w"], 0).T,
        "w_down1": padded(a["L1_ffn_down_w"], 1).T,
        "w_o1": a["L1_attn_W_o_w"].T,
        "gate_s1": padded(a["L1_ffn_gate_s"], 0).reshape(M1, P).T,
        "up_s1": padded(a["L1_ffn_up_s"], 0).reshape(M1, P).T,
        "down_s1": a["L1_ffn_down_s"],
        "b_o1": a["L1_attn_W_o_b"],
        "ident": np.eye(P, dtype=f32),
        "head_mask": np.where(lanes[:, None] // DH == lanes[None, :] // DH, f32(0.5), f32(0.0)),
        "causal": np.where(keys > lanes[:, None], f32(NEG), f32(0.0)),
    }
    nc = bacc.Bacc("TRN2", target_bir_lowering=False, num_devices=1)
    arrays, aps = {}, {}
    for name, value in laid.items():
        value = np.ascontiguousarray(value)
        arrays[f"in_{name}"] = value
        aps[name] = nc.dram_tensor(f"in_{name}", value.shape, mybir.dt.from_np(value.dtype), kind="ExternalInput").ap()
    out = nc.dram_tensor("out_y", (T, D), F32, kind="ExternalOutput").ap()
    build(nc, aps, out)
    r = run_bass_kernel_spmd(nc, [arrays], core_ids=[0])
    return np.asarray(r.results[0]["out_y"]).reshape(1, T, D)
```
